# Optimizing a Trainium2 kernel written in Bass

```python
import numpy as np
import jax
import jax.numpy as jnp

def _softmax(x, axis=-1):
    return jax.nn.softmax(x, axis=axis)

def _gelu(x):
    return jax.nn.gelu(x, approximate=True)

def _silu(x):
    return jax.nn.silu(x)

def _sigmoid(x):
    return jax.nn.sigmoid(x)

def _layernorm(x, axis=-1, eps=1e-05):
    m = jnp.mean(x, axis=axis, keepdims=True)
    v = jnp.var(x, axis=axis, keepdims=True)
    return (x - m) / jnp.sqrt(v + eps)

def _scatter_add(tgt, idx, src, axis=0):
    return tgt.at[idx].add(src)

def _segment_sum(src, seg, n):
    return jax.ops.segment_sum(src, seg, n)
kernel_name = 'mk_seq_preln_d2_jaxref_r4_501be4'

def setup_inputs(seed: int=0):
    np.random.seed(seed)
    _w = jnp.asarray

    def _L0_attn_setup():
        import jax, jax.numpy as jnp
        import numpy as np
        B, N, E = (4, 512, 256)
        H = 8
        D1 = 3 * E
        DH = D1 // H
        R = 128
        GAMMA = 0.99
        EPS = 1e-08

        def _srms(x):
            rms = jnp.linalg.norm(x, axis=-1, keepdims=True) * x.shape[-1] ** (-0.5)
            return x / (rms + EPS)
        key = jax.random.key(seed)
        ks = jax.random.split(key, 20)

        def lin(k, din, dout):
            kw, kb = jax.random.split(k)
            w = jax.random.normal(kw, (din, dout), jnp.float32) * din ** (-0.5)
            b = jax.random.normal(kb, (dout,), jnp.float32) * 0.02
            return (w, b)
        x = jax.random.normal(ks[0], (B, N, E), jnp.float32)
        u_w, u_b = lin(ks[1], E, D1)
        v_w, v_b = lin(ks[2], E, D1)
        o_w, o_b = lin(ks[3], D1, E)
        pos_w, pos_b = lin(ks[4], 1, R)
        lw0, lb0 = lin(ks[5], R, R)
        lw1, lb1 = lin(ks[6], R, R)
        lw2, lb2 = lin(ks[7], R, R)
        out_w, out_b = lin(ks[8], R, H * DH)
        return dict(x=x, u_w=u_w, u_b=u_b, v_w=v_w, v_b=v_b, o_w=o_w, o_b=o_b, pos_w=pos_w, pos_b=pos_b, lw0=lw0, lb0=lb0, lw1=lw1, lb1=lb1, lw2=lw2, lb2=lb2, out_w=out_w, out_b=out_b)
    _L0_attn_in = _L0_attn_setup()

    def _L0_ffn_setup():
        import jax, jax.numpy as jnp
        import numpy as np
        HIDDEN = 256
        N_ROUTED = 16
        N_SHARED = 2
        TOP_K = 2
        MID_R = HIDDEN // 4
        MID_S = HIDDEN // 2
        key = jax.random.key(seed)
        ks = jax.random.split(key, 8)
        s = 0.02
        return {'x': jax.random.normal(ks[0], (2, 256, HIDDEN), dtype=jnp.float32), 'router_w': jax.random.normal(ks[1], (HIDDEN, N_ROUTED), dtype=jnp.float32) * s, 'wg_r': jax.random.normal(ks[2], (N_ROUTED, HIDDEN, MID_R), dtype=jnp.float32) * s, 'wu_r': jax.random.normal(ks[3], (N_ROUTED, HIDDEN, MID_R), dtype=jnp.float32) * s, 'wd_r': jax.random.normal(ks[4], (N_ROUTED, MID_R, HIDDEN), dtype=jnp.float32) * s, 'wg_s': jax.random.normal(ks[5], (N_SHARED, HIDDEN, MID_S), dtype=jnp.float32) * s, 'wu_s': jax.random.normal(ks[6], (N_SHARED, HIDDEN, MID_S), dtype=jnp.float32) * s, 'wd_s': jax.random.normal(ks[7], (N_SHARED, MID_S, HIDDEN), dtype=jnp.float32) * s}
    _L0_ffn_in = _L0_ffn_setup()

    def _L1_attn_setup():
        import jax, jax.numpy as jnp
        import numpy as np
        from jax import lax
        D_MODEL, D_INNER, D_STATE, D_CONV, DT_RANK = (256, 512, 16, 4, 64)
        B, L = (1, 512)

        def _reference_tuple_inner(x, W_in, conv_w, conv_b, W_x, W_dt, b_dt, A_log, D, W_out):
            b, l, dm = x.shape
            di, n = (A_log.shape[0], A_log.shape[1])
            x_and_res = x @ W_in
            xc, res = (x_and_res[..., :di], x_and_res[..., di:])
            k = conv_w.shape[1]
            xp = jnp.pad(xc, ((0, 0), (k - 1, 0), (0, 0)))
            xconv = conv_b
            for j in range(k):
                xconv = xconv + xp[:, j:j + l, :] * conv_w[:, j]
            xs = jax.nn.silu(xconv)
            x_dbl = xs @ W_x
            dt_r = x_dbl[..., :DT_RANK]
            Bm = x_dbl[..., DT_RANK:DT_RANK + n]
            Cm = x_dbl[..., DT_RANK + n:]
            dt = jax.nn.softplus(dt_r @ W_dt + b_dt)
            A = -jnp.exp(A_log)
            dA = jnp.exp(jnp.einsum('bld,dn->bldn', dt, A))
            dBx = jnp.einsum('bld,bln->bldn', dt, Bm) * xs[..., None]

            def step(h, inp):
                dA_t, dBx_t, C_t = inp
                h = dA_t * h + dBx_t
                y = jnp.einsum('bdn,bn->bd', h, C_t)
                return (h, y)
            h0 = jnp.zeros((b, di, n), x.dtype)
            hT, ys = lax.scan(step, h0, (dA.transpose(1, 0, 2, 3), dBx.transpose(1, 0, 2, 3), Cm.transpose(1, 0, 2)))
            y = ys.transpose(1, 0, 2) + xs * D
            y = y * jax.nn.silu(res)
            out = y @ W_out
            return (out, hT)
        key = jax.random.key(seed)
        ks = jax.random.split(key, 10)
        s = lambda d: 1.0 / np.sqrt(d)
        return {'x': jax.random.normal(ks[0], (B, L, D_MODEL), jnp.float32), 'W_in': jax.random.normal(ks[1], (D_MODEL, 2 * D_INNER), jnp.float32) * s(D_MODEL), 'conv_w': jax.random.normal(ks[2], (D_INNER, D_CONV), jnp.float32) * s(D_CONV), 'conv_b': jax.random.normal(ks[3], (D_INNER,), jnp.float32) * 0.01, 'W_x': jax.random.normal(ks[4], (D_INNER, DT_RANK + 2 * D_STATE), jnp.float32) * s(D_INNER), 'W_dt': jax.random.normal(ks[5], (DT_RANK, D_INNER), jnp.float32) * s(DT_RANK), 'b_dt': jax.random.normal(ks[6], (D_INNER,), jnp.float32) * 0.01, 'A_log': jnp.log(jnp.tile(jnp.arange(1.0, D_STATE + 1.0, dtype=jnp.float32), (D_INNER, 1))), 'D': jnp.ones((D_INNER,), jnp.float32), 'W_out': jax.random.normal(ks[7], (D_INNER, D_MODEL), jnp.float32) * s(D_INNER)}
    _L1_attn_in = _L1_attn_setup()

    def _L1_ffn_setup():
        import jax, jax.numpy as jnp
        import numpy as np
        B, S, D, H, E, K = (4, 256, 256, 512, 8, 2)
        key = jax.random.key(seed)
        ks = jax.random.split(key, 5)
        s = 0.02
        return {'x': jax.random.normal(ks[0], (B, S, D), jnp.float32), 'W1': jax.random.normal(ks[1], (E, H, D), jnp.float32) * s, 'b1': jnp.zeros((E, H), jnp.float32), 'W2': jax.random.normal(ks[2], (E, D, H), jnp.float32) * s, 'b2': jnp.zeros((E, D), jnp.float32), 'Wg': jax.random.normal(ks[3], (E, D), jnp.float32) * s, 'bg': jnp.zeros((E,), jnp.float32)}
    _L1_ffn_in = _L1_ffn_setup()
    _d = {'L0_attn_x': _L0_attn_in['x'], 'L0_attn_u_w': _L0_attn_in['u_w'], 'L0_attn_u_b': _L0_attn_in['u_b'], 'L0_attn_v_w': _L0_attn_in['v_w'], 'L0_attn_v_b': _L0_attn_in['v_b'], 'L0_attn_o_w': _L0_attn_in['o_w'], 'L0_attn_o_b': _L0_attn_in['o_b'], 'L0_attn_pos_w': _L0_attn_in['pos_w'], 'L0_attn_pos_b': _L0_attn_in['pos_b'], 'L0_attn_lw0': _L0_attn_in['lw0'], 'L0_attn_lb0': _L0_attn_in['lb0'], 'L0_attn_lw1': _L0_attn_in['lw1'], 'L0_attn_lb1': _L0_attn_in['lb1'], 'L0_attn_lw2': _L0_attn_in['lw2'], 'L0_attn_lb2': _L0_attn_in['lb2'], 'L0_attn_out_w': _L0_attn_in['out_w'], 'L0_attn_out_b': _L0_attn_in['out_b'], 'L0_ffn_router_w': _L0_ffn_in['router_w'], 'L0_ffn_wg_r': _L0_ffn_in['wg_r'], 'L0_ffn_wu_r': _L0_ffn_in['wu_r'], 'L0_ffn_wd_r': _L0_ffn_in['wd_r'], 'L0_ffn_wg_s': _L0_ffn_in['wg_s'], 'L0_ffn_wu_s': _L0_ffn_in['wu_s'], 'L0_ffn_wd_s': _L0_ffn_in['wd_s'], 'L1_attn_W_in': _L1_attn_in['W_in'], 'L1_attn_conv_w': _L1_attn_in['conv_w'], 'L1_attn_conv_b': _L1_attn_in['conv_b'], 'L1_attn_W_x': _L1_attn_in['W_x'], 'L1_attn_W_dt': _L1_attn_in['W_dt'], 'L1_attn_b_dt': _L1_attn_in['b_dt'], 'L1_attn_A_log': _L1_attn_in['A_log'], 'L1_attn_D': _L1_attn_in['D'], 'L1_attn_W_out': _L1_attn_in['W_out'], 'L1_ffn_W1': _L1_ffn_in['W1'], 'L1_ffn_b1': _L1_ffn_in['b1'], 'L1_ffn_W2': _L1_ffn_in['W2'], 'L1_ffn_b2': _L1_ffn_in['b2'], 'L1_ffn_Wg': _L1_ffn_in['Wg'], 'L1_ffn_bg': _L1_ffn_in['bg']}
    _x0 = _d['L0_attn_x']
    _d['L0_attn_x'] = jax.random.normal(jax.random.fold_in(jax.random.key(seed), 1), (16, 512, 256), dtype=_x0.dtype)
    del _x0
    return _d

def reference(L0_attn_x, L0_attn_u_w, L0_attn_u_b, L0_attn_v_w, L0_attn_v_b, L0_attn_o_w, L0_attn_o_b, L0_attn_pos_w, L0_attn_pos_b, L0_attn_lw0, L0_attn_lb0, L0_attn_lw1, L0_attn_lb1, L0_attn_lw2, L0_attn_lb2, L0_attn_out_w, L0_attn_out_b, L0_ffn_router_w, L0_ffn_wg_r, L0_ffn_wu_r, L0_ffn_wd_r, L0_ffn_wg_s, L0_ffn_wu_s, L0_ffn_wd_s, L1_attn_W_in, L1_attn_conv_w, L1_attn_conv_b, L1_attn_W_x, L1_attn_W_dt, L1_attn_b_dt, L1_attn_A_log, L1_attn_D, L1_attn_W_out, L1_ffn_W1, L1_ffn_b1, L1_ffn_W2, L1_ffn_b2, L1_ffn_Wg, L1_ffn_bg):

    def _L0_attn_ref(x, u_w, u_b, v_w, v_b, o_w, o_b, pos_w, pos_b, lw0, lb0, lw1, lb1, lw2, lb2, out_w, out_b):
        import jax, jax.numpy as jnp
        import numpy as np
        B, N, E = (4, 512, 256)
        H = 8
        D1 = 3 * E
        DH = D1 // H
        R = 128
        GAMMA = 0.99
        EPS = 1e-08

        def _srms(x):
            rms = jnp.linalg.norm(x, axis=-1, keepdims=True) * x.shape[-1] ** (-0.5)
            return x / (rms + EPS)
        b, n, _ = x.shape
        u = jax.nn.silu(x @ u_w + u_b)
        v = jax.nn.silu(x @ v_w + v_b)
        v = v.reshape(b, n, H, DH).transpose(0, 2, 1, 3)
        pos_idx = jnp.arange(n, dtype=x.dtype)[:, None]
        h_ = pos_idx @ pos_w + pos_b
        for w, bb in ((lw0, lb0), (lw1, lb1), (lw2, lb2)):
            h_ = jax.nn.relu(_srms(h_)) @ w + bb
        coefs = jax.nn.relu(_srms(h_)) @ out_w + out_b
        coefs = coefs.reshape(n, H, DH).transpose(1, 0, 2)
        zero = coefs[:, :1]
        pos = coefs[:, 1:]
        decay = GAMMA ** jnp.arange(1, n, dtype=x.dtype)[None, :, None]
        pos = pos * decay
        a = jnp.concatenate([zero, pos, zero], axis=1)
        m = 2 * n
        av = jnp.fft.rfft(a, m, axis=1)
        xv = jnp.fft.rfft(v, m, axis=2)
        tv = jnp.fft.irfft(av[None] * xv, m, axis=2)[:, :, :n, :]
        out = tv.transpose(0, 2, 1, 3).reshape(b, n, H * DH)
        out = u * out
        return out @ o_w + o_b

    def _L0_ffn_ref(x, router_w, wg_r, wu_r, wd_r, wg_s, wu_s, wd_s):
        import jax, jax.numpy as jnp
        import numpy as np
        HIDDEN = 256
        N_ROUTED = 16
        N_SHARED = 2
        TOP_K = 2
        MID_R = HIDDEN // 4
        MID_S = HIDDEN // 2
        orig_shape = x.shape
        flat = x.reshape(-1, orig_shape[-1])
        gs = jnp.einsum('td,ndm->tnm', flat, wg_s)
        us = jnp.einsum('td,ndm->tnm', flat, wu_s)
        out = jnp.einsum('tnm,nmd->td', jax.nn.silu(gs) * us, wd_s)
        logits = (flat @ router_w).astype(jnp.float32)
        probs = jax.nn.softmax(logits, axis=-1)
        weights, indices = jax.lax.top_k(probs, TOP_K)
        weights = weights / (weights.sum(axis=-1, keepdims=True) + 1e-09)
        weights = weights.astype(x.dtype)
        comb = jnp.sum(jax.nn.one_hot(indices, N_ROUTED, dtype=x.dtype) * weights[..., None], axis=1)
        g = jnp.einsum('td,edm->tem', flat, wg_r)
        u = jnp.einsum('td,edm->tem', flat, wu_r)
        h = jax.nn.silu(g) * u
        h = h * comb[:, :, None]
        out = out + jnp.einsum('tem,emd->td', h, wd_r)
        return out.reshape(orig_shape)

    def _L1_attn_ref(x, W_in, conv_w, conv_b, W_x, W_dt, b_dt, A_log, D, W_out):
        import jax, jax.numpy as jnp
        import numpy as np
        from jax import lax
        D_MODEL, D_INNER, D_STATE, D_CONV, DT_RANK = (256, 512, 16, 4, 64)
        B, L = (1, 512)

        def _reference_tuple_inner(x, W_in, conv_w, conv_b, W_x, W_dt, b_dt, A_log, D, W_out):
            b, l, dm = x.shape
            di, n = (A_log.shape[0], A_log.shape[1])
            x_and_res = x @ W_in
            xc, res = (x_and_res[..., :di], x_and_res[..., di:])
            k = conv_w.shape[1]
            xp = jnp.pad(xc, ((0, 0), (k - 1, 0), (0, 0)))
            xconv = conv_b
            for j in range(k):
                xconv = xconv + xp[:, j:j + l, :] * conv_w[:, j]
            xs = jax.nn.silu(xconv)
            x_dbl = xs @ W_x
            dt_r = x_dbl[..., :DT_RANK]
            Bm = x_dbl[..., DT_RANK:DT_RANK + n]
            Cm = x_dbl[..., DT_RANK + n:]
            dt = jax.nn.softplus(dt_r @ W_dt + b_dt)
            A = -jnp.exp(A_log)
            dA = jnp.exp(jnp.einsum('bld,dn->bldn', dt, A))
            dBx = jnp.einsum('bld,bln->bldn', dt, Bm) * xs[..., None]

            def step(h, inp):
                dA_t, dBx_t, C_t = inp
                h = dA_t * h + dBx_t
                y = jnp.einsum('bdn,bn->bd', h, C_t)
                return (h, y)
            h0 = jnp.zeros((b, di, n), x.dtype)
            hT, ys = lax.scan(step, h0, (dA.transpose(1, 0, 2, 3), dBx.transpose(1, 0, 2, 3), Cm.transpose(1, 0, 2)))
            y = ys.transpose(1, 0, 2) + xs * D
            y = y * jax.nn.silu(res)
            out = y @ W_out
            return (out, hT)
        return _reference_tuple_inner(x, W_in, conv_w, conv_b, W_x, W_dt, b_dt, A_log, D, W_out)[0]

    def _L1_ffn_ref(x, W1, b1, W2, b2, Wg, bg):
        import jax, jax.numpy as jnp
        import numpy as np
        B, S, D, H, E, K = (4, 256, 256, 512, 8, 2)
        b, s, d = x.shape
        xt = x.reshape(-1, d)
        gate_logits = xt @ Wg.T + bg
        w, idx = jax.lax.top_k(gate_logits, K)
        w = jax.nn.softmax(w, axis=1)
        h = jax.nn.relu(jnp.einsum('td,ehd->eth', xt, W1) + b1[:, None, :])
        y = jnp.einsum('eth,eoh->eto', h, W2) + b2[:, None, :]
        comb = (jax.nn.one_hot(idx, E, dtype=xt.dtype) * w[..., None]).sum(axis=1)
        out = jnp.einsum('eto,te->to', y, comb)
        return out.reshape(b, s, d)
    x = L0_attn_x
    x = x + _L0_attn_ref(_layernorm(x, axis=-1), L0_attn_u_w, L0_attn_u_b, L0_attn_v_w, L0_attn_v_b, L0_attn_o_w, L0_attn_o_b, L0_attn_pos_w, L0_attn_pos_b, L0_attn_lw0, L0_attn_lb0, L0_attn_lw1, L0_attn_lb1, L0_attn_lw2, L0_attn_lb2, L0_attn_out_w, L0_attn_out_b)
    x = x + _L0_ffn_ref(_layernorm(x, axis=-1), L0_ffn_router_w, L0_ffn_wg_r, L0_ffn_wu_r, L0_ffn_wd_r, L0_ffn_wg_s, L0_ffn_wu_s, L0_ffn_wd_s)
    x = x + _L1_attn_ref(_layernorm(x, axis=-1), L1_attn_W_in, L1_attn_conv_w, L1_attn_conv_b, L1_attn_W_x, L1_attn_W_dt, L1_attn_b_dt, L1_attn_A_log, L1_attn_D, L1_attn_W_out)
    x = x + _L1_ffn_ref(_layernorm(x, axis=-1), L1_ffn_W1, L1_ffn_b1, L1_ffn_W2, L1_ffn_b2, L1_ffn_Wg, L1_ffn_bg)
    return x

_drawn_inputs = setup_inputs


def setup_inputs(seed=0):
    import zlib

    import numpy as np

    out = dict(_drawn_inputs(seed))
    spreads = {'L1_attn_D': (1.0, 0.6),
     'L1_ffn_b1': (0.0, 0.8),
     'L1_ffn_b2': (0.0, 0.8),
     'L1_ffn_bg': (0.0, 0.8)}
    factors = {'L0_attn_u_b': 2.829,
     'L0_attn_o_b': 8.0,
     'L0_attn_pos_b': 3.01,
     'L0_ffn_router_w': 8.0,
     'L0_ffn_wg_r': 8.0,
     'L0_ffn_wu_r': 8.0,
     'L0_ffn_wd_r': 8.0,
     'L0_ffn_wg_s': 8.0,
     'L0_ffn_wu_s': 8.0,
     'L0_ffn_wd_s': 8.0,
     'L1_attn_conv_b': 42.759,
     'L1_attn_b_dt': 64.0,
     'L1_attn_A_log': 39.853,
     'L1_ffn_W1': 7.399,
     'L1_ffn_W2': 5.904,
     'L1_ffn_Wg': 5.19,
     'L1_attn_W_dt': 2.944}
    for name, (base, spread) in spreads.items():
        noise = np.random.default_rng([zlib.crc32(name.encode()), seed]).standard_normal(out[name].shape)
        drawn = base * np.exp(spread * noise) if base else spread * noise
        out[name] = jnp.asarray(drawn.astype(out[name].dtype))
    for name, factor in factors.items():
        out[name] = (out[name] * factor).astype(out[name].dtype)
    return out
```

```python
from contextlib import ExitStack

import numpy as np

import concourse.bass as bass
from concourse import mybir

FP32 = mybir.dt.float32
BF16 = mybir.dt.bfloat16
U32 = mybir.dt.uint32
ALU = mybir.AluOpType
ACT = mybir.ActivationFunctionType
AX = mybir.AxisListType

P = 128
B, L, E = 16, 512, 256
NT = L // P
KE = E // P
LN_EPS = 1e-5

R = 128
D1 = 768
NCG = D1 // P
SRMS_EPS = 1e-8
PAD = P - 1
ROW = PAD + L + 1
CT = 4
NCH = P // CT
RING_T = 4
CB = 8
NJ = NT * B


def position_coefficients(nc, c, pad_dram):
    ctx = ExitStack()
    with ctx:
        def sb(name, shape, dt=FP32):
            return ctx.enter_context(nc.sbuf_tensor(name, shape, dt))

        def sem(name):
            return ctx.enter_context(nc.semaphore(name))

        ident = sb("p_ident", [P, P])
        positions = sb("p_positions", [P, NT])
        first_w = sb("p_first_w", [P, R])
        first_b = sb("p_first_b", [P, R])
        layer_w = sb("p_layer_w", [P, 3, R])
        layer_b = sb("p_layer_b", [P, 3, R])
        out_w = sb("p_out_w", [P, D1])
        out_b = sb("p_out_b", [P, NCG])
        decay = sb("p_decay", [P, L])
        h = sb("p_h", [P, NT, R])
        square = sb("p_square", [P, NT, R])
        norm = sb("p_norm", [P, NT])
        rms = sb("p_rms", [P, NT])
        inverse = sb("p_inverse", [P, NT])
        active = sb("p_active", [P, NT, R])
        activeT = sb("p_activeT", [P, L])
        raw = sb("p_raw", [P, NCG, L])
        padded = sb("p_padded", [P, NCG, ROW])
        pT = ctx.enter_context(nc.psum_tensor("p_pT", [P, L], FP32))
        pH = ctx.enter_context(nc.psum_tensor("p_pH", [P, NT, R], FP32))
        pC = [ctx.enter_context(nc.psum_tensor(f"p_pC{i}", [P, L], FP32)) for i in range(2)]

        loaded = sem("p_loaded")
        h_ready = sem("p_h_ready")
        squared = sem("p_squared")
        summed = sem("p_summed")
        rooted = sem("p_rooted")
        step = sem("p_step")
        active_ready = sem("p_active")
        turned = sem("p_turned")
        turned_out = sem("p_turned_out")
        layer_done = sem("p_layer_done")
        coef_done = sem("p_coef_done")
        coef_out = sem("p_coef_out")
        zeroed = sem("p_zeroed")
        decayed = sem("p_decayed")
        stored = sem("p_stored")

        block = ctx.enter_context(nc.Block())

        @block.sync
        def _(sp):
            for dst, src in ((ident[:, :], c["ident"]), (positions[:, :], c["positions"]),
                             (first_w[:, :], c["pos_w"].partition_broadcast(P)),
                             (first_b[:, :], c["pos_b"].partition_broadcast(P)),
                             (layer_w[:, :, :], c["layer_w"]),
                             (layer_b[:, :, :], c["layer_b"].partition_broadcast(P)),
                             (out_w[:, :], c["out_w"]), (out_b[:, :], c["out_b"]),
                             (decay[:, :], c["decay"].partition_broadcast(P))):
                sp.dma_start(dst, src).then_inc(loaded, 16)
            sp.wait_ge(decayed, NCG)
            sp.dma_start(pad_dram.rearrange("(g p) r -> p g r", p=P), padded[:, :, :]).then_inc(stored, 16)
            sp.wait_ge(stored, 16)

        @block.gpsimd
        def _(pool):
            nc.gpsimd.memset(padded[:, :, :], 0.0).then_inc(zeroed, 1)

        @block.vector
        def _(dve):
            steps = 0
            dve.wait_ge(loaded, 16 * 9)
            for i in range(NT):
                nc.vector.scalar_tensor_tensor(h[:, i, :], first_w[:, :], positions[:, i:i + 1], first_b[:, :],
                                               ALU.mult, ALU.add).then_inc(h_ready, 1)
            for layer in range(4):
                dve.wait_ge(h_ready, NT if layer == 0 else NT + layer)
                nc.vector.tensor_tensor(square[:, :, :], h[:, :, :], h[:, :, :], ALU.mult).then_inc(squared, 1)
                dve.wait_ge(squared, layer + 1)
                nc.vector.tensor_reduce(norm[:, :], square[:, :, :], AX.X, ALU.add).then_inc(summed, 1)
                dve.wait_ge(rooted, layer + 1)
                nc.vector.tensor_scalar(rms[:, :], rms[:, :], float(R) ** -0.5, SRMS_EPS, ALU.mult,
                                        ALU.add).then_inc(step, 1)
                steps += 1
                dve.wait_ge(step, steps)
                nc.vector.reciprocal(inverse[:, :], rms[:, :]).then_inc(step, 1)
                steps += 1
                dve.wait_ge(step, steps)
                for i in range(NT):
                    nc.vector.tensor_scalar(active[:, i, :], h[:, i, :], inverse[:, i:i + 1], 0.0, ALU.mult,
                                            ALU.max).then_inc(active_ready, 1)
                if layer < 3:
                    dve.wait_ge(layer_done, layer + 1)
                    dve.wait_ge(active_ready, NT * (layer + 1))
                    bias = layer_b[:, layer:layer + 1, :].to_broadcast([P, NT, R])
                    nc.vector.tensor_tensor(h[:, :, :], pH[:, :, :], bias, ALU.add).then_inc(h_ready, 1)
            dve.wait_ge(zeroed, 1)
            for g in range(NCG):
                dve.wait_ge(coef_out, g + 1)
                nc.vector.tensor_tensor(padded[:, g, PAD:PAD + L], raw[:, g, :], decay[:, :],
                                        ALU.mult).then_inc(decayed, 1)

        @block.scalar
        def _(act):
            for layer in range(4):
                act.wait_ge(summed, layer + 1)
                nc.scalar.activation(rms[:, :], norm[:, :], ACT.Sqrt).then_inc(rooted, 1)
                act.wait_ge(turned, layer + 1)
                nc.scalar.copy(activeT[:, :], pT[:, :]).then_inc(turned_out, 1)
            for g in range(NCG):
                act.wait_ge(coef_done, g + 1)
                nc.scalar.activation(raw[:, g, :], pC[g % 2][:, :], ACT.Identity,
                                     bias=out_b[:, g:g + 1]).then_inc(coef_out, 1)

        @block.tensor
        def _(pe):
            pe.wait_ge(loaded, 16 * 9)
            for layer in range(4):
                pe.wait_ge(active_ready, NT * (layer + 1))
                for i in range(NT):
                    last = nc.tensor.transpose(pT[:, i * P:(i + 1) * P], active[:, i, :], ident[:, :])
                last.then_inc(turned, 1)
                pe.wait_ge(turned_out, layer + 1)
                if layer < 3:
                    for i in range(NT):
                        last = nc.tensor.matmul(pH[:, i, :], activeT[:, i * P:(i + 1) * P], layer_w[:, layer, :],
                                                start=True, stop=True)
                    last.then_inc(layer_done, 1)
            for g in range(NCG):
                if g >= 2:
                    pe.wait_ge(coef_out, g - 1)
                nc.tensor.matmul(pC[g % 2][:, :], out_w[:, g * P:(g + 1) * P], activeT[:, :],
                                 start=True, stop=True).then_inc(coef_done, 1)


def toeplitz_unit(nc, c, x_dram, pad_dram, gated_dram):
    ctx = ExitStack()
    with ctx:
        def sb(name, shape, dt=FP32):
            return ctx.enter_context(nc.sbuf_tensor(name, shape, dt))

        def sem(name):
            return ctx.enter_context(nc.semaphore(name))

        ident = sb("t_ident", [P, P])
        half = sb("t_half", [P, NT])
        xnT = sb("t_xnT", [P, KE, B * L])
        V = sb("t_V", [P, P, NJ])
        G = sb("t_G", [P, NJ, P])
        T = sb("t_T", [P, RING_T, CT, L])
        x = sb("t_x", [P, 2, NT, E])
        xn = sb("t_xn", [P, 2, NT, E])
        stats = sb("t_stats", [P, 2, NT, 6])
        moments = sb("t_moments", [P, 2, NT, 2])
        shifted = sb("t_shifted", [P, 2, NT])
        rstd = sb("t_rstd", [P, 2, NT])
        v_w = sb("t_v_w", [P, KE, P])
        u_w = sb("t_u_w", [P, KE, P])
        v_b = sb("t_v_b", [P, P])
        u_b = sb("t_u_b", [P, NCG])
        v_sum = sb("t_v_sum", [P, 2, NT, P])
        u = sb("t_u", [P, 2, L])
        gated = sb("t_gated", [P, 2, L])
        bank = [ctx.enter_context(nc.psum_tensor(f"t_bank{i}", [P, L], FP32)) for i in range(8)]
        v_bank, conv_bank, u_bank, turn_bank = bank[0:2], bank[2:4], bank[4:6], bank[6:8]

        const_in = sem("t_const_in")
        half_set = sem("t_half_set")
        x_in = [sem(f"t_x_in{r}") for r in range(2)]
        stat_done = sem("t_stat")
        var_done = sem("t_var")
        eps_added = sem("t_eps")
        rstd_done = sem("t_rstd_done")
        xn_done = sem("t_xn_done")
        xnT_done = sem("t_xnT_done")
        xnT_out = sem("t_xnT_out")
        w_in = sem("t_w_in")
        v_done = sem("t_v_done")
        v_biased = sem("t_v_biased")
        v_out = sem("t_v_out")
        T_in = [sem(f"t_T_in{r}") for r in range(RING_T)]
        T_used = sem("t_T_used")
        conv_out = sem("t_conv_out")
        u_done = sem("t_u_done")
        u_out = sem("t_u_out")
        turned = sem("t_turned")
        gated_done = sem("t_gated_done")
        stored = [sem(f"t_stored{r}") for r in range(2)]

        passed = sem("t_passed")

        block = ctx.enter_context(nc.Block())
        x_v = x_dram.rearrange("b (i p) e -> b p i e", p=P)

        @block.sync
        def _(sp):
            sp.dma_start(ident[:, :], c["ident"]).then_inc(const_in, 16)
            sp.dma_start(u_b[:, :], c["u_b"]).then_inc(const_in, 16)
            with sp.Fori(0, B // 2) as pair:
                for r in range(2):
                    sp.wait_ge(xn_done, 2 * NT * pair + 1)
                    sp.dma_start(x[:, r, :, :], x_v[bass.ds(2 * pair + r, 1), :, :, :].rearrange("o p i e -> p (o i) e"))\
                        .then_inc(x_in[r], 16)
            with sp.Fori(0, NCG) as g:
                sp.wait_ge(u_done, B * g + 1)
                sp.wait_ge(v_biased, B * g + 1)
                sp.dma_start(v_w[:, :, :], c["v_w"][bass.ds(g, 1), :, :, :].rearrange("o p k n -> p (o k) n"))\
                    .then_inc(w_in, 16)
                sp.dma_start(u_w[:, :, :], c["u_w"][bass.ds(g, 1), :, :, :].rearrange("o p k n -> p (o k) n"))\
                    .then_inc(w_in, 16)
                sp.dma_start(v_b[:, :], c["v_b"][bass.ds(g, 1), :].partition_broadcast(P)
                             .rearrange("p o n -> p (o n)")).then_inc(w_in, 16)
                for ch in range(NCH):
                    r = ch % RING_T
                    if ch >= RING_T:
                        sp.wait_ge(T_used, g * NCH + ch - RING_T + 1 + 1)
                    else:
                        sp.wait_ge(T_used, g * NCH + 1)
                    src = bass.AP(pad_dram.tensor, g * (P * ROW) + ch * CT * ROW, [[1, P], [ROW, CT], [1, L]])
                    sp.dma_start(T[:, r, :, :], src).then_inc(T_in[r], 16)
                for b in range(B):
                    r = b % 2
                    sp.wait_ge(gated_done, g * B + b + 1 + 1)
                    sp.dma_start(gated_dram[bass.ds(g, 1), :, b, :].rearrange("o p t -> p (o t)"), gated[:, r, :])\
                        .then_inc(stored[r], 16)
            for r in range(2):
                sp.wait_ge(stored[r], 16 * NCG * B // 2 + 1)

        @block.gpsimd
        def _(pool):
            nc.gpsimd.memset(half[:, :], -0.5).then_inc(half_set, 1)
            pool.wait_ge(half_set, 1)
            with pool.Fori(0, B // 2) as pair:
                for r in range(2):
                    pool.wait_ge(var_done, (2 * pair + r + 1) * NT)
                    pool.sem_inc(passed, 1)
                    nc.gpsimd.tensor_scalar(shifted[:, r, :], moments[:, r, :, 1], LN_EPS, None,
                                            ALU.add).then_inc(eps_added, 1)
                    pool.wait_ge(eps_added, 2 * pair + r + 1)
                    nc.gpsimd.tensor_tensor(rstd[:, r, :], shifted[:, r, :], half[:, :], ALU.pow)\
                        .then_inc(rstd_done, 1)

        @block.vector
        def _(dve):
            for s in (xn_done, u_done, v_biased, T_used, xnT_done, v_out, conv_out, gated_done, u_out, xnT_out,
                      *stored):
                dve.sem_inc(s, 1)
            with dve.Fori(0, B // 2) as pair:
                for r in range(2):
                    s = 2 * pair + r
                    dve.wait_ge(x_in[r], (pair + 1) * 16)
                    for i in range(NT):
                        nc.vector.bn_stats(stats[:, r, i, :], x[:, r, i, :]).then_inc(stat_done, 1)
                    dve.wait_ge(stat_done, (s + 1) * NT)
                    dve.sem_inc(passed, 1)
                    for i in range(NT):
                        nc.vector.bn_aggr(moments[:, r, i, :], stats[:, r, i, :]).then_inc(var_done, 1)
                    dve.wait_ge(rstd_done, s + 1)
                    dve.wait_ge(var_done, (s + 1) * NT)
                    dve.wait_ge(xnT_done, 2 * pair + 1)
                    for i in range(NT):
                        last = nc.vector.tensor_scalar(xn[:, r, i, :], x[:, r, i, :], moments[:, r, i, 0:1],
                                                       rstd[:, r, i:i + 1], ALU.subtract, ALU.mult)
                        last.then_inc(xn_done, 1)
            with dve.Fori(0, NCG) as g:
                dve.wait_ge(w_in, (g + 1) * 48)
                for b in range(B):
                    dve.wait_ge(v_done, g * B + b + 1)
                    if b >= 2:
                        dve.wait_ge(v_out, g * B + b - 1 + 1)
                    else:
                        dve.wait_ge(v_out, g * B + 1)
                    psum = v_bank[b % 2][:, :].rearrange("p (i n) -> p i n", n=P)
                    bias = v_b[:, :].unsqueeze(1).to_broadcast([P, NT, P])
                    nc.vector.tensor_tensor(v_sum[:, b % 2, :, :], psum, bias, ALU.add).then_inc(v_biased, 1)
                for m in range(P // CB):
                    dve.wait_ge(T_used, g * NCH + (m + 1) * CB // CT + 1)
                    src = conv_bank[m % 2][:, :].rearrange("p (c j) -> p j c", c=CB)
                    nc.vector.tensor_copy(G[:, :, m * CB:(m + 1) * CB], src).then_inc(conv_out, 1)
                for b in range(B):
                    dve.wait_ge(turned, g * B + b + 1)
                    dve.wait_ge(u_out, g * B + b + 1 + 1)
                    dve.wait_ge(stored[b % 2], 16 * (g * (B // 2) + b // 2) + 1)
                    backwards = u[:, b % 2, :].rearrange("p (i t) -> p i t", t=P)[:, :, ::-1]
                    nc.vector.tensor_tensor(gated[:, b % 2, :].rearrange("p (i t) -> p i t", t=P),
                                            turn_bank[b % 2][:, :].rearrange("p (i t) -> p i t", t=P), backwards,
                                            ALU.mult).then_inc(gated_done, 1)

        @block.scalar
        def _(act):
            with act.Fori(0, B // 2) as pair:
                for r in range(2):
                    act.wait_ge(xnT_done, 2 * pair + r + 1 + 1)
                    act.sem_inc(passed, 1)
                    for k in range(KE):
                        nc.scalar.copy(xnT[:, k, bass.ds((2 * pair + r) * L, L)],
                                       bank[2 * r + k][:, :]).then_inc(xnT_out, 1)
            act.wait_ge(const_in, 32)
            with act.Fori(0, NCG) as g:
                for b in range(B):
                    act.wait_ge(v_biased, g * B + b + 1 + 1)
                    if b == 0:
                        act.wait_ge(T_used, g * NCH + 1)
                    dst = V[:, :, :].rearrange("p c (i b) -> p i c b", b=B)[:, :, :, b]
                    nc.scalar.activation(dst, v_sum[:, b % 2, :, :], ACT.Silu).then_inc(v_out, 1)
                for b in range(B):
                    act.wait_ge(u_done, g * B + b + 1 + 1)
                    if b >= 2:
                        act.wait_ge(gated_done, g * B + b - 1 + 1)
                    else:
                        act.wait_ge(gated_done, g * B + 1)
                    act.sem_inc(passed, 1)
                    nc.scalar.activation(u[:, b % 2, :], u_bank[b % 2][:, :], ACT.Silu,
                                         bias=u_b[:, bass.ds(g, 1)]).then_inc(u_out, 1)

        @block.tensor
        def _(pe):
            pe.wait_ge(const_in, 32)
            with pe.Fori(0, B // 2) as pair:
                for r in range(2):
                    pe.wait_ge(xn_done, (2 * pair + r + 1) * NT + 1)
                    pe.wait_ge(xnT_out, 2 * KE * pair + 1)
                    for k in range(KE):
                        for i in range(NT):
                            last = nc.tensor.transpose(bank[2 * r + k][:, i * P:(i + 1) * P],
                                                       xn[:, r, i, k * P:(k + 1) * P], ident[:, :])
                    last.then_inc(xnT_done, 1)
            pe.wait_ge(xnT_out, KE * B + 1)
            with pe.Fori(0, NCG) as g:
                pe.wait_ge(w_in, (g + 1) * 48)
                for b in range(B):
                    if b >= 2:
                        pe.wait_ge(v_biased, g * B + b - 1 + 1)
                    else:
                        pe.wait_ge(v_biased, g * B + 1)
                    for i in range(NT):
                        for k in range(KE):
                            last = nc.tensor.matmul(v_bank[b % 2][:, i * P:(i + 1) * P],
                                                    xnT[:, k, b * L + i * P:b * L + (i + 1) * P], v_w[:, k, :],
                                                    start=(k == 0), stop=(k == KE - 1))
                    last.then_inc(v_done, 1)
                pe.wait_ge(v_out, (g + 1) * B + 1)
                for ch in range(NCH):
                    r, m = ch % RING_T, ch * CT // CB
                    pe.wait_ge(T_in[r], (g * (NCH // RING_T) + ch // RING_T + 1) * 16)
                    if ch * CT % CB == 0:
                        if m >= 2:
                            pe.wait_ge(conv_out, g * (P // CB) + m - 1 + 1)
                        else:
                            pe.wait_ge(conv_out, g * (P // CB) + 1)
                    for q in range(CT):
                        chan = ch * CT + q
                        at = (chan % CB) * NJ
                        for lag in range(NT):
                            n = (NT - lag) * B
                            last = nc.tensor.matmul(conv_bank[m % 2][:, at + lag * B:at + NJ],
                                                    T[:, r, q, lag * P:(lag + 1) * P], V[:, chan, 0:n],
                                                    start=(lag == 0), stop=(lag == NT - 1))
                    last.then_inc(T_used, 1)
                pe.wait_ge(conv_out, (g + 1) * (P // CB) + 1)
                for b in range(B):
                    if b >= 2:
                        pe.wait_ge(u_out, g * B + b - 1 + 1)
                    else:
                        pe.wait_ge(u_out, g * B + 1)
                    for k in range(KE):
                        last = nc.tensor.matmul(u_bank[b % 2][:, :], u_w[:, k, :], xnT[:, k, b * L:(b + 1) * L],
                                                start=(k == 0), stop=(k == KE - 1))
                    last.then_inc(u_done, 1)
                    if b >= 2:
                        pe.wait_ge(gated_done, g * B + b - 1 + 1)
                    else:
                        pe.wait_ge(gated_done, g * B + 1)
                    for i in range(NT):
                        last = nc.tensor.transpose(turn_bank[b % 2][:, i * P:(i + 1) * P], G[:, i * B + b, :],
                                                   ident[:, :])
                    last.then_inc(turned, 1)


E0 = 16
H0 = 10
H0R = 8
DI = 512
NB = DI // P
N = 16
RK = 64
TAPS = 4
E1 = 8
H1 = 4
WEIGHT_EPS = 1e-9
A_LOG_MAX = 83.0
HALF = NB // 2


class Products:

    def __init__(self, sem, name, banks, order):
        self.ready = sem(f"{name}_ready")
        self.freed = [sem(f"{name}_freed{i}") for i in range(len(banks))]
        self.banks, self.total, uses = banks, len(order), [0] * len(banks)
        self.place = {}
        for i, key in enumerate(order):
            bank = i % len(banks)
            self.place[key] = (i, bank, uses[bank])
            uses[bank] += 1
        self.uses = uses

    def psum(self, *key):
        return self.banks[self.place[key][1]]

    def free(self, *key):
        return self.freed[self.place[key][1]]

    def before(self, seq, *key):
        _, bank, nth = self.place[key]
        return seq * self.uses[bank] + nth + 1

    def wait_read(self, engine, seq, *key):
        engine.wait_ge(self.free(*key), self.before(seq, *key) + 1)

    def done(self, seq, *key):
        return seq * self.total + self.place[key][0] + 1


class Steps:

    def __init__(self, engine, sem, per_seq, seq):
        self.engine, self.sem, self.per_seq, self.seq, self.n = engine, sem, per_seq, seq, 0

    def mark(self, instruction):
        instruction.then_inc(self.sem, 1)
        self.n += 1
        return self.n

    def wait(self, n=None):
        self.engine.wait_ge(self.sem, self.seq * self.per_seq + (self.n if n is None else n))

    def close(self):
        assert self.n == self.per_seq, (self.sem, self.n)


def mixtures_and_scan(nc, c, x_dram, gated_dram, out_dram):
    ctx = ExitStack()
    with ctx:
        def sb(name, shape, dt=FP32):
            return ctx.enter_context(nc.sbuf_tensor(name, shape, dt))

        def sem(name):
            return ctx.enter_context(nc.semaphore(name))

        ident = sb("ident", [P, P])
        half = sb("half", [P, NT])
        iota = sb("iota", [P, E0])
        pick32f = sb("pick32f", [96, 32])
        pick32 = sb("pick32", [96, 32], BF16)
        o_w = sb("o_w", [P, NCG, E])
        o_b = sb("o_b", [P, E])
        router_w = sb("router_w", [P, KE, E0])
        g_w = sb("g_w", [P, KE, H0, P])
        up_w = sb("up_w", [P, KE, H0, P])
        down_w = sb("down_w", [P, H0, E])
        in_w = sb("in_w", [P, KE, 2 * NB, P])
        conv_w = sb("conv_w", [P, NB, TAPS])
        conv_b = sb("conv_b", [P, NB])
        x_w = sb("x_w", [P, NB, RK + 96])
        shared = sb("shared", [P, L])
        dt_w = shared[0:RK, :].rearrange("p (j n) -> p j n", n=P)
        picks = shared[64:64 + 3 * E0, :].bitcast(BF16).rearrange("p (j n) -> p j n", n=P)
        dt_b = sb("dt_b", [P, NB])
        A = sb("A", [P, NB, N])
        D = sb("D", [P, NB])
        y_w = sb("y_w", [P, NB, E])
        gate_w = sb("gate_w", [P, KE, E1])
        gate_b = sb("gate_b", [P, E1])
        b1 = sb("b1", [P, E1, H1])
        b2 = sb("b2", [E1, E])
        w12 = sb("w12", [P, 2, KE * H1 * P + H1 * E])

        def norm_buffers(name, x, xn):
            class Norm:
                pass
            n = Norm()
            n.x, n.xn = x, xn
            n.stats = sb(f"{name}_stats", [P, NT, 6])
            n.moments = sb(f"{name}_moments", [P, NT, 2])
            n.shifted = sb(f"{name}_shifted", [P, NT])
            n.rstd = sb(f"{name}_rstd", [P, NT])
            n.xT = sb(f"{name}_xT", [P, KE, L])
            n.stat_done = sem(f"{name}_stat")
            n.var_done = sem(f"{name}_var")
            n.eps_added = sem(f"{name}_eps")
            n.rstd_done = sem(f"{name}_rstd_done")
            n.xn_done = sem(f"{name}_xn")
            return n

        def route_buffers(name, experts, copies):
            class Route:
                pass
            r = Route()
            r.experts = experts
            r.logits = sb(f"{name}_logits", [P, NT, experts])
            r.top = sb(f"{name}_top", [P, NT, 8])
            r.index = sb(f"{name}_index", [P, NT, 8], U32)
            r.indexf = sb(f"{name}_indexf", [P, NT, 2])
            r.gap = sb(f"{name}_gap", [P, NT, experts + 1])
            r.exp = r.gap
            r.total = sb(f"{name}_total", [P, NT, 1])
            r.weight = sb(f"{name}_weight", [P, NT, 2])
            r.one = sb(f"{name}_one", [P, NT, experts])
            r.two = sb(f"{name}_two", [P, NT, experts])
            r.comb = sb(f"{name}_comb", [P, NT, copies, experts])
            r.gap_done = sem(f"{name}_gap_done")
            r.exp_done = sem(f"{name}_exp_done")
            r.comb_done = sem(f"{name}_comb_done")
            return r

        f0_x = sb("f0_x", [P, NT, E])
        f0_h = sb("f0_h", [P, H0, L])
        f0_act = sb("f0_act", [P, 2, L])
        f0 = norm_buffers("f0", f0_x, f0_act[:, :, :].rearrange("p a (b e) -> p (a b) e", e=E))
        combT = sb("combT", [P, L])
        comb1T = combT[0:E1, :]
        parts = combT[64:64 + 3 * E0, 0:L // 2].bitcast(BF16)
        parts_rest = f0_act[64:64 + 2 * E0, 0, :]
        r0 = route_buffers("r0", E0, 3)
        m_x = sb("m_x", [P, NT, E])
        m_xc = sb("m_xc", [P, NB, TAPS - 1 + L])
        m_xs = sb("m_xs", [P, NB, L])
        m_res = sb("m_res", [P, NB, L])
        m_bc = sb("m_bc", [96, L], BF16)
        m_dt = sb("m_dt", [P, NB, L])
        m_dA = sb("m_dA", [P, NB, L])
        picks_f = m_dA[64:64 + 3 * E0, 0:2, :].rearrange("p a (b n) -> p (a b) n", n=P)
        m_dBx = sb("m_dBx", [P, NB, L])
        m_h = sb("m_h", [P, NB, L])
        m_B = sb("m_B", [P, 2, L])
        m_rest = m_B[0:64, 0, :]
        m_dtr = m_B[0:RK, 1, :]
        m_xn = m_h[:, 0:2, :].rearrange("p a (b e) -> p (a b) e", e=E)
        m = norm_buffers("m", f0_x, m_xn)
        f1_x = sb("f1_x", [P, NT, E])
        f1_h = sb("f1_h", [P, 2, H1, L])
        f1_acc = sb("f1_acc", [P, NT, E])
        f1_xn = f1_h[:, 1, 0:2, :].rearrange("p a (b e) -> p (a b) e", e=E)
        f1 = norm_buffers("f1", f1_x, f1_xn)
        r1 = route_buffers("r1", E1, 1)

        bank = [ctx.enter_context(nc.psum_tensor(f"bank{i}", [P, L], FP32)) for i in range(8)]
        pm = Products(sem, "pm", bank[0:2],
                      [("xT", k) for k in range(KE)] + [("xc", j) for j in range(NB)] + [("res", j) for j in range(NB)]
                      + [("dtr",), ("bc",)] + [("dt", j) for j in range(NB)]
                      + [(w, n) for n in range(N) for w in ("B", "C")] + [("out", i) for i in range(NT)])
        p0 = Products(sem, "p0", bank[2:5],
                      [("o", i) for i in range(NT)] + [("xT", k) for k in range(KE)] + [("logits",), ("combT",)]
                      + [(w, j) for j in range(H0) for w in ("g", "up", "comb") if j < H0R or w != "comb"]
                      + [("down", i) for i in range(NT)])
        p1 = Products(sem, "p1", bank[5:8],
                      [("xT", k) for k in range(KE)] + [("logits",), ("combT",)] + [("b2", i) for i in range(NT)]
                      + [(w, e, j) for e in range(E1) for w in ("z", "y") for j in range(4)])

        loaded = sem("loaded")
        half_set = sem("half_set")
        pick_set = sem("pick_set")
        pad_set = sem("pad_set")
        A_done = sem("A_done")
        passed = sem("passed")
        x_in = sem("x_in")
        gated_in = sem("gated_in")
        x_biased = sem("x_biased")
        x2_copied = sem("x2_copied")
        comb_high = sem("comb_high")
        comb_parts = sem("comb_parts")
        f0_step = sem("f0_step")
        m_step = sem("m_step")
        f1_step = sem("f1_step")
        conv_done = sem("conv_done")
        xs_done = sem("xs_done")
        high_out = sem("high_out")
        parts_done = sem("parts_done")
        soft_in = sem("soft_in")
        soft_exp = sem("soft_exp")
        soft_log = sem("soft_log")
        soft_lin = sem("soft_lin")
        soft_low = sem("soft_low")
        dt_done = sem("dt_done")
        dA_zero = sem("dA_zero")
        dtx_done = sem("dtx_done")
        y_begun = sem("y_begun")
        dA_done = sem("dA_done")
        dBx_done = sem("dBx_done")
        scanned = sem("scanned")
        m_product = sem("m_product")
        xc_copied = sem("xc_copied")
        summed = sem("summed")
        y_done = sem("y_done")
        w12_in = [sem(f"w12_in{r}") for r in range(2)]
        stored = sem("stored")

        block = ctx.enter_context(nc.Block())

        consts = [(ident[:, :], c["ident"]), (iota[:, :], c["iota"].partition_broadcast(P)),
                  (picks_f, c["picks"]), (pick32f[:, :], c["pick32"]),
                  (o_w[:, :, :], c["o_w"]), (o_b[:, :], c["o_b"].partition_broadcast(P)),
                  (router_w[:, :, :], c["router_w"]), (g_w[:, :, :, :], c["g_w"]), (up_w[:, :, :, :], c["up_w"]),
                  (down_w[:, :, :], c["down_w"]), (in_w[:, :, :, :], c["in_w"]), (conv_w[:, :, :], c["conv_w"]),
                  (conv_b[:, :], c["conv_b"]), (x_w[:, :, :], c["x_w"]), (dt_w, c["dt_w"]),
                  (dt_b[:, :], c["dt_b"]), (A[:, :, :], c["A_log"]), (D[:, :], c["D"]), (y_w[:, :, :], c["y_w"]),
                  (gate_w[:, :, :], c["gate_w"]), (gate_b[:, :], c["gate_b"].partition_broadcast(P)),
                  (b1[:, :, :], c["b1"]), (b2[:, :], c["b2"])]
        LOADED = 16 * len(consts)
        W1 = KE * H1 * P
        w1 = [w12[:, r, 0:W1].rearrange("p (k n) -> p k n", k=KE) for r in range(2)]
        w2 = [w12[:, r, W1:].rearrange("p (j n) -> p j n", j=H1) for r in range(2)]
        dtx = m_xc[:, :, TAPS - 1:]

        def turns(engine, turn):
            turn(0, True, False, False, True)
            turn(1, True, True, False, True)
            with engine.Fori(2, B - 1) as t:
                turn(t, True, True, True, True)
            turn(B - 1, True, True, True, False)
            turn(B, False, True, True, False)
            turn(B + 1, False, False, True, False)

        @block.sync
        def _(sp):
            for dst, src in consts:
                sp.dma_start(dst, src).then_inc(loaded, 16)

            def load_x(seq):
                sp.sem_inc(passed, 1)
                sp.dma_start(f0_x[:, :, :], x_dram[bass.ds(seq, 1), :, :].rearrange("o (i p) e -> p (o i) e", p=P))\
                    .then_inc(x_in, 16)

            def load_gated(seq):
                sp.sem_inc(passed, 1)
                sp.dma_start(f0_h[:, 0:NCG, :], gated_dram[:, :, bass.ds(seq, 1), :].rearrange("g p o t -> p g (o t)"))\
                    .then_inc(gated_in, 16)

            def load_expert(e):
                sp.dma_start(w12[:, e % 2, :], c["w12"][e]).then_inc(w12_in[e % 2], 16)

            load_gated(0)
            for e in range(2):
                load_expert(e)

            def turn(t, first, scan, second, more):
                if first:
                    if scan:
                        sp.wait_ge(m.xn_done, NT * t)
                        sp.wait_ge(x2_copied, t)
                    load_x(t)
                if second:
                    for e in range(2, E1 + 2):
                        if e == E1 + 1 and more:
                            sp.wait_ge(p0.ready, p0.done(t, "down", NT - 1))
                            load_gated(t + 1)
                        if e < E1 or first or scan:
                            sp.wait_ge(p1.ready, p1.done(t - 2, "y", e - 2, NT - 1))
                            load_expert(e % E1)
                    for i in range(1, NT):
                        p1.wait_read(sp, t - 2, "y", E1 - 1, i)
                        sp.sem_inc(passed, 1)
                    sp.dma_start(out_dram[bass.ds(t - 2, 1), :, :].rearrange("o (i p) e -> p (o i) e", p=P),
                                 f1_acc[:, :, :]).then_inc(stored, 16)
                elif more:
                    sp.wait_ge(p0.ready, p0.done(t, "down", NT - 1))
                    load_gated(t + 1)

            turns(sp, turn)
            sp.wait_ge(stored, 16 * B + 1)

        @block.gpsimd
        def _(pool):
            nc.gpsimd.memset(half[:, :], -0.5).then_inc(half_set, 1)
            nc.gpsimd.memset(m_xc[:, :, 0:TAPS - 1], 0.0).then_inc(pad_set, 1)
            pool.wait_ge(half_set, 1)
            pool.wait_ge(loaded, LOADED)

            def rstd(n, seq):
                pool.wait_ge(n.var_done, (seq + 1) * NT)
                pool.sem_inc(passed, 1)
                nc.gpsimd.tensor_scalar(n.shifted[:, :], n.moments[:, :, 1], LN_EPS, None, ALU.add)\
                    .then_inc(n.eps_added, 1)
                pool.wait_ge(n.eps_added, seq + 1)
                nc.gpsimd.tensor_tensor(n.rstd[:, :], n.shifted[:, :], half[:, :], ALU.pow)\
                    .then_inc(n.rstd_done, 1)

            def bias_x(seq):
                pool.wait_ge(x_in, 16 * (seq + 1))
                nc.gpsimd.tensor_tensor(f0_x[:, :, :], f0_x[:, :, :],
                                        o_b[:, :].unsqueeze(1).to_broadcast([P, NT, E]), ALU.add)\
                    .then_inc(x_biased, 1)

            def copy_x2(seq):
                for i in range(NT):
                    p0.wait_read(pool, seq, "down", i)
                pool.sem_inc(passed, 1)
                nc.gpsimd.tensor_copy(m_x[:, :, :], f0_x[:, :, :]).then_inc(x2_copied, 1)

            def softplus(seq):
                for j in range(NB):
                    pool.wait_ge(soft_exp, seq * NB + j + 1)
                    pool.sem_inc(passed, 1)
                    nc.gpsimd.tensor_scalar(m_dBx[:, j, :], m_dA[:, j, :], -0.5, 1.0, ALU.mult, ALU.add)\
                        .then_inc(soft_lin, 1)
                    pool.wait_ge(soft_lin, seq * NB + j + 1)
                    nc.gpsimd.tensor_tensor(m_dBx[:, j, :], m_dBx[:, j, :], m_dA[:, j, :], ALU.mult)\
                        .then_inc(soft_low, 1)
                pool.wait_ge(soft_log, (seq + 1) * NB)
                pool.wait_ge(soft_low, (seq + 1) * NB)
                pool.sem_inc(passed, 1)
                nc.gpsimd.memset(m_dA[:, :, 0:1], 0.0).then_inc(dA_zero, 1)
                pool.wait_ge(dt_done, seq + 1)
                nc.gpsimd.tensor_tensor(dtx, m_dt[:, :, :], m_xs[:, :, :], ALU.mult).then_inc(dtx_done, 1)

            def inputs(seq, n):
                for q in range(2):
                    if q == 0:
                        pm.wait_read(pool, seq, "B", n)
                        if n == 0:
                            pool.wait_ge(dtx_done, seq + 1)
                    if n:
                        pool.wait_ge(scanned, (seq * N + n - 1) * 2 + q + 1)
                    part = slice(q * HALF, (q + 1) * HALF)
                    nc.gpsimd.tensor_tensor(m_dBx[:, part, :], dtx[:, part, :],
                                            m_B[:, n % 2, :].unsqueeze(1).to_broadcast([P, HALF, L]), ALU.mult)\
                        .then_inc(dBx_done, 1)

            def gate(seq):
                pool.wait_ge(summed, (seq + 1) * N * 2)
                for j in range(NB):
                    pm.wait_read(pool, seq, "res", j)
                nc.gpsimd.tensor_tensor(m_xs[:, :, :], m_xs[:, :, :], m_res[:, :, :], ALU.mult)\
                    .then_inc(y_done, 1)

            def turn(t, first, scan, second, more):
                if scan:
                    rstd(m, t - 1)
                    copy_x2(t - 1)
                if second:
                    rstd(f1, t - 2)
                if first:
                    bias_x(t)
                    rstd(f0, t)
                if scan:
                    softplus(t - 1)
                    for n in range(N):
                        inputs(t - 1, n)
                    gate(t - 1)

            turns(pool, turn)

        @block.vector
        def _(dve):
            for p in (pm, p0, p1):
                for s in p.freed:
                    dve.sem_inc(s, 1)
            dve.sem_inc(stored, 1)
            dve.wait_ge(loaded, LOADED)
            nc.vector.tensor_copy(pick32[:, :], pick32f[:, :]).then_inc(pick_set, 1)
            nc.vector.tensor_copy(picks, picks_f).then_inc(pick_set, 1)
            nc.vector.tensor_scalar(A[:, :, :], A[:, :, :], A_LOG_MAX, None, ALU.min).then_inc(A_done, 1)
            dve.wait_ge(A_done, 2)
            nc.vector.tensor_scalar(A[:, :, :], A[:, :, :], -1.0, None, ALU.mult).then_inc(A_done, 1)

            def statistics(n, seq):
                for i in range(NT):
                    nc.vector.bn_stats(n.stats[:, i, :], n.x[:, i, :]).then_inc(n.stat_done, 1)
                dve.wait_ge(n.stat_done, (seq + 1) * NT)
                dve.sem_inc(passed, 1)
                for i in range(NT):
                    nc.vector.bn_aggr(n.moments[:, i, :], n.stats[:, i, :]).then_inc(n.var_done, 1)

            def normalise(n, seq):
                dve.wait_ge(n.rstd_done, seq + 1)
                dve.wait_ge(n.var_done, (seq + 1) * NT)
                for i in range(NT):
                    nc.vector.tensor_scalar(n.xn[:, i, :], n.x[:, i, :], n.moments[:, i, 0:1], n.rstd[:, i:i + 1],
                                            ALU.subtract, ALU.mult).then_inc(n.xn_done, 1)

            def rank(r, p, seq, s):
                n = r.experts
                dve.wait_ge(p.ready, p.done(seq, "logits"))
                psum = p.psum("logits")[:, 0:NT * n].rearrange("p (i n) -> p i n", n=n)
                if r is r1:
                    nc.vector.tensor_tensor(r.logits[:, :, :], psum,
                                            gate_b[:, :].unsqueeze(1).to_broadcast([P, NT, n]), ALU.add)\
                        .then_inc(p.free("logits"), 1)
                else:
                    nc.vector.tensor_copy(r.logits[:, :, :], psum).then_inc(p.free("logits"), 1)
                p.wait_read(dve, seq, "logits")
                dve.sem_inc(passed, 1)
                for i in range(NT):
                    s.mark(nc.vector.max(r.top[:, i, :], r.logits[:, i, :]))
                s.wait()
                dve.sem_inc(passed, 1)
                for i in range(NT):
                    s.mark(nc.vector.max_index(r.index[:, i, :], r.top[:, i, :], r.logits[:, i, :]))
                s.mark(nc.vector.tensor_tensor(r.gap[:, :, 0:n], r.logits[:, :, :],
                                               r.top[:, :, 0:1].to_broadcast([P, NT, n]), ALU.subtract))
                nc.vector.tensor_tensor(r.gap[:, :, n:n + 1], r.top[:, :, 1:2], r.top[:, :, 0:1], ALU.subtract)\
                    .then_inc(r.gap_done, 1)
                s.wait()
                s.mark(nc.vector.tensor_copy(r.indexf[:, :, :], r.index[:, :, 0:2]))

            def weigh(r, seq, s):
                n = r.experts
                shape = [P, NT, n]
                second = r.exp[:, :, n:n + 1]
                dve.wait_ge(r.exp_done, seq + 1)
                if r is r0:
                    s.mark(nc.vector.tensor_reduce(r.total[:, :, :], r.exp[:, :, 0:n], AX.X, ALU.add))
                    s.wait()
                    s.mark(nc.vector.tensor_scalar(r.total[:, :, :], r.total[:, :, :], WEIGHT_EPS, 1.0,
                                                   ALU.mult, ALU.add))
                    s.wait()
                    s.mark(nc.vector.tensor_tensor(r.total[:, :, :], r.total[:, :, :], second, ALU.add))
                else:
                    s.mark(nc.vector.tensor_scalar(r.total[:, :, :], second, 1.0, None, ALU.add))
                s.wait()
                s.mark(nc.vector.reciprocal(r.weight[:, :, 0:1], r.total[:, :, :]))
                s.wait()
                s.mark(nc.vector.tensor_tensor(r.weight[:, :, 1:2], r.weight[:, :, 0:1], second, ALU.mult))
                for k, one in enumerate((r.one, r.two)):
                    s.mark(nc.vector.tensor_tensor(one[:, :, :], iota[:, 0:n].unsqueeze(1).to_broadcast(shape),
                                                   r.indexf[:, :, k:k + 1].to_broadcast(shape), ALU.is_equal))
                s.wait()
                for k, one in enumerate((r.one, r.two)):
                    s.mark(nc.vector.tensor_tensor(one[:, :, :], one[:, :, :],
                                                   r.weight[:, :, k:k + 1].to_broadcast(shape), ALU.mult))
                s.wait()
                copies = r.comb.shape[2]
                nc.vector.tensor_tensor(r.comb[:, :, :, :],
                                        r.one[:, :, :].unsqueeze(2).to_broadcast([P, NT, copies, n]),
                                        r.two[:, :, :].unsqueeze(2).to_broadcast([P, NT, copies, n]), ALU.add)\
                    .then_inc(r.comb_done, 1)

            def split_comb(seq, s):
                dve.wait_ge(comb_high, seq + 1)
                nc.vector.tensor_tensor(parts_rest, p0.psum("combT")[0:2 * E0, :], parts[0:2 * E0, :],
                                        ALU.subtract).then_inc(p0.free("combT"), 1)
                p0.wait_read(dve, seq, "combT")
                s.mark(nc.vector.tensor_copy(parts[0:2 * E0, :], parts_rest))
                s.wait()
                nc.vector.tensor_tensor(parts[0:E0, :], parts_rest[0:E0, :], parts[0:E0, :], ALU.subtract)\
                    .then_inc(comb_parts, 1)

            def add_o(seq):
                dve.wait_ge(x_biased, seq + 1)
                for i in range(NT):
                    dve.wait_ge(p0.ready, p0.done(seq, "o", i))
                    nc.vector.tensor_tensor(f0_x[:, i, :], p0.psum("o", i)[:, 0:E], f0_x[:, i, :], ALU.add)\
                        .then_inc(p0.free("o", i), 1)

            def hide(seq, j, s):
                p0.wait_read(dve, seq, "g", j)
                dve.wait_ge(p0.ready, p0.done(seq, "up", j))
                nc.vector.tensor_tensor(f0_h[:, j, :], f0_act[:, j % 2, :], p0.psum("up", j)[:, :], ALU.mult)\
                    .then_inc(p0.free("up", j), 1)
                if j < H0R:
                    p0.wait_read(dve, seq, "up", j)
                    dve.wait_ge(p0.ready, p0.done(seq, "comb", j))
                    nc.vector.tensor_tensor(f0_h[:, j, :], f0_h[:, j, :], p0.psum("comb", j)[:, :], ALU.mult)\
                        .then_inc(p0.free("comb", j), 1)

            def add_down(seq, i):
                dve.wait_ge(p0.ready, p0.done(seq, "down", i))
                nc.vector.tensor_tensor(f0_x[:, i, :], p0.psum("down", i)[:, 0:E], f0_x[:, i, :], ALU.add)\
                    .then_inc(p0.free("down", i), 1)

            def convolve(seq, s):
                for tap in range(TAPS - 1):
                    for j in range(NB):
                        if tap == 0:
                            dve.wait_ge(xc_copied, seq * NB + j + 1)
                            pm.wait_read(dve, seq, "xc", j)
                        else:
                            s.wait((tap - 1) * NB + j + 1)
                        step = nc.vector.scalar_tensor_tensor(m_xs[:, j, :], m_xc[:, j, tap:tap + L],
                                                              conv_w[:, j, tap:tap + 1], m_xs[:, j, :],
                                                              ALU.mult, ALU.add)
                        if tap < TAPS - 2:
                            s.mark(step)
                        else:
                            step.then_inc(conv_done, 1)

            def split(seq, s):
                dve.wait_ge(high_out, seq + 1)
                nc.vector.tensor_tensor(m_rest[:, :], pm.psum("bc")[0:64, :], m_bc[0:64, :], ALU.subtract)\
                    .then_inc(pm.free("bc"), 1)
                pm.wait_read(dve, seq, "bc")
                s.mark(nc.vector.tensor_copy(m_bc[0:64, :], m_rest[:, :]))
                s.wait()
                nc.vector.tensor_tensor(m_bc[0:32, :], m_rest[0:32, :], m_bc[0:32, :], ALU.subtract)\
                    .then_inc(parts_done, 1)

            def step_sizes(seq, s):
                dve.wait_ge(soft_log, (seq + 1) * NB)
                dve.wait_ge(soft_low, (seq + 1) * NB)
                s.mark(nc.vector.tensor_tensor(m_h[:, :, :], m_h[:, :, :], m_dBx[:, :, :], ALU.max))
                s.wait()
                nc.vector.tensor_tensor(m_dt[:, :, :], m_dt[:, :, :], m_h[:, :, :], ALU.add).then_inc(dt_done, 1)

            def scan_state(seq, n, between):
                at = (seq * N + n) * 2
                rows = [slice(q * HALF, (q + 1) * HALF) for q in range(2)]
                for q in range(2):
                    dve.wait_ge(dA_done, at + q + 1)
                    dve.wait_ge(dBx_done, at + q + 1)
                    if n:
                        dve.wait_ge(summed, at - 1 + q)
                    h, a, b = (v[:, rows[q], :].rearrange("p j t -> p (j t)") for v in (m_h, m_dA, m_dBx))
                    nc.vector.tensor_tensor_scan(h, a, b, 0.0, ALU.mult, ALU.add).then_inc(scanned, 1)
                    between(q)
                dve.wait_ge(pm.ready, pm.done(seq, "C", n))
                for q in range(2):
                    dve.wait_ge(scanned, at + q + 1)
                    state_c = pm.psum("C", n)[:, :].unsqueeze(1).to_broadcast([P, HALF, L])
                    nc.vector.tensor_tensor(m_h[:, rows[q], :], m_h[:, rows[q], :], state_c, ALU.mult)\
                        .then_inc(pm.free("C", n) if q else m_product, 1)
                    between(2 + q)
                if n == 0:
                    dve.wait_ge(y_begun, (seq + 1) * NB)
                for q in range(2):
                    if q:
                        pm.wait_read(dve, seq, "C", n)
                    else:
                        dve.wait_ge(m_product, seq * N + n + 1)
                    if n:
                        dve.wait_ge(summed, at - 1 + q)
                    nc.vector.tensor_tensor(m_xs[:, rows[q], :], m_xs[:, rows[q], :], m_h[:, rows[q], :], ALU.add)\
                        .then_inc(summed, 1)

            def add_scan(seq):
                dve.wait_ge(x2_copied, seq + 1)
                for i in range(NT):
                    dve.wait_ge(pm.ready, pm.done(seq, "out", i))
                    nc.vector.tensor_tensor(f1_x[:, i, :], pm.psum("out", i)[:, 0:E], m_x[:, i, :], ALU.add)\
                        .then_inc(pm.free("out", i), 1)

            def begin_acc(seq):
                dve.wait_ge(stored, 16 * seq + 1)
                for i in range(NT):
                    dve.wait_ge(p1.ready, p1.done(seq, "b2", i))
                    nc.vector.tensor_tensor(f1_acc[:, i, :], p1.psum("b2", i)[:, 0:E], f1_x[:, i, :], ALU.add)\
                        .then_inc(p1.free("b2", i), 1)

            def add_expert(seq, e, i):
                dve.wait_ge(p1.ready, p1.done(seq, "y", e, i))
                if e:
                    p1.wait_read(dve, seq, "y", e - 1, i)
                else:
                    p1.wait_read(dve, seq, "b2", i)
                nc.vector.scalar_tensor_tensor(f1_acc[:, i, :], p1.psum("y", e, i)[:, 0:E], r1.comb[:, i, 0, e:e + 1],
                                               f1_acc[:, i, :], ALU.mult, ALU.add)\
                    .then_inc(p1.free("y", e, i), 1)

            def turn(t, first, scan, second, more):
                s0 = Steps(dve, f0_step, STEPS_F0, t)
                sm = Steps(dve, m_step, STEPS_M, t - 1)
                s1 = Steps(dve, f1_step, STEPS_F1, t - 2)
                if scan:
                    for i in range(NT):
                        p0.wait_read(dve, t - 1, "down", i)
                    statistics(m, t - 1)
                if second:
                    for i in range(NT):
                        pm.wait_read(dve, t - 2, "out", i)
                    statistics(f1, t - 2)
                if scan:
                    normalise(m, t - 1)
                if second:
                    normalise(f1, t - 2)
                if first:
                    add_o(t)
                    for i in range(NT):
                        p0.wait_read(dve, t, "o", i)
                    statistics(f0, t)
                if scan:
                    convolve(t - 1, sm)
                if first:
                    normalise(f0, t)
                if second:
                    rank(r1, p1, t - 2, s1)
                if first:
                    rank(r0, p0, t, s0)
                if second:
                    weigh(r1, t - 2, s1)
                if first:
                    weigh(r0, t, s0)
                if scan:
                    split(t - 1, sm)
                if second:
                    begin_acc(t - 2)
                if first:
                    split_comb(t, s0)
                for j in range(H0):
                    if first:
                        hide(t, j, s0)
                    if j == 5 and scan:
                        step_sizes(t - 1, sm)
                for n in range(N):
                    def between(q):
                        if second and n % 2:
                            add_expert(t - 2, n // 2, q)
                        if first and q == 3 and n in DOWN_AT:
                            add_down(t, DOWN_AT.index(n))
                    if scan:
                        scan_state(t - 1, n, between)
                    else:
                        for q in range(NT):
                            between(q)
                if scan:
                    add_scan(t - 1)
                if first:
                    s0.close()
                if scan:
                    sm.close()
                if second:
                    s1.close()

            turns(dve, turn)

        @block.scalar
        def _(act):
            act.wait_ge(A_done, 1)
            nc.scalar.activation(A[:, :, :], A[:, :, :], ACT.Exp).then_inc(A_done, 1)
            act.wait_ge(A_done, 3)
            act.wait_ge(pad_set, 1)

            def copy_xT(n, p, seq):
                for k in range(KE):
                    act.wait_ge(p.ready, p.done(seq, "xT", k))
                    nc.scalar.copy(n.xT[:, k, :], p.psum("xT", k)[:, :]).then_inc(p.free("xT", k), 1)

            def copy_xc(seq, j):
                act.wait_ge(pm.ready, pm.done(seq, "xc", j))
                psum = pm.psum("xc", j)[:, :]
                nc.scalar.copy(m_xc[:, j, TAPS - 1:], psum).then_inc(xc_copied, 1)
                nc.scalar.activation(m_xs[:, j, :], psum, ACT.Identity, bias=conv_b[:, j:j + 1],
                                     scale=conv_w[:, j, TAPS - 1:TAPS]).then_inc(pm.free("xc", j), 1)

            def gate(seq, j):
                act.wait_ge(pm.ready, pm.done(seq, "res", j))
                nc.scalar.activation(m_res[:, j, :], pm.psum("res", j)[:, :], ACT.Silu)\
                    .then_inc(pm.free("res", j), 1)

            def activate_conv(seq, j):
                act.wait_ge(conv_done, seq * NB + j + 1)
                nc.scalar.activation(m_xs[:, j, :], m_xs[:, j, :], ACT.Silu).then_inc(xs_done, 1)

            def exp_gap(r, seq):
                act.wait_ge(r.gap_done, seq + 1)
                nc.scalar.activation(r.exp[:, :, :], r.gap[:, :, :], ACT.Exp).then_inc(r.exp_done, 1)

            def copy_comb1T(seq):
                act.wait_ge(p1.ready, p1.done(seq, "combT"))
                nc.scalar.copy(comb1T, p1.psum("combT")[0:E1, :]).then_inc(p1.free("combT"), 1)

            def round_comb0T(seq):
                act.wait_ge(p0.ready, p0.done(seq, "combT"))
                nc.scalar.copy(parts, p0.psum("combT")[0:3 * E0, :]).then_inc(comb_high, 1)

            def low_rank(seq):
                act.wait_ge(pm.ready, pm.done(seq, "dtr"))
                nc.scalar.copy(m_dtr[:, :], pm.psum("dtr")[0:RK, :]).then_inc(pm.free("dtr"), 1)
                act.wait_ge(pm.ready, pm.done(seq, "bc"))
                nc.scalar.copy(m_bc[:, :], pm.psum("bc")[0:96, :]).then_inc(high_out, 1)

            def softplus(seq):
                for j in range(NB):
                    act.wait_ge(pm.ready, pm.done(seq, "dt", j))
                    psum = pm.psum("dt", j)[:, :]
                    nc.scalar.activation(m_dA[:, j, :], psum, ACT.Abs, bias=dt_b[:, j:j + 1]).then_inc(soft_in, 1)
                    nc.scalar.activation(m_dt[:, j, :], psum, ACT.Relu, bias=dt_b[:, j:j + 1])\
                        .then_inc(pm.free("dt", j), 1)
                for j in range(NB):
                    act.wait_ge(soft_in, seq * NB + j + 1)
                    nc.scalar.activation(m_dA[:, j, :], m_dA[:, j, :], ACT.Exp, scale=-1.0).then_inc(soft_exp, 1)
                for j in range(NB):
                    act.wait_ge(soft_exp, seq * NB + j + 1)
                    nc.scalar.activation(m_h[:, j, :], m_dA[:, j, :], ACT.Ln, bias=1.0).then_inc(soft_log, 1)

            def begin_y(seq):
                act.wait_ge(dtx_done, seq + 1)
                for j in range(NB):
                    nc.scalar.activation(m_xs[:, j, :], m_xs[:, j, :], ACT.Identity, scale=D[:, j:j + 1])\
                        .then_inc(y_begun, 1)

            def copy_B(seq, n):
                act.wait_ge(pm.ready, pm.done(seq, "B", n))
                if n >= 2:
                    act.wait_ge(dBx_done, (seq * N + n - 1) * 2)
                nc.scalar.copy(m_B[:, n % 2, :], pm.psum("B", n)[:, :]).then_inc(pm.free("B", n), 1)

            def decays(seq, n, q):
                if n:
                    act.wait_ge(scanned, (seq * N + n - 1) * 2 + q + 1)
                elif q == 0:
                    act.wait_ge(dA_zero, seq + 1)
                    act.wait_ge(dt_done, seq + 1)
                for j in range(q * HALF, (q + 1) * HALF):
                    last = nc.scalar.activation(m_dA[:, j, 1:], m_dt[:, j, 1:], ACT.Exp, scale=A[:, j, n:n + 1])
                last.then_inc(dA_done, 1)

            def relu(seq, e, j):
                act.wait_ge(p1.ready, p1.done(seq, "z", e, j))
                if e >= 2 and j == 0:
                    act.wait_ge(p1.ready, p1.done(seq, "y", e - 2, NT - 1))
                nc.scalar.activation(f1_h[:, e % 2, j, :], p1.psum("z", e, j)[:, :], ACT.Relu, bias=b1[:, e, j:j + 1])\
                    .then_inc(p1.free("z", e, j), 1)

            def silu(seq, j):
                act.wait_ge(p0.ready, p0.done(seq, "g", j))
                if j >= 2:
                    p0.wait_read(act, seq, "up", j - 2)
                elif j == 0:
                    act.wait_ge(comb_parts, seq + 1)
                nc.scalar.activation(f0_act[:, j % 2, :], p0.psum("g", j)[:, :], ACT.Silu)\
                    .then_inc(p0.free("g", j), 1)

            def turn(t, first, scan, second, more):
                if scan:
                    copy_xT(m, pm, t - 1)
                if second:
                    copy_xT(f1, p1, t - 2)
                if scan:
                    for j in range(NB):
                        copy_xc(t - 1, j)
                if first:
                    copy_xT(f0, p0, t)
                if scan:
                    for j in range(NB):
                        gate(t - 1, j)
                    for j in range(NB):
                        activate_conv(t - 1, j)
                if second:
                    exp_gap(r1, t - 2)
                if first:
                    exp_gap(r0, t)
                if scan:
                    low_rank(t - 1)
                if second:
                    copy_comb1T(t - 2)
                if first:
                    round_comb0T(t)
                    for j in range(4):
                        silu(t, j)
                if scan:
                    softplus(t - 1)
                if first:
                    for j in range(4, H0):
                        silu(t, j)
                if scan:
                    begin_y(t - 1)
                    copy_B(t - 1, 0)
                    for q in range(2):
                        decays(t - 1, 0, q)
                for n in range(N):
                    if scan and n + 1 < N:
                        copy_B(t - 1, n + 1)
                        decays(t - 1, n + 1, 0)
                    if second and n % 2 == 0:
                        relu(t - 2, n // 2, 0)
                        relu(t - 2, n // 2, 1)
                    if scan and n + 1 < N:
                        decays(t - 1, n + 1, 1)
                    if second and n % 2 == 0:
                        relu(t - 2, n // 2, 2)
                        relu(t - 2, n // 2, 3)

            turns(act, turn)

        @block.tensor
        def _(pe):
            pe.wait_ge(loaded, LOADED)
            pe.wait_ge(pick_set, 2)

            def transpose_x(n, p, seq):
                pe.wait_ge(n.xn_done, (seq + 1) * NT)
                for k in range(KE):
                    pe.wait_ge(p.free("xT", k), p.before(seq, "xT", k))
                    for i in range(NT):
                        last = nc.tensor.transpose(p.psum("xT", k)[:, i * P:(i + 1) * P],
                                                   n.xn[:, i, k * P:(k + 1) * P], ident[:, :])
                    last.then_inc(p.ready, 1)

            def product(p, seq, key, out, pairs):
                pe.wait_ge(p.free(*key), p.before(seq, *key))
                for k, (weights, moving) in enumerate(pairs):
                    last = nc.tensor.matmul(out, weights, moving, start=(k == 0), stop=(k == len(pairs) - 1))
                last.then_inc(p.ready, 1)

            def logits(n, p, seq, weights, experts):
                for k in range(KE):
                    p.wait_read(pe, seq, "xT", k)
                pe.wait_ge(p.free("logits"), p.before(seq, "logits"))
                for i in range(NT):
                    for k in range(KE):
                        last = nc.tensor.matmul(p.psum("logits")[:, i * experts:(i + 1) * experts],
                                                n.xT[:, k, i * P:(i + 1) * P], weights[:, k, :],
                                                start=(k == 0), stop=(k == KE - 1))
                last.then_inc(p.ready, 1)

            def transpose_comb(r, p, seq):
                pe.wait_ge(r.comb_done, seq + 1)
                pe.wait_ge(p.free("combT"), p.before(seq, "combT"))
                for i in range(NT):
                    comb = r.comb[:, i, :, :].rearrange("p a n -> p (a n)")
                    last = nc.tensor.matmul(p.psum("combT")[0:comb.shape[1], i * P:(i + 1) * P], comb,
                                            ident[:, :], start=True, stop=True)
                last.then_inc(p.ready, 1)

            def outputs(seq):
                pe.wait_ge(gated_in, 16 * (seq + 1))
                for i in range(NT):
                    product(p0, seq, ("o", i), p0.psum("o", i)[:, 0:E],
                            [(f0_h[:, k, i * P:(i + 1) * P], o_w[:, k, :]) for k in range(NCG)])

            def gate_up(seq, j):
                for w, name in ((g_w, "g"), (up_w, "up")):
                    product(p0, seq, (name, j), p0.psum(name, j)[:, :],
                            [(w[:, k, j, :], f0.xT[:, k, :]) for k in range(KE)])
                if j < H0R:
                    if j == 0:
                        pe.wait_ge(comb_parts, seq + 1)
                    product(p0, seq, ("comb", j), p0.psum("comb", j)[:, :], [(picks[:, j, :], parts)])

            def down(seq, i):
                for key in (("comb", H0R - 1), ("up", H0 - 2), ("up", H0 - 1)):
                    p0.wait_read(pe, seq, *key)
                product(p0, seq, ("down", i), p0.psum("down", i)[:, 0:E],
                        [(f0_h[:, j, i * P:(i + 1) * P], down_w[:, j, :]) for j in range(H0)])

            def enter(seq, name, at):
                for j in range(NB):
                    product(pm, seq, (name, j), pm.psum(name, j)[:, :],
                            [(in_w[:, k, at + j, :], m.xT[:, k, :]) for k in range(KE)])

            def low_rank(seq):
                pe.wait_ge(xs_done, (seq + 1) * NB)
                product(pm, seq, ("dtr",), pm.psum("dtr")[0:RK, :],
                        [(x_w[:, j, 0:RK], m_xs[:, j, :]) for j in range(NB)])
                product(pm, seq, ("bc",), pm.psum("bc")[0:96, :],
                        [(x_w[:, j, RK:], m_xs[:, j, :]) for j in range(NB)])

            def step_sizes(seq):
                pm.wait_read(pe, seq, "dtr")
                for j in range(NB):
                    product(pm, seq, ("dt", j), pm.psum("dt", j)[:, :], [(dt_w[:, j, :], m_dtr[:, :])])

            def spread(seq, name, n):
                row = n if name == "B" else N + n
                product(pm, seq, (name, n), pm.psum(name, n)[:, :],
                        [(pick32[:, row:row + 1].to_broadcast([96, P]), m_bc[:, :])])

            def leave(seq):
                pe.wait_ge(y_done, seq + 1)
                for i in range(NT):
                    product(pm, seq, ("out", i), pm.psum("out", i)[:, 0:E],
                            [(m_xs[:, j, i * P:(i + 1) * P], y_w[:, j, :]) for j in range(NB)])

            def bias2(seq):
                p1.wait_read(pe, seq, "combT")
                for i in range(NT):
                    product(p1, seq, ("b2", i), p1.psum("b2", i)[:, 0:E],
                            [(comb1T[:, i * P:(i + 1) * P], b2[:, :])])

            def expert_up(seq, e):
                pe.wait_ge(w12_in[e % 2], (seq * (E1 // 2) + e // 2 + 1) * 16)
                for j in range(H1):
                    product(p1, seq, ("z", e, j), p1.psum("z", e, j)[:, :],
                            [(w1[e % 2][:, k, j * P:(j + 1) * P], f1.xT[:, k, :]) for k in range(KE)])

            def expert_down(seq, e):
                for j in range(H1):
                    p1.wait_read(pe, seq, "z", e, j)
                for i in range(NT):
                    product(p1, seq, ("y", e, i), p1.psum("y", e, i)[:, 0:E],
                            [(f1_h[:, e % 2, j, i * P:(i + 1) * P], w2[e % 2][:, j, :]) for j in range(H1)])

            def turn(t, first, scan, second, more):
                if scan:
                    transpose_x(m, pm, t - 1)
                if second:
                    transpose_x(f1, p1, t - 2)
                if first:
                    outputs(t)
                if scan:
                    for k in range(KE):
                        pm.wait_read(pe, t - 1, "xT", k)
                    enter(t - 1, "xc", 0)
                if second:
                    logits(f1, p1, t - 2, gate_w, E1)
                if first:
                    transpose_x(f0, p0, t)
                if scan:
                    enter(t - 1, "res", NB)
                if first:
                    logits(f0, p0, t, router_w, E0)
                if scan:
                    low_rank(t - 1)
                if second:
                    transpose_comb(r1, p1, t - 2)
                if first:
                    transpose_comb(r0, p0, t)
                if second:
                    bias2(t - 2)
                if first:
                    for j in range(4):
                        gate_up(t, j)
                if scan:
                    step_sizes(t - 1)
                if first:
                    for j in range(4, H0):
                        gate_up(t, j)
                if scan:
                    pe.wait_ge(parts_done, t)
                    spread(t - 1, "B", 0)
                    spread(t - 1, "C", 0)
                for n in range(N):
                    if scan and n + 1 < N:
                        spread(t - 1, "B", n + 1)
                    if second:
                        if n % 2 == 0:
                            expert_up(t - 2, n // 2)
                        else:
                            expert_down(t - 2, n // 2)
                    if first and n in DOWN_AT:
                        down(t, DOWN_AT.index(n))
                    if scan and n + 1 < N:
                        spread(t - 1, "C", n + 1)
                if scan:
                    leave(t - 1)

            turns(pe, turn)


DOWN_AT = [10, 11, 12, 13]
STEPS_F0, STEPS_M, STEPS_F1 = 20, 10, 17


def build(nc, a, out):
    pad = nc.dram_tensor("pad_coefficients", (D1, ROW), FP32, kind="Internal").ap()
    gated = nc.dram_tensor("gated", (NCG, P, B, L), FP32, kind="Internal").ap()
    position_coefficients(nc, a, pad)
    toeplitz_unit(nc, a, a["x_back"], pad, gated)
    mixtures_and_scan(nc, a, a["x"], gated, out)


def arrays_of(w):
    def f(name):
        return np.asarray(w[name])

    def rows(m):
        return np.ascontiguousarray(m.reshape(-1, P, m.shape[-1]).transpose(1, 0, 2))

    def columns(v):
        return np.ascontiguousarray(v.reshape(-1, P).T)

    def grouped(m):
        return np.ascontiguousarray(m.reshape(-1, P, m.shape[1] // P, P).transpose(2, 1, 0, 3))

    a = {
        "x": f("L0_attn_x"),
        "x_back": np.ascontiguousarray(f("L0_attn_x").reshape(B, NT, P, E)[:, :, ::-1]).reshape(B, L, E),
        "ident": np.eye(P, dtype=np.float32),
        "positions": columns(np.arange(L, dtype=np.float32)),
        "decay": np.power(np.float32(0.99), np.arange(L, dtype=np.float32)).astype(np.float32),
        "pos_w": f("L0_attn_pos_w")[0], "pos_b": f("L0_attn_pos_b"),
        "layer_w": np.stack([f(f"L0_attn_lw{i}") for i in range(3)], axis=1),
        "layer_b": np.stack([f(f"L0_attn_lb{i}") for i in range(3)]),
        "out_w": f("L0_attn_out_w"), "out_b": columns(f("L0_attn_out_b")),
        "u_w": grouped(f("L0_attn_u_w")), "u_b": columns(f("L0_attn_u_b")),
        "v_w": grouped(f("L0_attn_v_w")), "v_b": f("L0_attn_v_b").reshape(-1, P),
        "o_w": rows(f("L0_attn_o_w")), "o_b": f("L0_attn_o_b"),
    }
    def merged(routed, shared):
        both = np.concatenate([m.transpose(1, 0, 2).reshape(E, -1) for m in (routed, shared)], axis=1)
        return np.ascontiguousarray(rows(both).reshape(P, KE, H0, P))

    def down(routed, shared):
        return rows(np.concatenate([m.reshape(-1, E) for m in (routed, shared)], axis=0))

    x_w = f("L1_attn_W_x")
    first = f("L1_ffn_W1").reshape(E1, H1 * P, KE, P).transpose(0, 3, 2, 1).reshape(E1, P, -1)
    second = f("L1_ffn_W2").reshape(E1, E, H1, P).transpose(0, 3, 2, 1).reshape(E1, P, -1)
    a |= {
        "iota": np.arange(E0, dtype=np.float32),
        "picks": np.tile(np.repeat(np.eye(E0, dtype=np.float32), P // 2, axis=1).reshape(E0, H0R, P), (3, 1, 1)),
        "pick32": np.tile(np.eye(32, dtype=np.float32), (3, 1)),
        "router_w": rows(f("L0_ffn_router_w")),
        "g_w": merged(f("L0_ffn_wg_r"), f("L0_ffn_wg_s")),
        "up_w": merged(f("L0_ffn_wu_r"), f("L0_ffn_wu_s")),
        "down_w": down(f("L0_ffn_wd_r"), f("L0_ffn_wd_s")),
        "in_w": np.ascontiguousarray(rows(f("L1_attn_W_in")).reshape(P, KE, 2 * NB, P)),
        "conv_w": rows(f("L1_attn_conv_w")), "conv_b": columns(f("L1_attn_conv_b")),
        "x_w": rows(np.concatenate([x_w[:, :RK]] + [x_w[:, RK:]] * 3, axis=1)),
        "dt_w": np.ascontiguousarray(f("L1_attn_W_dt").reshape(RK, NB, P)), "dt_b": columns(f("L1_attn_b_dt")),
        "A_log": rows(f("L1_attn_A_log")), "D": columns(f("L1_attn_D")), "y_w": rows(f("L1_attn_W_out")),
        "gate_w": rows(np.ascontiguousarray(f("L1_ffn_Wg").T)), "gate_b": f("L1_ffn_bg"),
        "b1": np.ascontiguousarray(f("L1_ffn_b1").reshape(E1, H1, P).transpose(2, 0, 1)), "b2": f("L1_ffn_b2"),
        "w12": np.ascontiguousarray(np.concatenate([first, second], axis=2)),
    }
    return a


def kernel(**inputs):
    import concourse.bacc as bacc
    from concourse.bass_utils import run_bass_kernel_spmd

    nc = bacc.Bacc("TRN2", target_bir_lowering=False, num_devices=1)
    arrays, aps = {}, {}
    for name, array in arrays_of(inputs).items():
        arrays[f"in_{name}"] = array
        aps[name] = nc.dram_tensor(f"in_{name}", array.shape, mybir.dt.from_np(array.dtype), kind="ExternalInput").ap()
    out = nc.dram_tensor("out", (B, L, E), FP32, kind="ExternalOutput").ap()
    build(nc, aps, out)
    result = run_bass_kernel_spmd(nc, [arrays], core_ids=[0])
    return result.results[0]["out"]
```

```python
from contextlib import ExitStack

import numpy as np

import concourse.bass as bass
from concourse import mybir

FP32 = mybir.dt.float32
BF16 = mybir.dt.bfloat16
U32 = mybir.dt.uint32
ALU = mybir.AluOpType
ACT = mybir.ActivationFunctionType
AX = mybir.AxisListType

P = 128
B, L, E = 16, 512, 256
NT = L // P
KE = E // P
LN_EPS = 1e-5

R = 128
D1 = 768
NCG = D1 // P
SRMS_EPS = 1e-8
PAD = P - 1
ROW = PAD + L + 1
NJ = NT * B
CB = 8
NM = P // CB
CT = 4
RING_T = 4
RING_C = 2


def position_coefficients(nc, c, pad_dram):
    ctx = ExitStack()
    with ctx:
        def sb(name, shape, dt=FP32):
            return ctx.enter_context(nc.sbuf_tensor(name, shape, dt))

        def sem(name):
            return ctx.enter_context(nc.semaphore(name))

        ident = sb("p_ident", [P, P])
        positions = sb("p_positions", [P, NT])
        first_w = sb("p_first_w", [P, R])
        first_b = sb("p_first_b", [P, R])
        layer_w = sb("p_layer_w", [P, 3, R])
        layer_b = sb("p_layer_b", [P, 3, R])
        out_w = sb("p_out_w", [P, D1])
        out_b = sb("p_out_b", [P, NCG])
        decay = sb("p_decay", [P, L])
        h = sb("p_h", [P, NT, R])
        square = sb("p_square", [P, NT, R])
        norm = sb("p_norm", [P, NT])
        rms = sb("p_rms", [P, NT])
        inverse = sb("p_inverse", [P, NT])
        active = sb("p_active", [P, NT, R])
        activeT = sb("p_activeT", [P, L])
        raw = sb("p_raw", [P, NCG, L])
        padded = sb("p_padded", [P, NCG, ROW])
        pT = ctx.enter_context(nc.psum_tensor("p_pT", [P, L], FP32))
        pH = ctx.enter_context(nc.psum_tensor("p_pH", [P, NT, R], FP32))
        pC = [ctx.enter_context(nc.psum_tensor(f"p_pC{i}", [P, L], FP32)) for i in range(2)]

        loaded = sem("p_loaded")
        h_ready = sem("p_h_ready")
        squared = sem("p_squared")
        summed = sem("p_summed")
        rooted = sem("p_rooted")
        step = sem("p_step")
        active_ready = sem("p_active")
        turned = sem("p_turned")
        turned_out = sem("p_turned_out")
        layer_done = sem("p_layer_done")
        coef_done = sem("p_coef_done")
        coef_out = sem("p_coef_out")
        zeroed = sem("p_zeroed")
        decayed = sem("p_decayed")
        stored = sem("p_stored")

        block = ctx.enter_context(nc.Block())

        @block.sync
        def _(sp):
            for dst, src in ((ident[:, :], c["ident"]), (positions[:, :], c["positions"]),
                             (first_w[:, :], c["pos_w"].partition_broadcast(P)),
                             (first_b[:, :], c["pos_b"].partition_broadcast(P)),
                             (layer_w[:, :, :], c["layer_w"]),
                             (layer_b[:, :, :], c["layer_b"].partition_broadcast(P)),
                             (out_w[:, :], c["out_w"]), (out_b[:, :], c["out_b"]),
                             (decay[:, :], c["decay"].partition_broadcast(P))):
                sp.dma_start(dst, src).then_inc(loaded, 16)
            sp.wait_ge(decayed, NCG)
            sp.dma_start(pad_dram.rearrange("(g p) r -> p g r", p=P), padded[:, :, :]).then_inc(stored, 16)
            sp.wait_ge(stored, 16)

        @block.gpsimd
        def _(pool):
            nc.gpsimd.memset(padded[:, :, :], 0.0).then_inc(zeroed, 1)

        @block.vector
        def _(dve):
            steps = 0
            dve.wait_ge(loaded, 16 * 9)
            for i in range(NT):
                nc.vector.scalar_tensor_tensor(h[:, i, :], first_w[:, :], positions[:, i:i + 1], first_b[:, :],
                                               ALU.mult, ALU.add).then_inc(h_ready, 1)
            for layer in range(4):
                dve.wait_ge(h_ready, NT if layer == 0 else NT + layer)
                nc.vector.tensor_tensor(square[:, :, :], h[:, :, :], h[:, :, :], ALU.mult).then_inc(squared, 1)
                dve.wait_ge(squared, layer + 1)
                nc.vector.tensor_reduce(norm[:, :], square[:, :, :], AX.X, ALU.add).then_inc(summed, 1)
                dve.wait_ge(rooted, layer + 1)
                nc.vector.tensor_scalar(rms[:, :], rms[:, :], float(R) ** -0.5, SRMS_EPS, ALU.mult,
                                        ALU.add).then_inc(step, 1)
                steps += 1
                dve.wait_ge(step, steps)
                nc.vector.reciprocal(inverse[:, :], rms[:, :]).then_inc(step, 1)
                steps += 1
                dve.wait_ge(step, steps)
                for i in range(NT):
                    nc.vector.tensor_scalar(active[:, i, :], h[:, i, :], inverse[:, i:i + 1], 0.0, ALU.mult,
                                            ALU.max).then_inc(active_ready, 1)
                if layer < 3:
                    dve.wait_ge(layer_done, layer + 1)
                    dve.wait_ge(active_ready, NT * (layer + 1))
                    bias = layer_b[:, layer:layer + 1, :].to_broadcast([P, NT, R])
                    nc.vector.tensor_tensor(h[:, :, :], pH[:, :, :], bias, ALU.add).then_inc(h_ready, 1)
            dve.wait_ge(zeroed, 1)
            for g in range(NCG):
                dve.wait_ge(coef_out, g + 1)
                nc.vector.tensor_tensor(padded[:, g, PAD:PAD + L], raw[:, g, :], decay[:, :],
                                        ALU.mult).then_inc(decayed, 1)

        @block.scalar
        def _(act):
            for layer in range(4):
                act.wait_ge(summed, layer + 1)
                nc.scalar.activation(rms[:, :], norm[:, :], ACT.Sqrt).then_inc(rooted, 1)
                act.wait_ge(turned, layer + 1)
                nc.scalar.copy(activeT[:, :], pT[:, :]).then_inc(turned_out, 1)
            for g in range(NCG):
                act.wait_ge(coef_done, g + 1)
                nc.scalar.activation(raw[:, g, :], pC[g % 2][:, :], ACT.Identity,
                                     bias=out_b[:, g:g + 1]).then_inc(coef_out, 1)

        @block.tensor
        def _(pe):
            pe.wait_ge(loaded, 16 * 9)
            for layer in range(4):
                pe.wait_ge(active_ready, NT * (layer + 1))
                for i in range(NT):
                    last = nc.tensor.transpose(pT[:, i * P:(i + 1) * P], active[:, i, :], ident[:, :])
                last.then_inc(turned, 1)
                pe.wait_ge(turned_out, layer + 1)
                if layer < 3:
                    for i in range(NT):
                        last = nc.tensor.matmul(pH[:, i, :], activeT[:, i * P:(i + 1) * P], layer_w[:, layer, :],
                                                start=True, stop=True)
                    last.then_inc(layer_done, 1)
            for g in range(NCG):
                if g >= 2:
                    pe.wait_ge(coef_out, g - 1)
                nc.tensor.matmul(pC[g % 2][:, :], out_w[:, g * P:(g + 1) * P], activeT[:, :],
                                 start=True, stop=True).then_inc(coef_done, 1)


def toeplitz_unit(nc, c, x_dram, pad_dram, conv_dram, gated_dram):
    ctx = ExitStack()
    with ctx:
        def sb(name, shape, dt=FP32):
            return ctx.enter_context(nc.sbuf_tensor(name, shape, dt))

        def sem(name):
            return ctx.enter_context(nc.semaphore(name))

        ident = sb("t_ident", [P, P])
        half = sb("t_half", [P, NT])
        xnT = sb("t_xnT", [P, KE, B * L])
        V = [sb(f"t_V{r}", [P, P, NJ]) for r in range(2)]
        T = sb("t_T", [P, RING_T, CT, L])
        result = sb("t_result", [P, RING_C, CB // 2, P])
        x = sb("t_x", [P, 2, NT, E])
        xn = T[:, 0:2, 0:2, :].rearrange("p r a (b e) -> p r (a b) e", e=E)
        stats = sb("t_stats", [P, 2, NT, 6])
        moments = sb("t_moments", [P, 2, NT, 2])
        shifted = sb("t_shifted", [P, 2, NT])
        rstd = sb("t_rstd", [P, 2, NT])
        v_w = sb("t_v_w", [P, 2, KE, P])
        v_b = sb("t_v_b", [P, 2, P])
        v_sum = sb("t_v_sum", [P, 2, NT, P])
        u_w = sb("t_u_w", [P, 2, KE, P])
        u_b = sb("t_u_b", [P, 2])
        u_act = sb("t_u_act", [P, 2, NT, P])
        conv = sb("t_conv", [P, 2, NT, P])
        gated = sb("t_gated", [P, 2, NT, P])
        zero = sb("t_zero", [1, L], BF16)
        bank = [ctx.enter_context(nc.psum_tensor(f"t_bank{i}", [P, L], FP32)) for i in range(8)]
        v_bank, conv_bank, u_bank = bank[0:2], bank[2:6], bank[6:8]
        NV = len(conv_bank)

        const_in = sem("t_const_in")
        half_set = sem("t_half_set")
        zero_set = sem("t_zero_set")
        x_in = [sem(f"t_x_in{r}") for r in range(2)]
        stat_done = sem("t_stat")
        var_done = sem("t_var")
        eps_added = sem("t_eps")
        rstd_done = sem("t_rstd_done")
        xn_done = sem("t_xn_done")
        xnT_done = sem("t_xnT_done")
        xnT_out = sem("t_xnT_out")
        v_done = sem("t_v_done")
        v_biased = sem("t_v_biased")
        v_out = sem("t_v_out")
        T_used = sem("t_T_used")
        conv_out = sem("t_conv_out")
        stored = [sem(f"t_stored{r}") for r in range(RING_C)]
        u_done = sem("t_u_done")
        u_out = sem("t_u_out")
        gated_done = sem("t_gated_done")
        gated_stored = [sem(f"t_gated_stored{r}") for r in range(2)]
        u_in = [sem(f"t_u_in{r}") for r in range(2)]
        conv_in = [sem(f"t_conv_in{r}") for r in range(2)]
        w_in = [sem(f"t_w_in{r}") for r in range(2)]
        T_in = [sem(f"t_T_in{r}") for r in range(RING_T)]
        passed = sem("t_passed")

        block = ctx.enter_context(nc.Block())
        x_v = x_dram.rearrange("b (i p) e -> b p i e", p=P)
        LOADS = P // CT
        PER = CB // CT

        def groups(engine, group):
            group(0, 0, 1, False, True)
            with engine.Fori(0, NCG // 2 - 1) as pair:
                group(2 * pair + 1, 1, pair + 2, True, True)
                group(2 * pair + 2, 0, pair + 2, True, True)
            group(NCG - 1, 1, NCG // 2 + 1, True, False)

        @block.sync
        def _(sp):
            sp.dma_start(ident[:, :], c["ident"]).then_inc(const_in, 16)

            def load_weights(g, r):
                sp.dma_start(v_w[:, r, :, :], c["v_w"][bass.ds(g, 1), :, :, :].rearrange("o p k n -> p (o k) n"))\
                    .then_inc(w_in[r], 16)
                sp.dma_start(v_b[:, r, :], c["v_b"][bass.ds(g, 1), :].partition_broadcast(P)
                             .rearrange("p o n -> p (o n)")).then_inc(w_in[r], 16)

            def load_tiles(g, n):
                src = bass.AP(pad_dram.tensor, g * (P * ROW) + n * CT * ROW, [[1, P], [ROW, CT], [1, L]])
                sp.dma_start(T[:, n % RING_T, :, :], src).then_inc(T_in[n % RING_T], 16)

            def store(g, m):
                sp.dma_start(conv_dram[bass.ds(g, 1), m, :, :, :].rearrange("o q p t -> p (o q) t"),
                             result[:, m % RING_C, :, :]).then_inc(stored[m % RING_C], 16)

            def load_gate_weights(g, r):
                sp.dma_start(u_w[:, r, :, :], c["u_w"][bass.ds(g, 1), :, :, :].rearrange("o p k n -> p (o k) n"))\
                    .then_inc(u_in[r], 16)
                sp.dma_start(u_b[:, r:r + 1], c["u_b"][bass.ds(g, 1), :, :].rearrange("o p n -> p (o n)")).then_inc(u_in[r], 16)

            def load_conv(g, b):
                sp.wait_ge(gated_done, g * B + max(b - 1, 0) + 1)
                sp.sem_inc(passed, 1)
                src = bass.AP(conv_dram.tensor, g * (P * NJ * P) + b * P, [[NJ * P, P], [B * P, NT], [1, P]])
                sp.dma_start(conv[:, b % 2, :, :], src).then_inc(conv_in[b % 2], 16)

            def store_gated(g, b):
                sp.wait_ge(gated_done, g * B + b + 2)
                sp.sem_inc(passed, 1)
                sp.dma_start(gated_dram[bass.ds(g, 1), :, b, :].rearrange("o p t -> p (o t)"),
                             gated[:, b % 2, :, :].rearrange("p i t -> p (i t)")).then_inc(gated_stored[b % 2], 16)

            load_weights(0, 0)
            with sp.Fori(0, B // 2) as pair:
                for r in range(2):
                    sp.wait_ge(xn_done, 2 * NT * pair + 1)
                    sp.dma_start(x[:, r, :, :], x_v[bass.ds(2 * pair + r, 1), :, :, :].rearrange("o p i e -> p (o i) e"))\
                        .then_inc(x_in[r], 16)
            sp.wait_ge(xnT_done, B + 1)
            for n in range(RING_T):
                load_tiles(0, n)

            def gate(g, m):
                if m == 0:
                    for r in range(RING_C):
                        sp.wait_ge(stored[r], 16 * (g + 1) * (NM // RING_C) + 1)
                load_conv(g, m)
                if m:
                    store_gated(g, m - 1)

            def group(g, r, loads, before, after):
                if after:
                    sp.wait_ge(v_biased, B * g + 1)
                    sp.sem_inc(passed, 1)
                    load_weights(g + 1, 1 - r)
                sp.wait_ge(u_done, B * (g - 1) + 1 if before else 1)
                sp.sem_inc(passed, 1)
                load_gate_weights(g, r)
                for m in range(NM):
                    for n in range(PER * m, PER * (m + 1)):
                        ahead = n + RING_T
                        if ahead < LOADS or after:
                            sp.wait_ge(T_used, g * LOADS + n + 2)
                            sp.sem_inc(passed, 1)
                            load_tiles(g + ahead // LOADS, ahead % LOADS)
                    if before:
                        gate(g - 1, m)
                    sp.wait_ge(conv_out, g * NM + m + 2)
                    sp.sem_inc(passed, 1)
                    store(g, m)
                if before:
                    store_gated(g - 1, B - 1)

            groups(sp, group)
            for m in range(NM):
                gate(NCG - 1, m)
            store_gated(NCG - 1, B - 1)
            for r in range(2):
                sp.wait_ge(gated_stored[r], 16 * NCG * B // 2 + 1)

        @block.gpsimd
        def _(pool):
            nc.gpsimd.memset(half[:, :], -0.5).then_inc(half_set, 1)
            nc.gpsimd.memset(zero[:, :], 0.0).then_inc(zero_set, 1)
            pool.wait_ge(half_set, 1)
            with pool.Fori(0, B // 2) as pair:
                for r in range(2):
                    pool.wait_ge(var_done, (2 * pair + r + 1) * NT)
                    pool.sem_inc(passed, 1)
                    nc.gpsimd.tensor_scalar(shifted[:, r, :], moments[:, r, :, 1], LN_EPS, None,
                                            ALU.add).then_inc(eps_added, 1)
                    pool.wait_ge(eps_added, 2 * pair + r + 1)
                    nc.gpsimd.tensor_tensor(rstd[:, r, :], shifted[:, r, :], half[:, :], ALU.pow)\
                        .then_inc(rstd_done, 1)

        @block.vector
        def _(dve):
            for s in (xn_done, xnT_done, xnT_out, v_done, v_biased, v_out, T_used, conv_out, *stored,
                      u_done, u_out, gated_done, *gated_stored):
                dve.sem_inc(s, 1)
            with dve.Fori(0, B // 2) as pair:
                for r in range(2):
                    s = 2 * pair + r
                    dve.wait_ge(x_in[r], (pair + 1) * 16)
                    for i in range(NT):
                        nc.vector.bn_stats(stats[:, r, i, :], x[:, r, i, :]).then_inc(stat_done, 1)
                    dve.wait_ge(stat_done, (s + 1) * NT)
                    dve.sem_inc(passed, 1)
                    for i in range(NT):
                        nc.vector.bn_aggr(moments[:, r, i, :], stats[:, r, i, :]).then_inc(var_done, 1)
                    dve.wait_ge(rstd_done, s + 1)
                    dve.wait_ge(var_done, (s + 1) * NT)
                    dve.wait_ge(xnT_done, 2 * pair + 1)
                    for i in range(NT):
                        nc.vector.tensor_scalar(xn[:, r, i, :], x[:, r, i, :], moments[:, r, i, 0:1],
                                                rstd[:, r, i:i + 1], ALU.subtract, ALU.mult).then_inc(xn_done, 1)

            def add_bias(g, r, b):
                dve.wait_ge(v_done, g * B + b + 2)
                dve.wait_ge(v_out, g * B + max(b - 1, 0) + 1)
                psum = v_bank[b % 2][:, :].rearrange("p (i n) -> p i n", n=P)
                nc.vector.tensor_tensor(v_sum[:, b % 2, :, :], psum,
                                        v_b[:, r, :].unsqueeze(1).to_broadcast([P, NT, P]), ALU.add)\
                    .then_inc(v_biased, 1)

            dve.wait_ge(w_in[0], 32)
            for b in range(B):
                add_bias(0, 0, b)

            def gate(g, b):
                dve.wait_ge(u_out, g * B + b + 2)
                dve.wait_ge(conv_in[b % 2], 16 * (g * (B // 2) + b // 2 + 1))
                dve.wait_ge(gated_stored[b % 2], 16 * (g * (B // 2) + b // 2) + 1)
                nc.vector.tensor_tensor(gated[:, b % 2, :, :], u_act[:, b % 2, :, :], conv[:, b % 2, ::-1, :],
                                        ALU.mult).then_inc(gated_done, 1)

            def group(g, r, loads, before, after):
                if after:
                    dve.wait_ge(w_in[1 - r], 32 * loads)
                for b in range(B):
                    if after:
                        add_bias(g + 1, 1 - r, b)
                    if before:
                        gate(g - 1, b)

            groups(dve, group)
            for b in range(B):
                gate(NCG - 1, b)

        @block.scalar
        def _(act):
            with act.Fori(0, B // 2) as pair:
                for r in range(2):
                    act.wait_ge(xnT_done, 2 * pair + r + 2)
                    act.sem_inc(passed, 1)
                    for k in range(KE):
                        nc.scalar.copy(xnT[:, k, bass.ds((2 * pair + r) * L, L)],
                                       bank[2 * r + k][:, :]).then_inc(xnT_out, 1)

            def activate(g, r, b):
                act.wait_ge(v_biased, g * B + b + 2)
                dst = V[r][:, :, :].rearrange("p c (i b) -> p i c b", b=B)[:, ::-1, :, b]
                nc.scalar.activation(dst, v_sum[:, b % 2, :, :], ACT.Silu).then_inc(v_out, 1)

            for b in range(B):
                activate(0, 0, b)

            def gate(g, r, b):
                act.wait_ge(u_done, g * B + b + 2)
                act.wait_ge(gated_done, g * B + max(b - 1, 0) + 1)
                nc.scalar.activation(u_act[:, b % 2, :, ::-1], u_bank[b % 2][:, :].rearrange("p (i t) -> p i t", t=P),
                                     ACT.Silu, bias=u_b[:, r:r + 1]).then_inc(u_out, 1)

            def group(g, r, loads, before, after):
                if before:
                    act.wait_ge(u_in[1 - r], 32 * (loads - 1))
                if after:
                    act.wait_ge(T_used, g * LOADS + 1)
                for m in range(NM):
                    if after:
                        activate(g + 1, 1 - r, m)
                    act.wait_ge(T_used, g * LOADS + PER * (m + 1) + 1)
                    if m >= RING_C:
                        act.wait_ge(stored[m % RING_C], 16 * (g * (NM // RING_C) + m // RING_C) + 1)
                    else:
                        act.wait_ge(stored[m % RING_C], 16 * (g * (NM // RING_C)) + 1)
                    nc.scalar.copy(result[:, m % RING_C, :, :].rearrange("p q t -> p (q t)"),
                                   conv_bank[m % NV][:, :]).then_inc(conv_out, 1)
                    if before:
                        gate(g - 1, 1 - r, m)

            groups(act, group)
            act.wait_ge(u_in[1], 16 * NCG)
            for b in range(B):
                gate(NCG - 1, 1, b)

        @block.tensor
        def _(pe):
            pe.wait_ge(const_in, 16)
            with pe.Fori(0, B // 2) as pair:
                for r in range(2):
                    pe.wait_ge(xn_done, (2 * pair + r + 1) * NT + 1)
                    pe.wait_ge(xnT_out, 2 * KE * pair + 1)
                    for k in range(KE):
                        for i in range(NT):
                            last = nc.tensor.transpose(bank[2 * r + k][:, i * P:(i + 1) * P],
                                                       xn[:, r, i, k * P:(k + 1) * P], ident[:, :])
                    last.then_inc(xnT_done, 1)
            pe.wait_ge(xnT_out, KE * B + 1)

            def values(g, r, b):
                pe.wait_ge(v_biased, g * B + max(b - 1, 0) + 1)
                for i in range(NT):
                    for k in range(KE):
                        last = nc.tensor.matmul(v_bank[b % 2][:, i * P:(i + 1) * P],
                                                xnT[:, k, b * L + i * P:b * L + (i + 1) * P], v_w[:, r, k, :],
                                                start=(k == 0), stop=(k == KE - 1))
                last.then_inc(v_done, 1)

            pe.wait_ge(w_in[0], 32)
            for b in range(B):
                values(0, 0, b)

            pe.wait_ge(zero_set, 1)

            def convolve(g, r, n):
                pe.wait_ge(T_in[n % RING_T], (g * (LOADS // RING_T) + n // RING_T + 1) * 16)
                m = n // PER
                if n % PER == 0:
                    nc.tensor.matmul(conv_bank[m % NV][:, :], zero[:, 0:P], zero[:, :], start=True, stop=False)
                for q in range(CT):
                    chan = n * CT + q
                    side, at = chan % 2 * NJ, chan % CB // 2 * P
                    for lag in reversed(range(NT)):
                        last = nc.tensor.matmul(conv_bank[m % NV][side:side + NJ - lag * B, at:at + P],
                                                V[r][:, chan, lag * B:NJ], T[:, n % RING_T, q, lag * P:(lag + 1) * P],
                                                start=False, stop=(lag == 0 and chan % CB >= CB - 2))
                last.then_inc(T_used, 1)

            def gate(g, r, b):
                pe.wait_ge(u_out, g * B + max(b - 1, 0) + 1)
                for k in range(KE):
                    last = nc.tensor.matmul(u_bank[b % 2][:, :], u_w[:, r, k, :], xnT[:, k, b * L:(b + 1) * L],
                                            start=(k == 0), stop=(k == KE - 1))
                last.then_inc(u_done, 1)

            def group(g, r, loads, before, after):
                pe.wait_ge(v_out, (g + 1) * B + 1)
                if after:
                    pe.wait_ge(w_in[1 - r], 32 * loads)
                if before:
                    pe.wait_ge(u_in[1 - r], 32 * (loads - 1))
                for m in range(NM):
                    pe.wait_ge(conv_out, g * NM + max(m - NV + 1, 0) + 1)
                    for n in range(PER * m, PER * (m + 1)):
                        convolve(g, r, n)
                    if after:
                        values(g + 1, 1 - r, m)
                    if before:
                        gate(g - 1, 1 - r, m)

            groups(pe, group)
            pe.wait_ge(u_in[1], 16 * NCG)
            for b in range(B):
                gate(NCG - 1, 1, b)


E0 = 16
H0 = 10
H0R = 8
DI = 512
NB = DI // P
N = 16
RK = 64
TAPS = 4
E1 = 8
H1 = 4
WEIGHT_EPS = 1e-9
A_LOG_MAX = 83.0
HALF = NB // 2


class Products:

    def __init__(self, sem, name, banks, order):
        self.ready = sem(f"{name}_ready")
        self.freed = [sem(f"{name}_freed{i}") for i in range(len(banks))]
        self.banks, self.total, uses = banks, len(order), [0] * len(banks)
        self.place = {}
        for i, key in enumerate(order):
            bank = i % len(banks)
            self.place[key] = (i, bank, uses[bank])
            uses[bank] += 1
        self.uses = uses

    def psum(self, *key):
        return self.banks[self.place[key][1]]

    def free(self, *key):
        return self.freed[self.place[key][1]]

    def before(self, seq, *key):
        _, bank, nth = self.place[key]
        return seq * self.uses[bank] + nth + 1

    def wait_read(self, engine, seq, *key):
        engine.wait_ge(self.free(*key), self.before(seq, *key) + 1)

    def done(self, seq, *key):
        return seq * self.total + self.place[key][0] + 1


class Steps:

    def __init__(self, engine, sem, per_seq, seq):
        self.engine, self.sem, self.per_seq, self.seq, self.n = engine, sem, per_seq, seq, 0

    def mark(self, instruction):
        instruction.then_inc(self.sem, 1)
        self.n += 1
        return self.n

    def wait(self, n=None):
        self.engine.wait_ge(self.sem, self.seq * self.per_seq + (self.n if n is None else n))

    def close(self):
        assert self.n == self.per_seq, (self.sem, self.n)


def mixtures_and_scan(nc, c, x_dram, gated_dram, out_dram):
    ctx = ExitStack()
    with ctx:
        def sb(name, shape, dt=FP32):
            return ctx.enter_context(nc.sbuf_tensor(name, shape, dt))

        def sem(name):
            return ctx.enter_context(nc.semaphore(name))

        ident = sb("ident", [P, P])
        half = sb("half", [P, NT])
        iota = sb("iota", [P, E0])
        pick32f = sb("pick32f", [96, 32])
        pick32 = sb("pick32", [96, 32], BF16)
        o_w = sb("o_w", [P, NCG, E])
        o_b = sb("o_b", [P, E])
        router_w = sb("router_w", [P, KE, E0])
        g_w = sb("g_w", [P, KE, H0, P])
        up_w = sb("up_w", [P, KE, H0, P])
        down_w = sb("down_w", [P, H0, E])
        in_w = sb("in_w", [P, KE, 2 * NB, P])
        conv_w = sb("conv_w", [P, NB, TAPS])
        conv_b = sb("conv_b", [P, NB])
        x_w = sb("x_w", [P, NB, RK + 96])
        shared = sb("shared", [P, L])
        dt_w = shared[0:RK, :].rearrange("p (j n) -> p j n", n=P)
        picks = shared[64:64 + 3 * E0, :].bitcast(BF16).rearrange("p (j n) -> p j n", n=P)
        dt_b = sb("dt_b", [P, NB])
        A = sb("A", [P, NB, N])
        D = sb("D", [P, NB])
        y_w = sb("y_w", [P, NB, E])
        gate_w = sb("gate_w", [P, KE, E1])
        gate_b = sb("gate_b", [P, E1])
        b1 = sb("b1", [P, E1, H1])
        b2 = sb("b2", [E1, E])
        w12 = sb("w12", [P, 2, KE * H1 * P + H1 * E])

        def norm_buffers(name, x, xn):
            class Norm:
                pass
            n = Norm()
            n.x, n.xn = x, xn
            n.stats = sb(f"{name}_stats", [P, NT, 6])
            n.moments = sb(f"{name}_moments", [P, NT, 2])
            n.shifted = sb(f"{name}_shifted", [P, NT])
            n.rstd = sb(f"{name}_rstd", [P, NT])
            n.xT = sb(f"{name}_xT", [P, KE, L])
            n.stat_done = sem(f"{name}_stat")
            n.var_done = sem(f"{name}_var")
            n.eps_added = sem(f"{name}_eps")
            n.rstd_done = sem(f"{name}_rstd_done")
            n.xn_done = sem(f"{name}_xn")
            return n

        def route_buffers(name, experts, copies):
            class Route:
                pass
            r = Route()
            r.experts = experts
            r.logits = sb(f"{name}_logits", [P, NT, experts])
            r.top = sb(f"{name}_top", [P, NT, 8])
            r.index = sb(f"{name}_index", [P, NT, 8], U32)
            r.indexf = sb(f"{name}_indexf", [P, NT, 2])
            r.gap = sb(f"{name}_gap", [P, NT, experts + 1])
            r.exp = r.gap
            r.total = sb(f"{name}_total", [P, NT, 1])
            r.weight = sb(f"{name}_weight", [P, NT, 2])
            r.one = sb(f"{name}_one", [P, NT, experts])
            r.two = sb(f"{name}_two", [P, NT, experts])
            r.comb = sb(f"{name}_comb", [P, NT, copies, experts])
            r.gap_done = sem(f"{name}_gap_done")
            r.exp_done = sem(f"{name}_exp_done")
            r.comb_done = sem(f"{name}_comb_done")
            return r

        f0_x = sb("f0_x", [P, NT, E])
        f0_h = sb("f0_h", [P, H0, L])
        f0_act = sb("f0_act", [P, 2, L])
        f0 = norm_buffers("f0", f0_x, f0_act[:, :, :].rearrange("p a (b e) -> p (a b) e", e=E))
        combT = sb("combT", [P, L])
        comb1T = combT[0:E1, :]
        parts = combT[64:64 + 3 * E0, 0:L // 2].bitcast(BF16)
        parts_rest = f0_act[64:64 + 2 * E0, 0, :]
        r0 = route_buffers("r0", E0, 3)
        m_x = sb("m_x", [P, NT, E])
        m_xc = sb("m_xc", [P, NB, TAPS - 1 + L])
        m_xs = sb("m_xs", [P, NB, L])
        m_res = sb("m_res", [P, NB, L])
        m_bc = sb("m_bc", [96, L], BF16)
        m_dt = sb("m_dt", [P, NB, L])
        m_dA = sb("m_dA", [P, NB, L])
        picks_f = m_dA[64:64 + 3 * E0, 0:2, :].rearrange("p a (b n) -> p (a b) n", n=P)
        m_dBx = sb("m_dBx", [P, NB, L])
        m_h = sb("m_h", [P, NB, L])
        m_B = sb("m_B", [P, 2, L])
        m_rest = m_B[0:64, 0, :]
        m_dtr = m_B[0:RK, 1, :]
        m_xn = m_h[:, 0:2, :].rearrange("p a (b e) -> p (a b) e", e=E)
        m = norm_buffers("m", f0_x, m_xn)
        f1_x = sb("f1_x", [P, NT, E])
        f1_h = sb("f1_h", [P, 2, H1, L])
        f1_acc = sb("f1_acc", [P, NT, E])
        f1_xn = f1_h[:, 1, 0:2, :].rearrange("p a (b e) -> p (a b) e", e=E)
        f1 = norm_buffers("f1", f1_x, f1_xn)
        r1 = route_buffers("r1", E1, 1)

        bank = [ctx.enter_context(nc.psum_tensor(f"bank{i}", [P, L], FP32)) for i in range(8)]
        pm = Products(sem, "pm", bank[0:2],
                      [("xT", k) for k in range(KE)] + [("xc", j) for j in range(NB)] + [("res", j) for j in range(NB)]
                      + [("dtr",), ("bc",)] + [("dt", j) for j in range(NB)]
                      + [(w, n) for n in range(N) for w in ("B", "C")] + [("out", i) for i in range(NT)])
        p0 = Products(sem, "p0", bank[2:5],
                      [("o", i) for i in range(NT)] + [("xT", k) for k in range(KE)] + [("logits",), ("combT",)]
                      + [(w, j) for j in range(H0) for w in ("g", "up", "comb") if j < H0R or w != "comb"]
                      + [("down", i) for i in range(NT)])
        p1 = Products(sem, "p1", bank[5:8],
                      [("xT", k) for k in range(KE)] + [("logits",), ("combT",)] + [("b2", i) for i in range(NT)]
                      + [(w, e, j) for e in range(E1) for w in ("z", "y") for j in range(4)])

        loaded = sem("loaded")
        half_set = sem("half_set")
        pick_set = sem("pick_set")
        pad_set = sem("pad_set")
        A_done = sem("A_done")
        passed = sem("passed")
        x_in = sem("x_in")
        gated_in = sem("gated_in")
        x_biased = sem("x_biased")
        x2_copied = sem("x2_copied")
        comb_high = sem("comb_high")
        comb_parts = sem("comb_parts")
        f0_step = sem("f0_step")
        m_step = sem("m_step")
        f1_step = sem("f1_step")
        conv_done = sem("conv_done")
        xs_done = sem("xs_done")
        high_out = sem("high_out")
        parts_done = sem("parts_done")
        soft_in = sem("soft_in")
        soft_exp = sem("soft_exp")
        soft_log = sem("soft_log")
        soft_lin = sem("soft_lin")
        soft_low = sem("soft_low")
        dt_done = sem("dt_done")
        dA_zero = sem("dA_zero")
        dtx_done = sem("dtx_done")
        y_begun = sem("y_begun")
        dA_done = sem("dA_done")
        dBx_done = sem("dBx_done")
        scanned = sem("scanned")
        m_product = sem("m_product")
        xc_copied = sem("xc_copied")
        summed = sem("summed")
        y_done = sem("y_done")
        w12_in = [sem(f"w12_in{r}") for r in range(2)]
        stored = sem("stored")

        block = ctx.enter_context(nc.Block())

        consts = [(ident[:, :], c["ident"]), (iota[:, :], c["iota"].partition_broadcast(P)),
                  (picks_f, c["picks"]), (pick32f[:, :], c["pick32"]),
                  (o_w[:, :, :], c["o_w"]), (o_b[:, :], c["o_b"].partition_broadcast(P)),
                  (router_w[:, :, :], c["router_w"]), (g_w[:, :, :, :], c["g_w"]), (up_w[:, :, :, :], c["up_w"]),
                  (down_w[:, :, :], c["down_w"]), (in_w[:, :, :, :], c["in_w"]), (conv_w[:, :, :], c["conv_w"]),
                  (conv_b[:, :], c["conv_b"]), (x_w[:, :, :], c["x_w"]), (dt_w, c["dt_w"]),
                  (dt_b[:, :], c["dt_b"]), (A[:, :, :], c["A_log"]), (D[:, :], c["D"]), (y_w[:, :, :], c["y_w"]),
                  (gate_w[:, :, :], c["gate_w"]), (gate_b[:, :], c["gate_b"].partition_broadcast(P)),
                  (b1[:, :, :], c["b1"]), (b2[:, :], c["b2"])]
        LOADED = 16 * len(consts)
        W1 = KE * H1 * P
        w1 = [w12[:, r, 0:W1].rearrange("p (k n) -> p k n", k=KE) for r in range(2)]
        w2 = [w12[:, r, W1:].rearrange("p (j n) -> p j n", j=H1) for r in range(2)]
        dtx = m_xc[:, :, TAPS - 1:]

        def turns(engine, turn):
            turn(0, True, False, False, True)
            turn(1, True, True, False, True)
            with engine.Fori(2, B - 1) as t:
                turn(t, True, True, True, True)
            turn(B - 1, True, True, True, False)
            turn(B, False, True, True, False)
            turn(B + 1, False, False, True, False)

        @block.sync
        def _(sp):
            for dst, src in consts:
                sp.dma_start(dst, src).then_inc(loaded, 16)

            def load_x(seq):
                sp.sem_inc(passed, 1)
                sp.dma_start(f0_x[:, :, :], x_dram[bass.ds(seq, 1), :, :].rearrange("o (i p) e -> p (o i) e", p=P))\
                    .then_inc(x_in, 16)

            def load_gated(seq):
                sp.sem_inc(passed, 1)
                sp.dma_start(f0_h[:, 0:NCG, :], gated_dram[:, :, bass.ds(seq, 1), :].rearrange("g p o t -> p g (o t)"))\
                    .then_inc(gated_in, 16)

            def load_expert(e):
                sp.dma_start(w12[:, e % 2, :], c["w12"][e]).then_inc(w12_in[e % 2], 16)

            load_gated(0)
            for e in range(2):
                load_expert(e)

            def turn(t, first, scan, second, more):
                if first:
                    if scan:
                        sp.wait_ge(m.xn_done, NT * t)
                        sp.wait_ge(x2_copied, t)
                    load_x(t)
                if second:
                    for e in range(2, E1 + 2):
                        if e == E1 + 1 and more:
                            sp.wait_ge(p0.ready, p0.done(t, "down", NT - 1))
                            load_gated(t + 1)
                        if e < E1 or first or scan:
                            sp.wait_ge(p1.ready, p1.done(t - 2, "y", e - 2, NT - 1))
                            load_expert(e % E1)
                    for i in range(1, NT):
                        p1.wait_read(sp, t - 2, "y", E1 - 1, i)
                        sp.sem_inc(passed, 1)
                    sp.dma_start(out_dram[bass.ds(t - 2, 1), :, :].rearrange("o (i p) e -> p (o i) e", p=P),
                                 f1_acc[:, :, :]).then_inc(stored, 16)
                elif more:
                    sp.wait_ge(p0.ready, p0.done(t, "down", NT - 1))
                    load_gated(t + 1)

            turns(sp, turn)
            sp.wait_ge(stored, 16 * B + 1)

        @block.gpsimd
        def _(pool):
            nc.gpsimd.memset(half[:, :], -0.5).then_inc(half_set, 1)
            nc.gpsimd.memset(m_xc[:, :, 0:TAPS - 1], 0.0).then_inc(pad_set, 1)
            pool.wait_ge(half_set, 1)
            pool.wait_ge(loaded, LOADED)

            def rstd(n, seq):
                pool.wait_ge(n.var_done, (seq + 1) * NT)
                pool.sem_inc(passed, 1)
                nc.gpsimd.tensor_scalar(n.shifted[:, :], n.moments[:, :, 1], LN_EPS, None, ALU.add)\
                    .then_inc(n.eps_added, 1)
                pool.wait_ge(n.eps_added, seq + 1)
                nc.gpsimd.tensor_tensor(n.rstd[:, :], n.shifted[:, :], half[:, :], ALU.pow)\
                    .then_inc(n.rstd_done, 1)

            def bias_x(seq):
                pool.wait_ge(x_in, 16 * (seq + 1))
                nc.gpsimd.tensor_tensor(f0_x[:, :, :], f0_x[:, :, :],
                                        o_b[:, :].unsqueeze(1).to_broadcast([P, NT, E]), ALU.add)\
                    .then_inc(x_biased, 1)

            def copy_x2(seq):
                for i in range(NT):
                    p0.wait_read(pool, seq, "down", i)
                pool.sem_inc(passed, 1)
                nc.gpsimd.tensor_copy(m_x[:, :, :], f0_x[:, :, :]).then_inc(x2_copied, 1)

            def softplus(seq):
                for j in range(NB):
                    pool.wait_ge(soft_exp, seq * NB + j + 1)
                    pool.sem_inc(passed, 1)
                    nc.gpsimd.tensor_scalar(m_dBx[:, j, :], m_dA[:, j, :], -0.5, 1.0, ALU.mult, ALU.add)\
                        .then_inc(soft_lin, 1)
                    pool.wait_ge(soft_lin, seq * NB + j + 1)
                    nc.gpsimd.tensor_tensor(m_dBx[:, j, :], m_dBx[:, j, :], m_dA[:, j, :], ALU.mult)\
                        .then_inc(soft_low, 1)
                pool.wait_ge(soft_log, (seq + 1) * NB)
                pool.wait_ge(soft_low, (seq + 1) * NB)
                pool.sem_inc(passed, 1)
                nc.gpsimd.memset(m_dA[:, :, 0:1], 0.0).then_inc(dA_zero, 1)
                pool.wait_ge(dt_done, seq + 1)
                nc.gpsimd.tensor_tensor(dtx, m_dt[:, :, :], m_xs[:, :, :], ALU.mult).then_inc(dtx_done, 1)

            def inputs(seq, n):
                for q in range(2):
                    if q == 0:
                        pm.wait_read(pool, seq, "B", n)
                        if n == 0:
                            pool.wait_ge(dtx_done, seq + 1)
                    if n:
                        pool.wait_ge(scanned, (seq * N + n - 1) * 2 + q + 1)
                    part = slice(q * HALF, (q + 1) * HALF)
                    nc.gpsimd.tensor_tensor(m_dBx[:, part, :], dtx[:, part, :],
                                            m_B[:, n % 2, :].unsqueeze(1).to_broadcast([P, HALF, L]), ALU.mult)\
                        .then_inc(dBx_done, 1)

            def gate(seq):
                pool.wait_ge(summed, (seq + 1) * N * 2)
                for j in range(NB):
                    pm.wait_read(pool, seq, "res", j)
                nc.gpsimd.tensor_tensor(m_xs[:, :, :], m_xs[:, :, :], m_res[:, :, :], ALU.mult)\
                    .then_inc(y_done, 1)

            def turn(t, first, scan, second, more):
                if scan:
                    rstd(m, t - 1)
                    copy_x2(t - 1)
                if second:
                    rstd(f1, t - 2)
                if first:
                    bias_x(t)
                    rstd(f0, t)
                if scan:
                    softplus(t - 1)
                    for n in range(N):
                        inputs(t - 1, n)
                    gate(t - 1)

            turns(pool, turn)

        @block.vector
        def _(dve):
            for p in (pm, p0, p1):
                for s in p.freed:
                    dve.sem_inc(s, 1)
            dve.sem_inc(stored, 1)
            dve.wait_ge(loaded, LOADED)
            nc.vector.tensor_copy(pick32[:, :], pick32f[:, :]).then_inc(pick_set, 1)
            nc.vector.tensor_copy(picks, picks_f).then_inc(pick_set, 1)
            nc.vector.tensor_scalar(A[:, :, :], A[:, :, :], A_LOG_MAX, None, ALU.min).then_inc(A_done, 1)
            dve.wait_ge(A_done, 2)
            nc.vector.tensor_scalar(A[:, :, :], A[:, :, :], -1.0, None, ALU.mult).then_inc(A_done, 1)

            def statistics(n, seq):
                for i in range(NT):
                    nc.vector.bn_stats(n.stats[:, i, :], n.x[:, i, :]).then_inc(n.stat_done, 1)
                dve.wait_ge(n.stat_done, (seq + 1) * NT)
                dve.sem_inc(passed, 1)
                for i in range(NT):
                    nc.vector.bn_aggr(n.moments[:, i, :], n.stats[:, i, :]).then_inc(n.var_done, 1)

            def normalise(n, seq):
                dve.wait_ge(n.rstd_done, seq + 1)
                dve.wait_ge(n.var_done, (seq + 1) * NT)
                for i in range(NT):
                    nc.vector.tensor_scalar(n.xn[:, i, :], n.x[:, i, :], n.moments[:, i, 0:1], n.rstd[:, i:i + 1],
                                            ALU.subtract, ALU.mult).then_inc(n.xn_done, 1)

            def rank(r, p, seq, s):
                n = r.experts
                dve.wait_ge(p.ready, p.done(seq, "logits"))
                psum = p.psum("logits")[:, 0:NT * n].rearrange("p (i n) -> p i n", n=n)
                if r is r1:
                    nc.vector.tensor_tensor(r.logits[:, :, :], psum,
                                            gate_b[:, :].unsqueeze(1).to_broadcast([P, NT, n]), ALU.add)\
                        .then_inc(p.free("logits"), 1)
                else:
                    nc.vector.tensor_copy(r.logits[:, :, :], psum).then_inc(p.free("logits"), 1)
                p.wait_read(dve, seq, "logits")
                dve.sem_inc(passed, 1)
                for i in range(NT):
                    s.mark(nc.vector.max(r.top[:, i, :], r.logits[:, i, :]))
                s.wait()
                dve.sem_inc(passed, 1)
                for i in range(NT):
                    s.mark(nc.vector.max_index(r.index[:, i, :], r.top[:, i, :], r.logits[:, i, :]))
                s.mark(nc.vector.tensor_tensor(r.gap[:, :, 0:n], r.logits[:, :, :],
                                               r.top[:, :, 0:1].to_broadcast([P, NT, n]), ALU.subtract))
                nc.vector.tensor_tensor(r.gap[:, :, n:n + 1], r.top[:, :, 1:2], r.top[:, :, 0:1], ALU.subtract)\
                    .then_inc(r.gap_done, 1)
                s.wait()
                s.mark(nc.vector.tensor_copy(r.indexf[:, :, :], r.index[:, :, 0:2]))

            def weigh(r, seq, s):
                n = r.experts
                shape = [P, NT, n]
                second = r.exp[:, :, n:n + 1]
                dve.wait_ge(r.exp_done, seq + 1)
                if r is r0:
                    s.mark(nc.vector.tensor_reduce(r.total[:, :, :], r.exp[:, :, 0:n], AX.X, ALU.add))
                    s.wait()
                    s.mark(nc.vector.tensor_scalar(r.total[:, :, :], r.total[:, :, :], WEIGHT_EPS, 1.0,
                                                   ALU.mult, ALU.add))
                    s.wait()
                    s.mark(nc.vector.tensor_tensor(r.total[:, :, :], r.total[:, :, :], second, ALU.add))
                else:
                    s.mark(nc.vector.tensor_scalar(r.total[:, :, :], second, 1.0, None, ALU.add))
                s.wait()
                s.mark(nc.vector.reciprocal(r.weight[:, :, 0:1], r.total[:, :, :]))
                s.wait()
                s.mark(nc.vector.tensor_tensor(r.weight[:, :, 1:2], r.weight[:, :, 0:1], second, ALU.mult))
                for k, one in enumerate((r.one, r.two)):
                    s.mark(nc.vector.tensor_tensor(one[:, :, :], iota[:, 0:n].unsqueeze(1).to_broadcast(shape),
                                                   r.indexf[:, :, k:k + 1].to_broadcast(shape), ALU.is_equal))
                s.wait()
                for k, one in enumerate((r.one, r.two)):
                    s.mark(nc.vector.tensor_tensor(one[:, :, :], one[:, :, :],
                                                   r.weight[:, :, k:k + 1].to_broadcast(shape), ALU.mult))
                s.wait()
                copies = r.comb.shape[2]
                nc.vector.tensor_tensor(r.comb[:, :, :, :],
                                        r.one[:, :, :].unsqueeze(2).to_broadcast([P, NT, copies, n]),
                                        r.two[:, :, :].unsqueeze(2).to_broadcast([P, NT, copies, n]), ALU.add)\
                    .then_inc(r.comb_done, 1)

            def split_comb(seq, s):
                dve.wait_ge(comb_high, seq + 1)
                nc.vector.tensor_tensor(parts_rest, p0.psum("combT")[0:2 * E0, :], parts[0:2 * E0, :],
                                        ALU.subtract).then_inc(p0.free("combT"), 1)
                p0.wait_read(dve, seq, "combT")
                s.mark(nc.vector.tensor_copy(parts[0:2 * E0, :], parts_rest))
                s.wait()
                nc.vector.tensor_tensor(parts[0:E0, :], parts_rest[0:E0, :], parts[0:E0, :], ALU.subtract)\
                    .then_inc(comb_parts, 1)

            def add_o(seq):
                dve.wait_ge(x_biased, seq + 1)
                for i in range(NT):
                    dve.wait_ge(p0.ready, p0.done(seq, "o", i))
                    nc.vector.tensor_tensor(f0_x[:, i, :], p0.psum("o", i)[:, 0:E], f0_x[:, i, :], ALU.add)\
                        .then_inc(p0.free("o", i), 1)

            def hide(seq, j, s):
                p0.wait_read(dve, seq, "g", j)
                dve.wait_ge(p0.ready, p0.done(seq, "up", j))
                nc.vector.tensor_tensor(f0_h[:, j, :], f0_act[:, j % 2, :], p0.psum("up", j)[:, :], ALU.mult)\
                    .then_inc(p0.free("up", j), 1)
                if j < H0R:
                    p0.wait_read(dve, seq, "up", j)
                    dve.wait_ge(p0.ready, p0.done(seq, "comb", j))
                    nc.vector.tensor_tensor(f0_h[:, j, :], f0_h[:, j, :], p0.psum("comb", j)[:, :], ALU.mult)\
                        .then_inc(p0.free("comb", j), 1)

            def add_down(seq, i):
                dve.wait_ge(p0.ready, p0.done(seq, "down", i))
                nc.vector.tensor_tensor(f0_x[:, i, :], p0.psum("down", i)[:, 0:E], f0_x[:, i, :], ALU.add)\
                    .then_inc(p0.free("down", i), 1)

            def convolve(seq, s):
                for tap in range(TAPS - 1):
                    for j in range(NB):
                        if tap == 0:
                            dve.wait_ge(xc_copied, seq * NB + j + 1)
                            pm.wait_read(dve, seq, "xc", j)
                        else:
                            s.wait((tap - 1) * NB + j + 1)
                        step = nc.vector.scalar_tensor_tensor(m_xs[:, j, :], m_xc[:, j, tap:tap + L],
                                                              conv_w[:, j, tap:tap + 1], m_xs[:, j, :],
                                                              ALU.mult, ALU.add)
                        if tap < TAPS - 2:
                            s.mark(step)
                        else:
                            step.then_inc(conv_done, 1)

            def split(seq, s):
                dve.wait_ge(high_out, seq + 1)
                nc.vector.tensor_tensor(m_rest[:, :], pm.psum("bc")[0:64, :], m_bc[0:64, :], ALU.subtract)\
                    .then_inc(pm.free("bc"), 1)
                pm.wait_read(dve, seq, "bc")
                s.mark(nc.vector.tensor_copy(m_bc[0:64, :], m_rest[:, :]))
                s.wait()
                nc.vector.tensor_tensor(m_bc[0:32, :], m_rest[0:32, :], m_bc[0:32, :], ALU.subtract)\
                    .then_inc(parts_done, 1)

            def step_sizes(seq, s):
                dve.wait_ge(soft_log, (seq + 1) * NB)
                dve.wait_ge(soft_low, (seq + 1) * NB)
                s.mark(nc.vector.tensor_tensor(m_h[:, :, :], m_h[:, :, :], m_dBx[:, :, :], ALU.max))
                s.wait()
                nc.vector.tensor_tensor(m_dt[:, :, :], m_dt[:, :, :], m_h[:, :, :], ALU.add).then_inc(dt_done, 1)

            def scan_state(seq, n, between):
                at = (seq * N + n) * 2
                rows = [slice(q * HALF, (q + 1) * HALF) for q in range(2)]
                for q in range(2):
                    dve.wait_ge(dA_done, at + q + 1)
                    dve.wait_ge(dBx_done, at + q + 1)
                    if n:
                        dve.wait_ge(summed, at - 1 + q)
                    h, a, b = (v[:, rows[q], :].rearrange("p j t -> p (j t)") for v in (m_h, m_dA, m_dBx))
                    nc.vector.tensor_tensor_scan(h, a, b, 0.0, ALU.mult, ALU.add).then_inc(scanned, 1)
                    between(q)
                dve.wait_ge(pm.ready, pm.done(seq, "C", n))
                for q in range(2):
                    dve.wait_ge(scanned, at + q + 1)
                    state_c = pm.psum("C", n)[:, :].unsqueeze(1).to_broadcast([P, HALF, L])
                    nc.vector.tensor_tensor(m_h[:, rows[q], :], m_h[:, rows[q], :], state_c, ALU.mult)\
                        .then_inc(pm.free("C", n) if q else m_product, 1)
                    between(2 + q)
                if n == 0:
                    dve.wait_ge(y_begun, (seq + 1) * NB)
                for q in range(2):
                    if q:
                        pm.wait_read(dve, seq, "C", n)
                    else:
                        dve.wait_ge(m_product, seq * N + n + 1)
                    if n:
                        dve.wait_ge(summed, at - 1 + q)
                    nc.vector.tensor_tensor(m_xs[:, rows[q], :], m_xs[:, rows[q], :], m_h[:, rows[q], :], ALU.add)\
                        .then_inc(summed, 1)

            def add_scan(seq):
                dve.wait_ge(x2_copied, seq + 1)
                for i in range(NT):
                    dve.wait_ge(pm.ready, pm.done(seq, "out", i))
                    nc.vector.tensor_tensor(f1_x[:, i, :], pm.psum("out", i)[:, 0:E], m_x[:, i, :], ALU.add)\
                        .then_inc(pm.free("out", i), 1)

            def begin_acc(seq):
                dve.wait_ge(stored, 16 * seq + 1)
                for i in range(NT):
                    dve.wait_ge(p1.ready, p1.done(seq, "b2", i))
                    nc.vector.tensor_tensor(f1_acc[:, i, :], p1.psum("b2", i)[:, 0:E], f1_x[:, i, :], ALU.add)\
                        .then_inc(p1.free("b2", i), 1)

            def add_expert(seq, e, i):
                dve.wait_ge(p1.ready, p1.done(seq, "y", e, i))
                if e:
                    p1.wait_read(dve, seq, "y", e - 1, i)
                else:
                    p1.wait_read(dve, seq, "b2", i)
                nc.vector.scalar_tensor_tensor(f1_acc[:, i, :], p1.psum("y", e, i)[:, 0:E], r1.comb[:, i, 0, e:e + 1],
                                               f1_acc[:, i, :], ALU.mult, ALU.add)\
                    .then_inc(p1.free("y", e, i), 1)

            def turn(t, first, scan, second, more):
                s0 = Steps(dve, f0_step, STEPS_F0, t)
                sm = Steps(dve, m_step, STEPS_M, t - 1)
                s1 = Steps(dve, f1_step, STEPS_F1, t - 2)
                if scan:
                    for i in range(NT):
                        p0.wait_read(dve, t - 1, "down", i)
                    statistics(m, t - 1)
                if second:
                    for i in range(NT):
                        pm.wait_read(dve, t - 2, "out", i)
                    statistics(f1, t - 2)
                if scan:
                    normalise(m, t - 1)
                if second:
                    normalise(f1, t - 2)
                if first:
                    add_o(t)
                    for i in range(NT):
                        p0.wait_read(dve, t, "o", i)
                    statistics(f0, t)
                if scan:
                    convolve(t - 1, sm)
                if first:
                    normalise(f0, t)
                if second:
                    rank(r1, p1, t - 2, s1)
                if first:
                    rank(r0, p0, t, s0)
                if second:
                    weigh(r1, t - 2, s1)
                if first:
                    weigh(r0, t, s0)
                if scan:
                    split(t - 1, sm)
                if second:
                    begin_acc(t - 2)
                if first:
                    split_comb(t, s0)
                for j in range(H0):
                    if first:
                        hide(t, j, s0)
                    if j == 5 and scan:
                        step_sizes(t - 1, sm)
                for n in range(N):
                    def between(q):
                        if second and n % 2:
                            add_expert(t - 2, n // 2, q)
                        if first and q == 3 and n in DOWN_AT:
                            add_down(t, DOWN_AT.index(n))
                    if scan:
                        scan_state(t - 1, n, between)
                    else:
                        for q in range(NT):
                            between(q)
                if scan:
                    add_scan(t - 1)
                if first:
                    s0.close()
                if scan:
                    sm.close()
                if second:
                    s1.close()

            turns(dve, turn)

        @block.scalar
        def _(act):
            act.wait_ge(A_done, 1)
            nc.scalar.activation(A[:, :, :], A[:, :, :], ACT.Exp).then_inc(A_done, 1)
            act.wait_ge(A_done, 3)
            act.wait_ge(pad_set, 1)

            def copy_xT(n, p, seq):
                for k in range(KE):
                    act.wait_ge(p.ready, p.done(seq, "xT", k))
                    nc.scalar.copy(n.xT[:, k, :], p.psum("xT", k)[:, :]).then_inc(p.free("xT", k), 1)

            def copy_xc(seq, j):
                act.wait_ge(pm.ready, pm.done(seq, "xc", j))
                psum = pm.psum("xc", j)[:, :]
                nc.scalar.copy(m_xc[:, j, TAPS - 1:], psum).then_inc(xc_copied, 1)
                nc.scalar.activation(m_xs[:, j, :], psum, ACT.Identity, bias=conv_b[:, j:j + 1],
                                     scale=conv_w[:, j, TAPS - 1:TAPS]).then_inc(pm.free("xc", j), 1)

            def gate(seq, j):
                act.wait_ge(pm.ready, pm.done(seq, "res", j))
                nc.scalar.activation(m_res[:, j, :], pm.psum("res", j)[:, :], ACT.Silu)\
                    .then_inc(pm.free("res", j), 1)

            def activate_conv(seq, j):
                act.wait_ge(conv_done, seq * NB + j + 1)
                nc.scalar.activation(m_xs[:, j, :], m_xs[:, j, :], ACT.Silu).then_inc(xs_done, 1)

            def exp_gap(r, seq):
                act.wait_ge(r.gap_done, seq + 1)
                nc.scalar.activation(r.exp[:, :, :], r.gap[:, :, :], ACT.Exp).then_inc(r.exp_done, 1)

            def copy_comb1T(seq):
                act.wait_ge(p1.ready, p1.done(seq, "combT"))
                nc.scalar.copy(comb1T, p1.psum("combT")[0:E1, :]).then_inc(p1.free("combT"), 1)

            def round_comb0T(seq):
                act.wait_ge(p0.ready, p0.done(seq, "combT"))
                nc.scalar.copy(parts, p0.psum("combT")[0:3 * E0, :]).then_inc(comb_high, 1)

            def low_rank(seq):
                act.wait_ge(pm.ready, pm.done(seq, "dtr"))
                nc.scalar.copy(m_dtr[:, :], pm.psum("dtr")[0:RK, :]).then_inc(pm.free("dtr"), 1)
                act.wait_ge(pm.ready, pm.done(seq, "bc"))
                nc.scalar.copy(m_bc[:, :], pm.psum("bc")[0:96, :]).then_inc(high_out, 1)

            def softplus(seq):
                for j in range(NB):
                    act.wait_ge(pm.ready, pm.done(seq, "dt", j))
                    psum = pm.psum("dt", j)[:, :]
                    nc.scalar.activation(m_dA[:, j, :], psum, ACT.Abs, bias=dt_b[:, j:j + 1]).then_inc(soft_in, 1)
                    nc.scalar.activation(m_dt[:, j, :], psum, ACT.Relu, bias=dt_b[:, j:j + 1])\
                        .then_inc(pm.free("dt", j), 1)
                for j in range(NB):
                    act.wait_ge(soft_in, seq * NB + j + 1)
                    nc.scalar.activation(m_dA[:, j, :], m_dA[:, j, :], ACT.Exp, scale=-1.0).then_inc(soft_exp, 1)
                for j in range(NB):
                    act.wait_ge(soft_exp, seq * NB + j + 1)
                    nc.scalar.activation(m_h[:, j, :], m_dA[:, j, :], ACT.Ln, bias=1.0).then_inc(soft_log, 1)

            def begin_y(seq):
                act.wait_ge(dtx_done, seq + 1)
                for j in range(NB):
                    nc.scalar.activation(m_xs[:, j, :], m_xs[:, j, :], ACT.Identity, scale=D[:, j:j + 1])\
                        .then_inc(y_begun, 1)

            def copy_B(seq, n):
                act.wait_ge(pm.ready, pm.done(seq, "B", n))
                if n >= 2:
                    act.wait_ge(dBx_done, (seq * N + n - 1) * 2)
                nc.scalar.copy(m_B[:, n % 2, :], pm.psum("B", n)[:, :]).then_inc(pm.free("B", n), 1)

            def decays(seq, n, q):
                if n:
                    act.wait_ge(scanned, (seq * N + n - 1) * 2 + q + 1)
                elif q == 0:
                    act.wait_ge(dA_zero, seq + 1)
                    act.wait_ge(dt_done, seq + 1)
                for j in range(q * HALF, (q + 1) * HALF):
                    last = nc.scalar.activation(m_dA[:, j, 1:], m_dt[:, j, 1:], ACT.Exp, scale=A[:, j, n:n + 1])
                last.then_inc(dA_done, 1)

            def relu(seq, e, j):
                act.wait_ge(p1.ready, p1.done(seq, "z", e, j))
                if e >= 2 and j == 0:
                    act.wait_ge(p1.ready, p1.done(seq, "y", e - 2, NT - 1))
                nc.scalar.activation(f1_h[:, e % 2, j, :], p1.psum("z", e, j)[:, :], ACT.Relu, bias=b1[:, e, j:j + 1])\
                    .then_inc(p1.free("z", e, j), 1)

            def silu(seq, j):
                act.wait_ge(p0.ready, p0.done(seq, "g", j))
                if j >= 2:
                    p0.wait_read(act, seq, "up", j - 2)
                elif j == 0:
                    act.wait_ge(comb_parts, seq + 1)
                nc.scalar.activation(f0_act[:, j % 2, :], p0.psum("g", j)[:, :], ACT.Silu)\
                    .then_inc(p0.free("g", j), 1)

            def turn(t, first, scan, second, more):
                if scan:
                    copy_xT(m, pm, t - 1)
                if second:
                    copy_xT(f1, p1, t - 2)
                if scan:
                    for j in range(NB):
                        copy_xc(t - 1, j)
                if first:
                    copy_xT(f0, p0, t)
                if scan:
                    for j in range(NB):
                        gate(t - 1, j)
                    for j in range(NB):
                        activate_conv(t - 1, j)
                if second:
                    exp_gap(r1, t - 2)
                if first:
                    exp_gap(r0, t)
                if scan:
                    low_rank(t - 1)
                if second:
                    copy_comb1T(t - 2)
                if first:
                    round_comb0T(t)
                    for j in range(4):
                        silu(t, j)
                if scan:
                    softplus(t - 1)
                if first:
                    for j in range(4, H0):
                        silu(t, j)
                if scan:
                    begin_y(t - 1)
                    copy_B(t - 1, 0)
                    for q in range(2):
                        decays(t - 1, 0, q)
                for n in range(N):
                    if scan and n + 1 < N:
                        copy_B(t - 1, n + 1)
                        decays(t - 1, n + 1, 0)
                    if second and n % 2 == 0:
                        relu(t - 2, n // 2, 0)
                        relu(t - 2, n // 2, 1)
                    if scan and n + 1 < N:
                        decays(t - 1, n + 1, 1)
                    if second and n % 2 == 0:
                        relu(t - 2, n // 2, 2)
                        relu(t - 2, n // 2, 3)

            turns(act, turn)

        @block.tensor
        def _(pe):
            pe.wait_ge(loaded, LOADED)
            pe.wait_ge(pick_set, 2)

            def transpose_x(n, p, seq):
                pe.wait_ge(n.xn_done, (seq + 1) * NT)
                for k in range(KE):
                    pe.wait_ge(p.free("xT", k), p.before(seq, "xT", k))
                    for i in range(NT):
                        last = nc.tensor.transpose(p.psum("xT", k)[:, i * P:(i + 1) * P],
                                                   n.xn[:, i, k * P:(k + 1) * P], ident[:, :])
                    last.then_inc(p.ready, 1)

            def product(p, seq, key, out, pairs):
                pe.wait_ge(p.free(*key), p.before(seq, *key))
                for k, (weights, moving) in enumerate(pairs):
                    last = nc.tensor.matmul(out, weights, moving, start=(k == 0), stop=(k == len(pairs) - 1))
                last.then_inc(p.ready, 1)

            def logits(n, p, seq, weights, experts):
                for k in range(KE):
                    p.wait_read(pe, seq, "xT", k)
                pe.wait_ge(p.free("logits"), p.before(seq, "logits"))
                for i in range(NT):
                    for k in range(KE):
                        last = nc.tensor.matmul(p.psum("logits")[:, i * experts:(i + 1) * experts],
                                                n.xT[:, k, i * P:(i + 1) * P], weights[:, k, :],
                                                start=(k == 0), stop=(k == KE - 1))
                last.then_inc(p.ready, 1)

            def transpose_comb(r, p, seq):
                pe.wait_ge(r.comb_done, seq + 1)
                pe.wait_ge(p.free("combT"), p.before(seq, "combT"))
                for i in range(NT):
                    comb = r.comb[:, i, :, :].rearrange("p a n -> p (a n)")
                    last = nc.tensor.matmul(p.psum("combT")[0:comb.shape[1], i * P:(i + 1) * P], comb,
                                            ident[:, :], start=True, stop=True)
                last.then_inc(p.ready, 1)

            def outputs(seq):
                pe.wait_ge(gated_in, 16 * (seq + 1))
                for i in range(NT):
                    product(p0, seq, ("o", i), p0.psum("o", i)[:, 0:E],
                            [(f0_h[:, k, i * P:(i + 1) * P], o_w[:, k, :]) for k in range(NCG)])

            def gate_up(seq, j):
                for w, name in ((g_w, "g"), (up_w, "up")):
                    product(p0, seq, (name, j), p0.psum(name, j)[:, :],
                            [(w[:, k, j, :], f0.xT[:, k, :]) for k in range(KE)])
                if j < H0R:
                    if j == 0:
                        pe.wait_ge(comb_parts, seq + 1)
                    product(p0, seq, ("comb", j), p0.psum("comb", j)[:, :], [(picks[:, j, :], parts)])

            def down(seq, i):
                for key in (("comb", H0R - 1), ("up", H0 - 2), ("up", H0 - 1)):
                    p0.wait_read(pe, seq, *key)
                product(p0, seq, ("down", i), p0.psum("down", i)[:, 0:E],
                        [(f0_h[:, j, i * P:(i + 1) * P], down_w[:, j, :]) for j in range(H0)])

            def enter(seq, name, at):
                for j in range(NB):
                    product(pm, seq, (name, j), pm.psum(name, j)[:, :],
                            [(in_w[:, k, at + j, :], m.xT[:, k, :]) for k in range(KE)])

            def low_rank(seq):
                pe.wait_ge(xs_done, (seq + 1) * NB)
                product(pm, seq, ("dtr",), pm.psum("dtr")[0:RK, :],
                        [(x_w[:, j, 0:RK], m_xs[:, j, :]) for j in range(NB)])
                product(pm, seq, ("bc",), pm.psum("bc")[0:96, :],
                        [(x_w[:, j, RK:], m_xs[:, j, :]) for j in range(NB)])

            def step_sizes(seq):
                pm.wait_read(pe, seq, "dtr")
                for j in range(NB):
                    product(pm, seq, ("dt", j), pm.psum("dt", j)[:, :], [(dt_w[:, j, :], m_dtr[:, :])])

            def spread(seq, name, n):
                row = n if name == "B" else N + n
                product(pm, seq, (name, n), pm.psum(name, n)[:, :],
                        [(pick32[:, row:row + 1].to_broadcast([96, P]), m_bc[:, :])])

            def leave(seq):
                pe.wait_ge(y_done, seq + 1)
                for i in range(NT):
                    product(pm, seq, ("out", i), pm.psum("out", i)[:, 0:E],
                            [(m_xs[:, j, i * P:(i + 1) * P], y_w[:, j, :]) for j in range(NB)])

            def bias2(seq):
                p1.wait_read(pe, seq, "combT")
                for i in range(NT):
                    product(p1, seq, ("b2", i), p1.psum("b2", i)[:, 0:E],
                            [(comb1T[:, i * P:(i + 1) * P], b2[:, :])])

            def expert_up(seq, e):
                pe.wait_ge(w12_in[e % 2], (seq * (E1 // 2) + e // 2 + 1) * 16)
                for j in range(H1):
                    product(p1, seq, ("z", e, j), p1.psum("z", e, j)[:, :],
                            [(w1[e % 2][:, k, j * P:(j + 1) * P], f1.xT[:, k, :]) for k in range(KE)])

            def expert_down(seq, e):
                for j in range(H1):
                    p1.wait_read(pe, seq, "z", e, j)
                for i in range(NT):
                    product(p1, seq, ("y", e, i), p1.psum("y", e, i)[:, 0:E],
                            [(f1_h[:, e % 2, j, i * P:(i + 1) * P], w2[e % 2][:, j, :]) for j in range(H1)])

            def turn(t, first, scan, second, more):
                if scan:
                    transpose_x(m, pm, t - 1)
                if second:
                    transpose_x(f1, p1, t - 2)
                if first:
                    outputs(t)
                if scan:
                    for k in range(KE):
                        pm.wait_read(pe, t - 1, "xT", k)
                    enter(t - 1, "xc", 0)
                if second:
                    logits(f1, p1, t - 2, gate_w, E1)
                if first:
                    transpose_x(f0, p0, t)
                if scan:
                    enter(t - 1, "res", NB)
                if first:
                    logits(f0, p0, t, router_w, E0)
                if scan:
                    low_rank(t - 1)
                if second:
                    transpose_comb(r1, p1, t - 2)
                if first:
                    transpose_comb(r0, p0, t)
                if second:
                    bias2(t - 2)
                if first:
                    for j in range(4):
                        gate_up(t, j)
                if scan:
                    step_sizes(t - 1)
                if first:
                    for j in range(4, H0):
                        gate_up(t, j)
                if scan:
                    pe.wait_ge(parts_done, t)
                    spread(t - 1, "B", 0)
                    spread(t - 1, "C", 0)
                for n in range(N):
                    if scan and n + 1 < N:
                        spread(t - 1, "B", n + 1)
                    if second:
                        if n % 2 == 0:
                            expert_up(t - 2, n // 2)
                        else:
                            expert_down(t - 2, n // 2)
                    if first and n in DOWN_AT:
                        down(t, DOWN_AT.index(n))
                    if scan and n + 1 < N:
                        spread(t - 1, "C", n + 1)
                if scan:
                    leave(t - 1)

            turns(pe, turn)


DOWN_AT = [10, 11, 12, 13]
STEPS_F0, STEPS_M, STEPS_F1 = 20, 10, 17


def build(nc, a, out):
    pad = nc.dram_tensor("pad_coefficients", (D1, ROW), FP32, kind="Internal").ap()
    gated = nc.dram_tensor("gated", (NCG, P, B, L), FP32, kind="Internal").ap()
    position_coefficients(nc, a, pad)
    conv = nc.dram_tensor("convolved", (NCG, NM, CB // 2, P, P), FP32, kind="Internal").ap()
    toeplitz_unit(nc, a, a["x_back"], pad, conv, gated)
    mixtures_and_scan(nc, a, a["x"], gated, out)


def arrays_of(w):
    def f(name):
        return np.asarray(w[name])

    def rows(m):
        return np.ascontiguousarray(m.reshape(-1, P, m.shape[-1]).transpose(1, 0, 2))

    def columns(v):
        return np.ascontiguousarray(v.reshape(-1, P).T)

    def grouped(m):
        return np.ascontiguousarray(m.reshape(-1, P, m.shape[1] // P, P).transpose(2, 1, 0, 3))

    a = {
        "x": f("L0_attn_x"),
        "x_back": np.ascontiguousarray(f("L0_attn_x").reshape(B, NT, P, E)[:, :, ::-1]).reshape(B, L, E),
        "ident": np.eye(P, dtype=np.float32),
        "positions": columns(np.arange(L, dtype=np.float32)),
        "decay": np.power(np.float32(0.99), np.arange(L, dtype=np.float32)).astype(np.float32),
        "pos_w": f("L0_attn_pos_w")[0], "pos_b": f("L0_attn_pos_b"),
        "layer_w": np.stack([f(f"L0_attn_lw{i}") for i in range(3)], axis=1),
        "layer_b": np.stack([f(f"L0_attn_lb{i}") for i in range(3)]),
        "out_w": f("L0_attn_out_w"), "out_b": columns(f("L0_attn_out_b")),
        "u_w": grouped(f("L0_attn_u_w")), "u_b": f("L0_attn_u_b").reshape(-1, P, 1),
        "v_w": grouped(f("L0_attn_v_w")), "v_b": f("L0_attn_v_b").reshape(-1, P),
        "o_w": rows(f("L0_attn_o_w")), "o_b": f("L0_attn_o_b"),
    }
    def merged(routed, shared):
        both = np.concatenate([m.transpose(1, 0, 2).reshape(E, -1) for m in (routed, shared)], axis=1)
        return np.ascontiguousarray(rows(both).reshape(P, KE, H0, P))

    def down(routed, shared):
        return rows(np.concatenate([m.reshape(-1, E) for m in (routed, shared)], axis=0))

    x_w = f("L1_attn_W_x")
    first = f("L1_ffn_W1").reshape(E1, H1 * P, KE, P).transpose(0, 3, 2, 1).reshape(E1, P, -1)
    second = f("L1_ffn_W2").reshape(E1, E, H1, P).transpose(0, 3, 2, 1).reshape(E1, P, -1)
    a |= {
        "iota": np.arange(E0, dtype=np.float32),
        "picks": np.tile(np.repeat(np.eye(E0, dtype=np.float32), P // 2, axis=1).reshape(E0, H0R, P), (3, 1, 1)),
        "pick32": np.tile(np.eye(32, dtype=np.float32), (3, 1)),
        "router_w": rows(f("L0_ffn_router_w")),
        "g_w": merged(f("L0_ffn_wg_r"), f("L0_ffn_wg_s")),
        "up_w": merged(f("L0_ffn_wu_r"), f("L0_ffn_wu_s")),
        "down_w": down(f("L0_ffn_wd_r"), f("L0_ffn_wd_s")),
        "in_w": np.ascontiguousarray(rows(f("L1_attn_W_in")).reshape(P, KE, 2 * NB, P)),
        "conv_w": rows(f("L1_attn_conv_w")), "conv_b": columns(f("L1_attn_conv_b")),
        "x_w": rows(np.concatenate([x_w[:, :RK]] + [x_w[:, RK:]] * 3, axis=1)),
        "dt_w": np.ascontiguousarray(f("L1_attn_W_dt").reshape(RK, NB, P)), "dt_b": columns(f("L1_attn_b_dt")),
        "A_log": rows(f("L1_attn_A_log")), "D": columns(f("L1_attn_D")), "y_w": rows(f("L1_attn_W_out")),
        "gate_w": rows(np.ascontiguousarray(f("L1_ffn_Wg").T)), "gate_b": f("L1_ffn_bg"),
        "b1": np.ascontiguousarray(f("L1_ffn_b1").reshape(E1, H1, P).transpose(2, 0, 1)), "b2": f("L1_ffn_b2"),
        "w12": np.ascontiguousarray(np.concatenate([first, second], axis=2)),
    }
    return a


def kernel(**inputs):
    import concourse.bacc as bacc
    from concourse.bass_utils import run_bass_kernel_spmd

    nc = bacc.Bacc("TRN2", target_bir_lowering=False, num_devices=1)
    arrays, aps = {}, {}
    for name, array in arrays_of(inputs).items():
        arrays[f"in_{name}"] = array
        aps[name] = nc.dram_tensor(f"in_{name}", array.shape, mybir.dt.from_np(array.dtype), kind="ExternalInput").ap()
    out = nc.dram_tensor("out", (B, L, E), FP32, kind="ExternalOutput").ap()
    build(nc, aps, out)
    result = run_bass_kernel_spmd(nc, [arrays], core_ids=[0])
    return result.results[0]["out"]
```

```python
from contextlib import ExitStack

import numpy as np

import concourse.bass as bass
from concourse import mybir

FP32 = mybir.dt.float32
BF16 = mybir.dt.bfloat16
F32R = mybir.dt.float32r
U32 = mybir.dt.uint32
ALU = mybir.AluOpType
ACT = mybir.ActivationFunctionType
AX = mybir.AxisListType

P = 128
B, L, E = 16, 512, 256
NT = L // P
KE = E // P
LN_EPS = 1e-5

R = 128
D1 = 768
NCG = D1 // P
SRMS_EPS = 1e-8
PAD = P - 1
ROW = PAD + L + 1
NJ = NT * B
CB = 8
NM = P // CB
E1 = 8
H1 = 4
W1 = KE * H1 * P
CT = 4
RING_T = 4
RING_C = 2
PH = P // 2


def position_coefficients(nc, c, pad_dram):
    ctx = ExitStack()
    with ctx:
        def sb(name, shape, dt=FP32):
            return ctx.enter_context(nc.sbuf_tensor(name, shape, dt))

        def sem(name):
            return ctx.enter_context(nc.semaphore(name))

        ident = sb("p_ident", [P, P])
        positions = sb("p_positions", [P, NT])
        first_w = sb("p_first_w", [P, R])
        first_b = sb("p_first_b", [P, R])
        layer_w = sb("p_layer_w", [P, 3, R])
        layer_b = sb("p_layer_b", [P, 3, R])
        out_w = sb("p_out_w", [P, D1])
        out_b = sb("p_out_b", [P, NCG])
        decay = sb("p_decay", [P, L])
        h = sb("p_h", [P, NT, R])
        square = sb("p_square", [P, NT, R])
        norm = sb("p_norm", [P, NT])
        rms = sb("p_rms", [P, NT])
        inverse = sb("p_inverse", [P, NT])
        active = sb("p_active", [P, NT, R])
        activeT = sb("p_activeT", [P, L])
        raw = sb("p_raw", [P, NCG, L])
        padded = sb("p_padded", [P, NCG, ROW])
        pT = ctx.enter_context(nc.psum_tensor("p_pT", [P, L], FP32))
        pH = ctx.enter_context(nc.psum_tensor("p_pH", [P, NT, R], FP32))
        pC = [ctx.enter_context(nc.psum_tensor(f"p_pC{i}", [P, L], FP32)) for i in range(2)]

        loaded = sem("p_loaded")
        h_ready = sem("p_h_ready")
        squared = sem("p_squared")
        summed = sem("p_summed")
        rooted = sem("p_rooted")
        step = sem("p_step")
        active_ready = sem("p_active")
        turned = sem("p_turned")
        turned_out = sem("p_turned_out")
        layer_done = sem("p_layer_done")
        coef_done = sem("p_coef_done")
        coef_out = sem("p_coef_out")
        zeroed = sem("p_zeroed")
        decayed = sem("p_decayed")
        stored = sem("p_stored")

        block = ctx.enter_context(nc.Block())

        @block.sync
        def _(sp):
            for dst, src in ((ident[:, :], c["ident"]), (positions[:, :], c["positions"]),
                             (first_w[:, :], c["pos_w"].partition_broadcast(P)),
                             (first_b[:, :], c["pos_b"].partition_broadcast(P)),
                             (layer_w[:, :, :], c["layer_w"]),
                             (layer_b[:, :, :], c["layer_b"].partition_broadcast(P)),
                             (out_w[:, :], c["out_w"]), (out_b[:, :], c["out_b"]),
                             (decay[:, :], c["decay"].partition_broadcast(P))):
                sp.dma_start(dst, src).then_inc(loaded, 16)
            sp.wait_ge(decayed, NCG)
            sp.dma_start(pad_dram.rearrange("(g p) r -> p g r", p=P), padded[:, :, :]).then_inc(stored, 16)
            sp.wait_ge(stored, 16)

        @block.gpsimd
        def _(pool):
            nc.gpsimd.memset(padded[:, :, :], 0.0).then_inc(zeroed, 1)

        @block.vector
        def _(dve):
            steps = 0
            dve.wait_ge(loaded, 16 * 9)
            for i in range(NT):
                nc.vector.scalar_tensor_tensor(h[:, i, :], first_w[:, :], positions[:, i:i + 1], first_b[:, :],
                                               ALU.mult, ALU.add).then_inc(h_ready, 1)
            for layer in range(4):
                dve.wait_ge(h_ready, NT if layer == 0 else NT + layer)
                nc.vector.tensor_tensor(square[:, :, :], h[:, :, :], h[:, :, :], ALU.mult).then_inc(squared, 1)
                dve.wait_ge(squared, layer + 1)
                nc.vector.tensor_reduce(norm[:, :], square[:, :, :], AX.X, ALU.add).then_inc(summed, 1)
                dve.wait_ge(rooted, layer + 1)
                nc.vector.tensor_scalar(rms[:, :], rms[:, :], float(R) ** -0.5, SRMS_EPS, ALU.mult,
                                        ALU.add).then_inc(step, 1)
                steps += 1
                dve.wait_ge(step, steps)
                nc.vector.reciprocal(inverse[:, :], rms[:, :]).then_inc(step, 1)
                steps += 1
                dve.wait_ge(step, steps)
                for i in range(NT):
                    nc.vector.tensor_scalar(active[:, i, :], h[:, i, :], inverse[:, i:i + 1], 0.0, ALU.mult,
                                            ALU.max).then_inc(active_ready, 1)
                if layer < 3:
                    dve.wait_ge(layer_done, layer + 1)
                    dve.wait_ge(active_ready, NT * (layer + 1))
                    bias = layer_b[:, layer:layer + 1, :].to_broadcast([P, NT, R])
                    nc.vector.tensor_tensor(h[:, :, :], pH[:, :, :], bias, ALU.add).then_inc(h_ready, 1)
            dve.wait_ge(zeroed, 1)
            for g in range(NCG):
                dve.wait_ge(coef_out, g + 1)
                nc.vector.tensor_tensor(padded[:, g, PAD:PAD + L], raw[:, g, :], decay[:, :],
                                        ALU.mult).then_inc(decayed, 1)

        @block.scalar
        def _(act):
            for layer in range(4):
                act.wait_ge(summed, layer + 1)
                nc.scalar.activation(rms[:, :], norm[:, :], ACT.Sqrt).then_inc(rooted, 1)
                act.wait_ge(turned, layer + 1)
                nc.scalar.copy(activeT[:, :], pT[:, :]).then_inc(turned_out, 1)
            for g in range(NCG):
                act.wait_ge(coef_done, g + 1)
                nc.scalar.activation(raw[:, g, :], pC[g % 2][:, :], ACT.Identity,
                                     bias=out_b[:, g:g + 1]).then_inc(coef_out, 1)

        @block.tensor
        def _(pe):
            pe.wait_ge(loaded, 16 * 9)
            for layer in range(4):
                pe.wait_ge(active_ready, NT * (layer + 1))
                for i in range(NT):
                    last = nc.tensor.transpose(pT[:, i * P:(i + 1) * P], active[:, i, :], ident[:, :])
                last.then_inc(turned, 1)
                pe.wait_ge(turned_out, layer + 1)
                if layer < 3:
                    for i in range(NT):
                        last = nc.tensor.matmul(pH[:, i, :], activeT[:, i * P:(i + 1) * P], layer_w[:, layer, :],
                                                start=True, stop=True)
                    last.then_inc(layer_done, 1)
            for g in range(NCG):
                if g >= 2:
                    pe.wait_ge(coef_out, g - 1)
                nc.tensor.matmul(pC[g % 2][:, :], out_w[:, g * P:(g + 1) * P], activeT[:, :],
                                 start=True, stop=True).then_inc(coef_done, 1)


def toeplitz_unit(nc, c, x_dram, pad_dram, conv_dram, gated_dram, w1_dram):
    ctx = ExitStack()
    with ctx:
        def sb(name, shape, dt=FP32):
            return ctx.enter_context(nc.sbuf_tensor(name, shape, dt))

        def sem(name):
            return ctx.enter_context(nc.semaphore(name))

        ident = sb("t_ident", [P, P])
        half = sb("t_half", [P, NT])
        xnT = sb("t_xnT", [P, KE, B * L])
        V = [sb(f"t_V{r}", [P, P, NJ]) for r in range(2)]
        T = sb("t_T", [P, RING_T, CT, L + PH])
        result = sb("t_result", [P, RING_C, CB // 2, P])
        x = sb("t_x", [P, 2, NT, E])
        xn = T[:, :, :, :].rearrange("p r a f -> p (r a f)")[:, 0:2 * NT * E]\
            .rearrange("p (r i e) -> p r i e", r=2, e=E)
        stats = sb("t_stats", [P, 2, NT, 6])
        moments = sb("t_moments", [P, 2, NT, 2])
        shifted = sb("t_shifted", [P, 2, NT])
        rstd = sb("t_rstd", [P, 2, NT])
        v_w = sb("t_v_w", [P, 2, KE, P])
        v_b = sb("t_v_b", [P, 2, P])
        v_sum = sb("t_v_sum", [P, 2, NT, P])
        u_w = sb("t_u_w", [P, 2, KE, P])
        u_b = sb("t_u_b", [P, 2])
        u_act = sb("t_u_act", [P, 2, NT, P])
        conv = sb("t_conv", [P, 2, NT, P])
        gated = sb("t_gated", [P, 2, NT, P])
        zero = sb("t_zero", [1, L], BF16)
        bank = [ctx.enter_context(nc.psum_tensor(f"t_bank{i}", [P, L], FP32)) for i in range(8)]
        v_bank, conv_bank, u_bank = bank[0:2], bank[2:6], bank[6:8]
        NV = len(conv_bank)

        const_in = sem("t_const_in")
        half_set = sem("t_half_set")
        zero_set = sem("t_zero_set")
        x_in = [sem(f"t_x_in{r}") for r in range(2)]
        stat_done = sem("t_stat")
        var_done = sem("t_var")
        eps_added = sem("t_eps")
        rstd_done = sem("t_rstd_done")
        xn_done = sem("t_xn_done")
        xnT_done = sem("t_xnT_done")
        xnT_out = sem("t_xnT_out")
        v_done = sem("t_v_done")
        v_biased = sem("t_v_biased")
        v_out = sem("t_v_out")
        T_used = sem("t_T_used")
        conv_out = sem("t_conv_out")
        stored = [sem(f"t_stored{r}") for r in range(RING_C)]
        u_done = sem("t_u_done")
        u_out = sem("t_u_out")
        gated_done = sem("t_gated_done")
        gated_stored = [sem(f"t_gated_stored{r}") for r in range(2)]
        u_in = [sem(f"t_u_in{r}") for r in range(2)]
        conv_in = [sem(f"t_conv_in{r}") for r in range(2)]
        w_in = [sem(f"t_w_in{r}") for r in range(2)]
        T_in = [sem(f"t_T_in{r}") for r in range(RING_T)]
        T_full = [sem(f"t_T_full{r}") for r in range(2)]
        split_in = sem("t_split_in")
        split_high = sem("t_split_high")
        split_low = sem("t_split_low")
        split_stored = sem("t_split_stored")
        passed = sem("t_passed")

        block = ctx.enter_context(nc.Block())
        x_v = x_dram.rearrange("b (i p) e -> b p i e", p=P)
        LOADS = P // CT
        PER = CB // CT

        def groups(engine, group):
            group(0, 0, 1, False, True)
            with engine.Fori(0, NCG // 2 - 1) as pair:
                group(2 * pair + 1, 1, pair + 2, True, True)
                group(2 * pair + 2, 0, pair + 2, True, True)
            group(NCG - 1, 1, NCG // 2 + 1, True, False)

        whole, high, low = (t[:, :, :, :].rearrange("p r i t -> p (r i t)") for t in (conv, gated, u_act))

        def upper(n):
            return T[PH:P, n % RING_T, :, 0:L], T[0:PH, n % RING_T, :, PH:PH + L]

        def loads_of(g, n):
            return (g * (LOADS // RING_T) + n // RING_T + 1) * 16

        @block.sync
        def _(sp):
            sp.dma_start(ident[:, :], c["ident"]).then_inc(const_in, 16)

            def load_weights(g, r):
                sp.dma_start(v_w[:, r, :, :], c["v_w"][bass.ds(g, 1), :, :, :].rearrange("o p k n -> p (o k) n"))\
                    .then_inc(w_in[r], 16)
                sp.dma_start(v_b[:, r, :], c["v_b"][bass.ds(g, 1), :].partition_broadcast(P)
                             .rearrange("p o n -> p (o n)")).then_inc(w_in[r], 16)

            def load_tiles(g, n):
                src = bass.AP(pad_dram.tensor, g * (P * ROW) + n * CT * ROW, [[1, PH], [ROW, CT], [1, L + PH]])
                sp.dma_start(T[0:PH, n % RING_T, :, :], src).then_inc(T_in[n % RING_T], 16)

            def store(g, m):
                sp.dma_start(conv_dram[bass.ds(g, 1), m, :, :, :].rearrange("o q p t -> p (o q) t"),
                             result[:, m % RING_C, :, :]).then_inc(stored[m % RING_C], 16)

            def load_gate_weights(g, r):
                sp.dma_start(u_w[:, r, :, :], c["u_w"][bass.ds(g, 1), :, :, :].rearrange("o p k n -> p (o k) n"))\
                    .then_inc(u_in[r], 16)
                sp.dma_start(u_b[:, r:r + 1], c["u_b"][bass.ds(g, 1), :, :].rearrange("o p n -> p (o n)")).then_inc(u_in[r], 16)

            def load_conv(g, b):
                sp.wait_ge(gated_done, g * B + max(b - 1, 0) + 1)
                sp.sem_inc(passed, 1)
                src = bass.AP(conv_dram.tensor, g * (P * NJ * P) + b * P, [[NJ * P, P], [B * P, NT], [1, P]])
                sp.dma_start(conv[:, b % 2, :, :], src).then_inc(conv_in[b % 2], 16)

            def store_gated(g, b):
                sp.wait_ge(gated_done, g * B + b + 2)
                sp.sem_inc(passed, 1)
                sp.dma_start(gated_dram[bass.ds(g, 1), :, b, :].rearrange("o p t -> p (o t)"),
                             gated[:, b % 2, :, :].rearrange("p i t -> p (i t)")).then_inc(gated_stored[b % 2], 16)

            load_weights(0, 0)

            def load_x(pair, r):
                sp.dma_start(x[:, r, :, :], x_v[bass.ds(2 * pair + r, 1), :, :, :].rearrange("o p i e -> p (o i) e"))\
                    .then_inc(x_in[r], 16)

            for r in range(2):
                load_x(0, r)
            with sp.Fori(1, B // 2) as pair:
                for r in range(2):
                    sp.wait_ge(xn_done, (2 * pair + r - 1) * NT + 1)
                    sp.sem_inc(passed, 1)
                    load_x(pair, r)
            sp.wait_ge(xnT_done, B + 1)
            for n in range(RING_T):
                load_tiles(0, n)

            def gate(g, m):
                if m == 0:
                    for r in range(RING_C):
                        sp.wait_ge(stored[r], 16 * (g + 1) * (NM // RING_C) + 1)
                load_conv(g, m)
                if m:
                    store_gated(g, m - 1)

            def group(g, r, loads, before, after):
                if after:
                    sp.wait_ge(v_biased, B * g + 1)
                    sp.sem_inc(passed, 1)
                    load_weights(g + 1, 1 - r)
                sp.wait_ge(u_done, B * (g - 1) + 1 if before else 1)
                sp.sem_inc(passed, 1)
                load_gate_weights(g, r)
                for m in range(NM):
                    for n in range(PER * m, PER * (m + 1)):
                        ahead = n + RING_T
                        if ahead < LOADS or after:
                            sp.wait_ge(T_used, g * LOADS + n + 2)
                            sp.sem_inc(passed, 1)
                            load_tiles(g + ahead // LOADS, ahead % LOADS)
                    if before:
                        gate(g - 1, m)
                    elif m % 2 == 0:
                        if m:
                            sp.wait_ge(split_low, m // 2)
                        sp.dma_start(whole, c["w12"][m // 2, :, 0:W1]).then_inc(split_in, 16)
                    else:
                        sp.wait_ge(split_low, m // 2 + 1)
                        sp.dma_start(w1_dram[m // 2, :, 0, :], high).then_inc(split_stored, 16)
                        sp.dma_start(w1_dram[m // 2, :, 1, :], low).then_inc(split_stored, 16)
                    sp.wait_ge(conv_out, g * NM + m + 2)
                    sp.sem_inc(passed, 1)
                    store(g, m)
                if before:
                    store_gated(g - 1, B - 1)

            groups(sp, group)
            for m in range(NM):
                gate(NCG - 1, m)
            store_gated(NCG - 1, B - 1)
            for r in range(2):
                sp.wait_ge(gated_stored[r], 16 * NCG * B // 2 + 1)

        @block.gpsimd
        def _(pool):
            nc.gpsimd.memset(half[:, :], -0.5).then_inc(half_set, 1)
            nc.gpsimd.memset(zero[:, :], 0.0).then_inc(zero_set, 1)
            pool.wait_ge(half_set, 1)
            with pool.Fori(0, B // 2) as pair:
                for r in range(2):
                    pool.wait_ge(var_done, (2 * pair + r + 1) * NT)
                    pool.sem_inc(passed, 1)
                    nc.gpsimd.tensor_scalar(shifted[:, r, :], moments[:, r, :, 1], LN_EPS, None,
                                            ALU.add).then_inc(eps_added, 1)
                    pool.wait_ge(eps_added, 2 * pair + r + 1)
                    nc.gpsimd.tensor_tensor(rstd[:, r, :], shifted[:, r, :], half[:, :], ALU.pow)\
                        .then_inc(rstd_done, 1)

        @block.vector
        def _(dve):
            for s in (xn_done, xnT_done, xnT_out, v_done, v_biased, v_out, T_used, conv_out, *stored,
                      u_done, u_out, gated_done, *gated_stored):
                dve.sem_inc(s, 1)
            with dve.Fori(0, B // 2) as pair:
                for r in range(2):
                    s = 2 * pair + r
                    dve.wait_ge(x_in[r], (pair + 1) * 16)
                    for i in range(NT):
                        nc.vector.bn_stats(stats[:, r, i, :], x[:, r, i, :]).then_inc(stat_done, 1)
                    dve.wait_ge(stat_done, (s + 1) * NT)
                    dve.sem_inc(passed, 1)
                    for i in range(NT):
                        nc.vector.bn_aggr(moments[:, r, i, :], stats[:, r, i, :]).then_inc(var_done, 1)
                for r in range(2):
                    s = 2 * pair + r
                    dve.wait_ge(rstd_done, s + 1)
                    dve.wait_ge(var_done, (s + 1) * NT)
                    dve.wait_ge(xnT_done, 2 * pair + 1)
                    for i in range(NT):
                        nc.vector.tensor_scalar(xn[:, r, i, :], x[:, r, i, :], moments[:, r, i, 0:1],
                                                rstd[:, r, i:i + 1], ALU.subtract, ALU.mult).then_inc(xn_done, 1)

            def add_bias(g, r, b):
                dve.wait_ge(v_done, g * B + b + 2)
                dve.wait_ge(v_out, g * B + max(b - 1, 0) + 1)
                psum = v_bank[b % 2][:, :].rearrange("p (i n) -> p i n", n=P)
                nc.vector.tensor_tensor(v_sum[:, b % 2, :, :], psum,
                                        v_b[:, r, :].unsqueeze(1).to_broadcast([P, NT, P]), ALU.add)\
                    .then_inc(v_biased, 1)

            def fill(g, n):
                dve.wait_ge(T_in[n % RING_T], loads_of(g, n))
                nc.vector.tensor_copy(*upper(n)).then_inc(T_full[0], 1)

            fill(0, 0)
            dve.wait_ge(w_in[0], 32)
            for b in range(B):
                add_bias(0, 0, b)

            def gate(g, b):
                dve.wait_ge(u_out, g * B + b + 2)
                dve.wait_ge(conv_in[b % 2], 16 * (g * (B // 2) + b // 2 + 1))
                dve.wait_ge(gated_stored[b % 2], 16 * (g * (B // 2) + b // 2) + 1)
                nc.vector.tensor_tensor(gated[:, b % 2, :, :], u_act[:, b % 2, :, :], conv[:, b % 2, ::-1, :],
                                        ALU.mult).then_inc(gated_done, 1)

            def group(g, r, loads, before, after):
                if after:
                    dve.wait_ge(w_in[1 - r], 32 * loads)
                for b in range(B):
                    ahead = PER * (b + 1)
                    if ahead < LOADS or after:
                        fill(g + ahead // LOADS, ahead % LOADS)
                    if after:
                        add_bias(g + 1, 1 - r, b)
                    if before:
                        gate(g - 1, b)
                    elif b % 2 == 0:
                        dve.wait_ge(split_high, b // 2 + 1)
                        if b:
                            dve.wait_ge(split_stored, 32 * (b // 2))
                        nc.vector.tensor_tensor(low.bitcast(F32R), whole, high, ALU.subtract).then_inc(split_low, 1)
                if not before:
                    dve.wait_ge(split_stored, 32 * E1)

            groups(dve, group)
            for b in range(B):
                gate(NCG - 1, b)

        @block.scalar
        def _(act):
            with act.Fori(0, B // 2) as pair:
                for r in range(2):
                    act.wait_ge(xnT_done, 2 * pair + r + 2)
                    act.sem_inc(passed, 1)
                    for k in range(KE):
                        nc.scalar.copy(xnT[:, k, bass.ds((2 * pair + r) * L, L)],
                                       bank[2 * r + k][:, :]).then_inc(xnT_out, 1)

            def activate(g, r, b):
                act.wait_ge(v_biased, g * B + b + 2)
                dst = V[r][:, :, :].rearrange("p c (i b) -> p i c b", b=B)[:, ::-1, :, b]
                nc.scalar.activation(dst, v_sum[:, b % 2, :, :], ACT.Silu).then_inc(v_out, 1)

            def fill(g, n):
                act.wait_ge(T_in[n % RING_T], loads_of(g, n))
                nc.scalar.copy(*upper(n)).then_inc(T_full[1], 1)

            fill(0, 1)
            for b in range(B):
                activate(0, 0, b)

            def gate(g, r, b):
                act.wait_ge(u_done, g * B + b + 2)
                act.wait_ge(gated_done, g * B + max(b - 1, 0) + 1)
                nc.scalar.activation(u_act[:, b % 2, :, ::-1], u_bank[b % 2][:, :].rearrange("p (i t) -> p i t", t=P),
                                     ACT.Silu, bias=u_b[:, r:r + 1]).then_inc(u_out, 1)

            def group(g, r, loads, before, after):
                if before:
                    act.wait_ge(u_in[1 - r], 32 * (loads - 1))
                if after:
                    act.wait_ge(T_used, g * LOADS + 1)
                for m in range(NM):
                    ahead = PER * (m + 1) + 1
                    if ahead < LOADS or after:
                        fill(g + ahead // LOADS, ahead % LOADS)
                    if after:
                        activate(g + 1, 1 - r, m)
                    act.wait_ge(T_used, g * LOADS + PER * (m + 1) + 1)
                    if m >= RING_C:
                        act.wait_ge(stored[m % RING_C], 16 * (g * (NM // RING_C) + m // RING_C) + 1)
                    else:
                        act.wait_ge(stored[m % RING_C], 16 * (g * (NM // RING_C)) + 1)
                    nc.scalar.copy(result[:, m % RING_C, :, :].rearrange("p q t -> p (q t)"),
                                   conv_bank[m % NV][:, :]).then_inc(conv_out, 1)
                    if before:
                        gate(g - 1, 1 - r, m)
                    elif m % 2 == 0:
                        act.wait_ge(split_in, 16 * (m // 2 + 1))
                        if m:
                            act.wait_ge(split_stored, 32 * (m // 2))
                        nc.scalar.copy(high.bitcast(F32R), whole).then_inc(split_high, 1)
                if not before:
                    act.wait_ge(split_stored, 32 * E1)

            groups(act, group)
            act.wait_ge(u_in[1], 16 * NCG)
            for b in range(B):
                gate(NCG - 1, 1, b)

        @block.tensor
        def _(pe):
            pe.wait_ge(const_in, 16)
            with pe.Fori(0, B // 2) as pair:
                for r in range(2):
                    pe.wait_ge(xn_done, (2 * pair + r + 1) * NT + 1)
                    pe.wait_ge(xnT_out, 2 * KE * pair + 1)
                    for k in range(KE):
                        for i in range(NT):
                            last = nc.tensor.transpose(bank[2 * r + k][:, i * P:(i + 1) * P],
                                                       xn[:, r, i, k * P:(k + 1) * P], ident[:, :])
                    last.then_inc(xnT_done, 1)
            pe.wait_ge(xnT_out, KE * B + 1)

            def values(g, r, b):
                pe.wait_ge(v_biased, g * B + max(b - 1, 0) + 1)
                for i in range(NT):
                    for k in range(KE):
                        last = nc.tensor.matmul(v_bank[b % 2][:, i * P:(i + 1) * P],
                                                xnT[:, k, b * L + i * P:b * L + (i + 1) * P], v_w[:, r, k, :],
                                                start=(k == 0), stop=(k == KE - 1))
                last.then_inc(v_done, 1)

            pe.wait_ge(w_in[0], 32)
            for b in range(B):
                values(0, 0, b)

            pe.wait_ge(zero_set, 1)

            def convolve(g, r, n):
                pe.wait_ge(T_full[n % 2], g * (LOADS // 2) + n // 2 + 1)
                m = n // PER
                if n % PER == 0:
                    nc.tensor.matmul(conv_bank[m % NV][:, :], zero[:, 0:P], zero[:, :], start=True, stop=False)
                for q in range(CT):
                    chan = n * CT + q
                    side, at = chan % 2 * NJ, chan % CB // 2 * P
                    for lag in reversed(range(NT)):
                        last = nc.tensor.matmul(conv_bank[m % NV][side:side + NJ - lag * B, at:at + P],
                                                V[r][:, chan, lag * B:NJ], T[:, n % RING_T, q, lag * P:(lag + 1) * P],
                                                start=False, stop=(lag == 0 and chan % CB >= CB - 2))
                last.then_inc(T_used, 1)

            def gate(g, r, b):
                pe.wait_ge(u_out, g * B + max(b - 1, 0) + 1)
                for k in range(KE):
                    last = nc.tensor.matmul(u_bank[b % 2][:, :], u_w[:, r, k, :], xnT[:, k, b * L:(b + 1) * L],
                                            start=(k == 0), stop=(k == KE - 1))
                last.then_inc(u_done, 1)

            def group(g, r, loads, before, after):
                pe.wait_ge(v_out, (g + 1) * B + 1)
                if after:
                    pe.wait_ge(w_in[1 - r], 32 * loads)
                if before:
                    pe.wait_ge(u_in[1 - r], 32 * (loads - 1))
                for m in range(NM):
                    pe.wait_ge(conv_out, g * NM + max(m - NV + 1, 0) + 1)
                    for n in range(PER * m, PER * (m + 1)):
                        convolve(g, r, n)
                    if after:
                        values(g + 1, 1 - r, m)
                    if before:
                        gate(g - 1, 1 - r, m)

            groups(pe, group)
            pe.wait_ge(u_in[1], 16 * NCG)
            for b in range(B):
                gate(NCG - 1, 1, b)


E0 = 16
H0 = 10
H0R = 8
DI = 512
NB = DI // P
N = 16
RK = 64
TAPS = 4
RING_G = 3
WEIGHT_EPS = 1e-9
A_LOG_MAX = 83.0
HALF = NB // 2


class Products:

    def __init__(self, sem, name, banks, order):
        self.ready = sem(f"{name}_ready")
        self.freed = [sem(f"{name}_freed{i}") for i in range(len(banks))]
        self.banks, self.total, uses = banks, len(order), [0] * len(banks)
        self.place = {}
        for i, key in enumerate(order):
            bank = i % len(banks)
            self.place[key] = (i, bank, uses[bank])
            uses[bank] += 1
        self.uses = uses

    def psum(self, *key):
        return self.banks[self.place[key][1]]

    def free(self, *key):
        return self.freed[self.place[key][1]]

    def before(self, seq, *key):
        _, bank, nth = self.place[key]
        return seq * self.uses[bank] + nth + 1

    def wait_read(self, engine, seq, *key):
        engine.wait_ge(self.free(*key), self.before(seq, *key) + 1)

    def done(self, seq, *key):
        return seq * self.total + self.place[key][0] + 1


class Steps:

    def __init__(self, engine, sem, per_seq, seq):
        self.engine, self.sem, self.per_seq, self.seq, self.n = engine, sem, per_seq, seq, 0

    def mark(self, instruction):
        instruction.then_inc(self.sem, 1)
        self.n += 1

    def wait(self, n=None):
        self.engine.wait_ge(self.sem, self.seq * self.per_seq + (self.n if n is None else n))

    def close(self):
        assert self.n == self.per_seq, (self.sem, self.n)


def expert_products(n):
    e = n // 2
    return [("z", e, n % 2 * 2 + i) for i in range(2) if e < E1] + [("y", e - 1, n % 2)] * (e > 0)


def mixtures_and_scan(nc, c, x_dram, gated_dram, w1_dram, out_dram):
    ctx = ExitStack()
    with ctx:
        def sb(name, shape, dt=FP32):
            return ctx.enter_context(nc.sbuf_tensor(name, shape, dt))

        def sem(name):
            return ctx.enter_context(nc.semaphore(name))

        ident = sb("ident", [P, P])
        half = sb("half", [P, NT])
        iota = sb("iota", [P, E0])
        pick32f = sb("pick32f", [96, 32])
        pick32 = sb("pick32", [96, 32], BF16)
        o_w = sb("o_w", [P, NCG, E])
        o_b = sb("o_b", [P, E])
        router_w = sb("router_w", [P, KE, E0])
        gu_w = sb("gu_w", [P, RING_G, 2, KE, P])
        down_w = sb("down_w", [P, H0, E])
        in_w = sb("in_w", [P, KE, 2 * NB, P])
        conv_w = sb("conv_w", [P, NB, TAPS])
        conv_b = sb("conv_b", [P, NB])
        x_w = sb("x_w", [P, NB, RK + 96])
        shared = sb("shared", [P, L])
        dt_w = shared[0:RK, :].rearrange("p (j n) -> p j n", n=P)
        picks = shared[64:64 + 3 * E0, :].bitcast(BF16).rearrange("p (j n) -> p j n", n=P)
        dt_b = sb("dt_b", [P, NB])
        A = sb("A", [P, NB, N])
        D = sb("D", [P, NB])
        y_w = sb("y_w", [P, NB, E])
        gate_w = sb("gate_w", [P, KE, E1])
        gate_b = sb("gate_b", [P, E1])
        b1 = sb("b1", [P, E1, H1])
        b2 = sb("b2", [E1, E])
        w1 = sb("w1", [P, 2, 2, KE, H1 * P])
        w2 = sb("w2", [P, 2, H1, E])

        def norm_buffers(name, x, xn, turned=True):
            class Norm:
                pass
            n = Norm()
            n.x, n.xn = x, xn
            n.stats = sb(f"{name}_stats", [P, NT, 6])
            n.moments = sb(f"{name}_moments", [P, NT, 2])
            n.shifted = sb(f"{name}_shifted", [P, NT])
            n.rstd = sb(f"{name}_rstd", [P, NT])
            n.xT = sb(f"{name}_xT", [P, KE, L]) if turned else None
            n.stat_done = sem(f"{name}_stat")
            n.var_done = sem(f"{name}_var")
            n.eps_added = sem(f"{name}_eps")
            n.rstd_done = sem(f"{name}_rstd_done")
            n.xn_done = sem(f"{name}_xn")
            return n

        def route_buffers(name, experts, copies):
            class Route:
                pass
            r = Route()
            r.experts = experts
            r.logits = sb(f"{name}_logits", [P, NT, experts])
            r.top = sb(f"{name}_top", [P, NT, 8])
            r.index = sb(f"{name}_index", [P, NT, 8], U32)
            r.indexf = sb(f"{name}_indexf", [P, NT, 2])
            r.gap = sb(f"{name}_gap", [P, NT, experts + 1])
            r.exp = r.gap
            r.total = sb(f"{name}_total", [P, NT, 1])
            r.weight = sb(f"{name}_weight", [P, NT, 2])
            r.one = sb(f"{name}_one", [P, NT, experts])
            r.two = sb(f"{name}_two", [P, NT, experts])
            r.comb = sb(f"{name}_comb", [P, NT, copies, experts])
            r.gap_done = sem(f"{name}_gap_done")
            r.exp_done = sem(f"{name}_exp_done")
            r.comb_done = sem(f"{name}_comb_done")
            return r

        f0_x = sb("f0_x", [P, NT, E])
        f0_h = sb("f0_h", [P, H0, L])
        f0_act = sb("f0_act", [P, 2, L])
        f0 = norm_buffers("f0", f0_x, f0_act[:, :, :].rearrange("p a (b e) -> p (a b) e", e=E))
        combT = sb("combT", [P, L])
        comb1T = combT[0:E1, :]
        parts = combT[64:64 + 3 * E0, 0:L // 2].bitcast(BF16)
        parts_rest = f0_act[64:64 + 2 * E0, 0, :]
        r0 = route_buffers("r0", E0, 3)
        m_x = sb("m_x", [P, NT, E])
        m_xc = sb("m_xc", [P, NB, TAPS - 1 + L])
        m_xs = sb("m_xs", [P, NB, L])
        m_res = sb("m_res", [P, NB, L])
        m_bc = sb("m_bc", [96, L], BF16)
        m_dt = sb("m_dt", [P, NB, L])
        m_dA = sb("m_dA", [P, NB, L])
        picks_f = m_dA[64:64 + 3 * E0, 0:2, :].rearrange("p a (b n) -> p (a b) n", n=P)
        m_dBx = sb("m_dBx", [P, NB, L])
        m_h = sb("m_h", [P, NB, L])
        m_B = sb("m_B", [P, 2, L])
        m_C = sb("m_C", [P, L])
        m_rest = m_B[0:64, 0, :]
        m_dtr = m_B[0:RK, 1, :]
        m = norm_buffers("m", f0_x, f0.xn)
        f1_x = sb("f1_x", [P, NT, E])
        f1_h = sb("f1_h", [P, 2, H1, L])
        f1_acc = sb("f1_acc", [P, NT, E])
        f1_xn = f1_h[:, 1, 0:2, :].rearrange("p a (b e) -> p (a b) e", e=E)
        f1 = norm_buffers("f1", f1_x, f1_xn, turned=False)
        f1_high = sb("f1_high", [P, KE, L], F32R)
        f1_low = sb("f1_low", [P, KE, L], F32R)
        r1 = route_buffers("r1", E1, 1)

        bank = [ctx.enter_context(nc.psum_tensor(f"bank{i}", [P, L], FP32)) for i in range(8)]
        pm = Products(sem, "pm", bank[0:2],
                      [("xc", j) for j in range(NB)] + [("res", j) for j in range(NB)]
                      + [("dtr",), ("bc",)] + [("dt", j) for j in range(NB)]
                      + [(w, n) for n in range(N) for w in ("B", "C")])
        p0 = Products(sem, "p0", bank[2:5],
                      [("o", i) for i in range(NT)] + [("xT", k) for k in range(KE)] + [("logits",), ("combT",)]
                      + [(w, j) for j in range(H0) for w in ("g", "up", "comb") if j < H0R or w != "comb"]
                      + [("down", i) for i in range(NT)] + [("mxT", k) for k in range(KE)])
        p1 = Products(sem, "p1", bank[5:8],
                      [("out", i) for i in range(NT)]
                      + [("xT", k) for k in range(KE)] + [("logits",), ("combT",)] + [("b2", i) for i in range(NT)]
                      + [key for n in range(N + 2) for key in expert_products(n)])

        entered = sem("entered")
        loaded = sem("loaded")
        half_set = sem("half_set")
        pick_set = sem("pick_set")
        pad_set = sem("pad_set")
        A_done = sem("A_done")
        passed = sem("passed")
        x_in = sem("x_in")
        gated_in = sem("gated_in")
        x_biased = sem("x_biased")
        x2_copied = sem("x2_copied")
        x2_moved = sem("x2_moved")
        comb_high = sem("comb_high")
        comb_parts = sem("comb_parts")
        f0_step = sem("f0_step")
        m_step = sem("m_step")
        f1_step = sem("f1_step")
        conv_done = sem("conv_done")
        xs_done = sem("xs_done")
        high_out = sem("high_out")
        parts_done = sem("parts_done")
        soft_in = sem("soft_in")
        soft_exp = sem("soft_exp")
        soft_log = sem("soft_log")
        soft_lin = sem("soft_lin")
        soft_low = sem("soft_low")
        dt_done = sem("dt_done")
        dA_zero = sem("dA_zero")
        dtx_done = sem("dtx_done")
        y_begun = sem("y_begun")
        dA_done = sem("dA_done")
        dBx_done = sem("dBx_done")
        scanned = sem("scanned")
        m_product = sem("m_product")
        xc_copied = sem("xc_copied")
        summed = sem("summed")
        y_done = sem("y_done")
        f1_high_out = sem("f1_high_out")
        gu_in = [sem(f"gu_in{r}") for r in range(RING_G)]
        w1_in = [sem(f"w1_in{r}") for r in range(2)]
        w2_in = [sem(f"w2_in{r}") for r in range(2)]
        stored = sem("stored")

        block = ctx.enter_context(nc.Block())

        first_consts = [(ident[:, :], c["ident"]), (o_w[:, :, :], c["o_w"]),
                        (o_b[:, :], c["o_b"].partition_broadcast(P))]
        consts = [(iota[:, :], c["iota"].partition_broadcast(P)),
                  (picks_f, c["picks"]), (pick32f[:, :], c["pick32"]),
                  (router_w[:, :, :], c["router_w"]), 
                  (down_w[:, :, :], c["down_w"]), (in_w[:, :, :, :], c["in_w"]), (conv_w[:, :, :], c["conv_w"]),
                  (conv_b[:, :], c["conv_b"]), (x_w[:, :, :], c["x_w"]), (dt_w, c["dt_w"]),
                  (dt_b[:, :], c["dt_b"]), (A[:, :, :], c["A_log"]), (D[:, :], c["D"]), (y_w[:, :, :], c["y_w"]),
                  (gate_w[:, :, :], c["gate_w"]), (gate_b[:, :], c["gate_b"].partition_broadcast(P)),
                  (b1[:, :, :], c["b1"]), (b2[:, :], c["b2"])]
        ENTERED, LOADED = 16 * len(first_consts), 16 * len(consts)
        dtx = m_xc[:, :, TAPS - 1:]

        def turns(engine, turn):
            turn(0, True, False, False, True)
            turn(1, True, True, False, True)
            with engine.Fori(2, B - 1) as t:
                turn(t, True, True, True, True)
            turn(B - 1, True, True, True, False)
            turn(B, False, True, True, False)
            turn(B + 1, False, False, True, False)

        @block.sync
        def _(sp):
            for dst, src in first_consts:
                sp.dma_start(dst, src).then_inc(entered, 16)

            def load_x(seq):
                sp.sem_inc(passed, 1)
                sp.dma_start(f0_x[:, :, :], x_dram[bass.ds(seq, 1), :, :].rearrange("o (i p) e -> p (o i) e", p=P))\
                    .then_inc(x_in, 16)

            def load_gated(seq):
                sp.sem_inc(passed, 1)
                sp.dma_start(f0_h[:, 0:NCG, :], gated_dram[:, :, bass.ds(seq, 1), :].rearrange("g p o t -> p g (o t)"))\
                    .then_inc(gated_in, 16)

            def load_w1(e):
                sp.dma_start(w1[:, e % 2, :, :, :].rearrange("p s k n -> p (s k n)"),
                             w1_dram[e, :, :, :].rearrange("p s n -> p (s n)")).then_inc(w1_in[e % 2], 16)

            def load_w2(e):
                sp.dma_start(w2[:, e % 2, :, :].rearrange("p j n -> p (j n)"), c["w12"][e, :, W1:])\
                    .then_inc(w2_in[e % 2], 16)

            def load_gate_up(j):
                sp.dma_start(gu_w[:, j % RING_G, :, :, :].rearrange("p w k n -> p (w k n)"), c["gu_w"][j])\
                    .then_inc(gu_in[j % RING_G], 16)

            load_gated(0)
            load_x(0)
            for dst, src in consts:
                sp.dma_start(dst, src).then_inc(loaded, 16)
            for j in range(RING_G):
                load_gate_up(j)
            for e in range(2):
                load_w1(e)
                load_w2(e)

            def turn(t, first, scan, second, more):
                if first:
                    for j in range(RING_G, H0):
                        sp.wait_ge(p0.ready, p0.done(t, "up", j - RING_G))
                        sp.sem_inc(passed, 1)
                        load_gate_up(j)
                if scan:
                    if second:
                        for i in range(NT):
                            p1.wait_read(sp, t - 2, "b2", i)
                            sp.sem_inc(passed, 1)
                    sp.wait_ge(x2_copied, 16 * t)
                    sp.sem_inc(passed, 1)
                    sp.dma_start(f1_x[:, :, :], m_x[:, :, :]).then_inc(x2_moved, 16)
                if more:
                    for j in range(H0 - RING_G, H0):
                        sp.wait_ge(p0.ready, p0.done(t, "up", j))
                        sp.sem_inc(passed, 1)
                        load_gate_up(j % RING_G)
                again = first or scan
                for n in range(1, N + 2):
                    e = n // 2 + 2
                    if second and n % 2 and n < N and (e < E1 or again):
                        sp.wait_ge(p1.ready, p1.done(t - 2, "z", e - 2, H1 - 1))
                        sp.sem_inc(passed, 1)
                        load_w1(e % E1)
                    e = n // 2 + 1
                    if second and n % 2 and e > 1 and (e < E1 or again):
                        sp.wait_ge(p1.ready, p1.done(t - 2, "y", e - 2, 1))
                        sp.sem_inc(passed, 1)
                        load_w2(e % E1)
                    if n == DOWN_AT[-1] and more:
                        sp.wait_ge(p0.ready, p0.done(t, "down", NT - 1))
                        load_gated(t + 1)
                    if n == DOWN_AT[-1] and first:
                        for i in range(NT):
                            p0.wait_read(sp, t, "down", i)
                            sp.sem_inc(passed, 1)
                        if scan:
                            sp.wait_ge(x2_moved, 16 * t)
                            sp.sem_inc(passed, 1)
                        sp.dma_start(m_x[:, :, :], f0_x[:, :, :]).then_inc(x2_copied, 16)
                    if n == M_STATS_AT + 1 and more:
                        sp.wait_ge(x2_copied, 16 * (t + 1))
                        sp.sem_inc(passed, 1)
                        sp.wait_ge(m.xn_done, NT * (t + 1))
                        load_x(t + 1)
                if second:
                    for half in range(2):
                        p1.wait_read(sp, t - 2, "y", E1 - 1, half)
                        sp.sem_inc(passed, 1)
                    sp.dma_start(out_dram[bass.ds(t - 2, 1), :, :].rearrange("o (i p) e -> p (o i) e", p=P),
                                 f1_acc[:, :, :]).then_inc(stored, 16)

            turns(sp, turn)
            sp.wait_ge(stored, 16 * B + 1)

        @block.gpsimd
        def _(pool):
            nc.gpsimd.memset(half[:, :], -0.5).then_inc(half_set, 1)
            nc.gpsimd.memset(m_xc[:, :, 0:TAPS - 1], 0.0).then_inc(pad_set, 1)
            pool.wait_ge(half_set, 1)
            pool.wait_ge(entered, ENTERED)

            def rstd(n, seq):
                pool.wait_ge(n.var_done, (seq + 1) * NT)
                pool.sem_inc(passed, 1)
                nc.gpsimd.tensor_scalar(n.shifted[:, :], n.moments[:, :, 1], LN_EPS, None, ALU.add)\
                    .then_inc(n.eps_added, 1)
                pool.wait_ge(n.eps_added, seq + 1)
                nc.gpsimd.tensor_tensor(n.rstd[:, :], n.shifted[:, :], half[:, :], ALU.pow)\
                    .then_inc(n.rstd_done, 1)

            def bias_x(seq):
                pool.wait_ge(x_in, 16 * (seq + 1))
                nc.gpsimd.tensor_tensor(f0_x[:, :, :], f0_x[:, :, :],
                                        o_b[:, :].unsqueeze(1).to_broadcast([P, NT, E]), ALU.add)\
                    .then_inc(x_biased, 1)

            def softplus(seq):
                for j in range(NB):
                    pool.wait_ge(soft_exp, seq * NB + j + 1)
                    pool.sem_inc(passed, 1)
                    nc.gpsimd.tensor_scalar(m_dBx[:, j, :], m_dA[:, j, :], -0.5, 1.0, ALU.mult, ALU.add)\
                        .then_inc(soft_lin, 1)
                    pool.wait_ge(soft_lin, seq * NB + j + 1)
                    nc.gpsimd.tensor_tensor(m_dBx[:, j, :], m_dBx[:, j, :], m_dA[:, j, :], ALU.mult)\
                        .then_inc(soft_low, 1)
                pool.wait_ge(soft_log, (seq + 1) * NB)
                pool.wait_ge(soft_low, (seq + 1) * NB)
                pool.sem_inc(passed, 1)
                nc.gpsimd.memset(m_dA[:, :, 0:1], 0.0).then_inc(dA_zero, 1)
                pool.wait_ge(dt_done, seq + 1)
                nc.gpsimd.tensor_tensor(dtx, m_dt[:, :, :], m_xs[:, :, :], ALU.mult).then_inc(dtx_done, 1)

            def inputs(seq, n):
                for q in range(2):
                    if q == 0:
                        pm.wait_read(pool, seq, "B", n)
                        if n == 0:
                            pool.wait_ge(dtx_done, seq + 1)
                    if n:
                        pool.wait_ge(scanned, (seq * N + n - 1) * 2 + q + 1)
                    part = slice(q * HALF, (q + 1) * HALF)
                    nc.gpsimd.tensor_tensor(m_dBx[:, part, :], dtx[:, part, :],
                                            m_B[:, n % 2, :].unsqueeze(1).to_broadcast([P, HALF, L]), ALU.mult)\
                        .then_inc(dBx_done, 1)

            def gate(seq):
                for q in range(2):
                    pool.wait_ge(summed, (seq * N + N - 1) * 2 + q + 1)
                    if q == 0:
                        for j in range(NB):
                            pm.wait_read(pool, seq, "res", j)
                    part = slice(q * HALF, (q + 1) * HALF)
                    nc.gpsimd.tensor_tensor(m_xs[:, part, :], m_xs[:, part, :], m_res[:, part, :], ALU.mult)\
                        .then_inc(y_done, 1)

            bias_x(0)
            rstd(f0, 0)

            def turn(t, first, scan, second, more):
                if second:
                    rstd(f1, t - 2)
                if scan:
                    softplus(t - 1)
                for n in range(N):
                    if scan:
                        inputs(t - 1, n)
                    if first and n == M_STATS_AT + 1:
                        rstd(m, t)
                    if more and n == OUTPUTS_AT[0]:
                        bias_x(t + 1)
                    if more and n == X_STATS_AT + 1:
                        rstd(f0, t + 1)
                if scan:
                    gate(t - 1)

            turns(pool, turn)

        @block.vector
        def _(dve):
            for p in (pm, p0, p1):
                for s in p.freed:
                    dve.sem_inc(s, 1)
            dve.sem_inc(stored, 1)
            def statistics(n, seq):
                for i in range(NT):
                    nc.vector.bn_stats(n.stats[:, i, :], n.x[:, i, :]).then_inc(n.stat_done, 1)
                dve.wait_ge(n.stat_done, (seq + 1) * NT)
                dve.sem_inc(passed, 1)
                for i in range(NT):
                    nc.vector.bn_aggr(n.moments[:, i, :], n.stats[:, i, :]).then_inc(n.var_done, 1)

            def normalise(n, seq):
                dve.wait_ge(n.rstd_done, seq + 1)
                dve.wait_ge(n.var_done, (seq + 1) * NT)
                for i in range(NT):
                    nc.vector.tensor_scalar(n.xn[:, i, :], n.x[:, i, :], n.moments[:, i, 0:1], n.rstd[:, i:i + 1],
                                            ALU.subtract, ALU.mult).then_inc(n.xn_done, 1)

            def rank(r, p, seq, s):
                n = r.experts
                dve.wait_ge(p.ready, p.done(seq, "logits"))
                psum = p.psum("logits")[:, 0:NT * n].rearrange("p (i n) -> p i n", n=n)
                if r is r1:
                    nc.vector.tensor_tensor(r.logits[:, :, :], psum,
                                            gate_b[:, :].unsqueeze(1).to_broadcast([P, NT, n]), ALU.add)\
                        .then_inc(p.free("logits"), 1)
                else:
                    nc.vector.tensor_copy(r.logits[:, :, :], psum).then_inc(p.free("logits"), 1)
                p.wait_read(dve, seq, "logits")
                dve.sem_inc(passed, 1)
                for i in range(NT):
                    s.mark(nc.vector.max(r.top[:, i, :], r.logits[:, i, :]))
                s.wait()
                dve.sem_inc(passed, 1)
                for i in range(NT):
                    s.mark(nc.vector.max_index(r.index[:, i, :], r.top[:, i, :], r.logits[:, i, :]))
                s.mark(nc.vector.tensor_tensor(r.gap[:, :, 0:n], r.logits[:, :, :],
                                               r.top[:, :, 0:1].to_broadcast([P, NT, n]), ALU.subtract))
                nc.vector.tensor_tensor(r.gap[:, :, n:n + 1], r.top[:, :, 1:2], r.top[:, :, 0:1], ALU.subtract)\
                    .then_inc(r.gap_done, 1)
                s.wait()
                s.mark(nc.vector.tensor_copy(r.indexf[:, :, :], r.index[:, :, 0:2]))

            def weigh(r, seq, s):
                n = r.experts
                shape = [P, NT, n]
                second = r.exp[:, :, n:n + 1]
                dve.wait_ge(r.exp_done, seq + 1)
                if r is r0:
                    s.mark(nc.vector.tensor_reduce(r.total[:, :, :], r.exp[:, :, 0:n], AX.X, ALU.add))
                    s.wait()
                    s.mark(nc.vector.tensor_scalar(r.total[:, :, :], r.total[:, :, :], WEIGHT_EPS, 1.0,
                                                   ALU.mult, ALU.add))
                    s.wait()
                    s.mark(nc.vector.tensor_tensor(r.total[:, :, :], r.total[:, :, :], second, ALU.add))
                else:
                    s.mark(nc.vector.tensor_scalar(r.total[:, :, :], second, 1.0, None, ALU.add))
                s.wait()
                s.mark(nc.vector.reciprocal(r.weight[:, :, 0:1], r.total[:, :, :]))
                s.wait()
                s.mark(nc.vector.tensor_tensor(r.weight[:, :, 1:2], r.weight[:, :, 0:1], second, ALU.mult))
                for k, one in enumerate((r.one, r.two)):
                    s.mark(nc.vector.tensor_tensor(one[:, :, :], iota[:, 0:n].unsqueeze(1).to_broadcast(shape),
                                                   r.indexf[:, :, k:k + 1].to_broadcast(shape), ALU.is_equal))
                s.wait()
                for k, one in enumerate((r.one, r.two)):
                    s.mark(nc.vector.tensor_tensor(one[:, :, :], one[:, :, :],
                                                   r.weight[:, :, k:k + 1].to_broadcast(shape), ALU.mult))
                s.wait()
                copies = r.comb.shape[2]
                nc.vector.tensor_tensor(r.comb[:, :, :, :],
                                        r.one[:, :, :].unsqueeze(2).to_broadcast([P, NT, copies, n]),
                                        r.two[:, :, :].unsqueeze(2).to_broadcast([P, NT, copies, n]), ALU.add)\
                    .then_inc(r.comb_done, 1)

            def split_comb(seq, s):
                dve.wait_ge(comb_high, seq + 1)
                nc.vector.tensor_tensor(parts_rest, p0.psum("combT")[0:2 * E0, :], parts[0:2 * E0, :],
                                        ALU.subtract).then_inc(p0.free("combT"), 1)
                p0.wait_read(dve, seq, "combT")
                s.mark(nc.vector.tensor_copy(parts[0:2 * E0, :], parts_rest))
                s.wait()
                nc.vector.tensor_tensor(parts[0:E0, :], parts_rest[0:E0, :], parts[0:E0, :], ALU.subtract)\
                    .then_inc(comb_parts, 1)

            def add_o(seq, i):
                if i == 0:
                    dve.wait_ge(x_biased, seq + 1)
                dve.wait_ge(p0.ready, p0.done(seq, "o", i))
                nc.vector.tensor_tensor(f0_x[:, i, :], p0.psum("o", i)[:, 0:E], f0_x[:, i, :], ALU.add)\
                    .then_inc(p0.free("o", i), 1)

            def enter_statistics(seq):
                for i in range(NT):
                    p0.wait_read(dve, seq, "o", i)
                statistics(f0, seq)

            def leave_statistics(seq):
                for i in range(NT):
                    p0.wait_read(dve, seq, "down", i)
                statistics(m, seq)

            def leave_normalise(seq):
                for j in (H0 - 2, H0 - 1):
                    p0.wait_read(dve, seq, "up", j)
                normalise(m, seq)

            def hide(seq, j):
                p0.wait_read(dve, seq, "g", j)
                dve.wait_ge(p0.ready, p0.done(seq, "up", j))
                nc.vector.tensor_tensor(f0_h[:, j, :], f0_act[:, j % 2, :], p0.psum("up", j)[:, :], ALU.mult)\
                    .then_inc(p0.free("up", j), 1)
                if j < H0R:
                    p0.wait_read(dve, seq, "up", j)
                    dve.wait_ge(p0.ready, p0.done(seq, "comb", j))
                    nc.vector.tensor_tensor(f0_h[:, j, :], f0_h[:, j, :], p0.psum("comb", j)[:, :], ALU.mult)\
                        .then_inc(p0.free("comb", j), 1)

            def add_down(seq, i):
                dve.wait_ge(p0.ready, p0.done(seq, "down", i))
                nc.vector.tensor_tensor(f0_x[:, i, :], p0.psum("down", i)[:, 0:E], f0_x[:, i, :], ALU.add)\
                    .then_inc(p0.free("down", i), 1)

            def convolve(seq, s):
                for tap in range(TAPS - 1):
                    for j in range(NB):
                        if tap == 0:
                            dve.wait_ge(xc_copied, seq * NB + j + 1)
                            pm.wait_read(dve, seq, "xc", j)
                        else:
                            s.wait((tap - 1) * NB + j + 1)
                        step = nc.vector.scalar_tensor_tensor(m_xs[:, j, :], m_xc[:, j, tap:tap + L],
                                                              conv_w[:, j, tap:tap + 1], m_xs[:, j, :],
                                                              ALU.mult, ALU.add)
                        if tap < TAPS - 2:
                            s.mark(step)
                        else:
                            step.then_inc(conv_done, 1)

            def split(seq, s):
                dve.wait_ge(high_out, seq + 1)
                nc.vector.tensor_tensor(m_rest[:, :], pm.psum("bc")[0:64, :], m_bc[0:64, :], ALU.subtract)\
                    .then_inc(pm.free("bc"), 1)
                pm.wait_read(dve, seq, "bc")
                s.mark(nc.vector.tensor_copy(m_bc[0:64, :], m_rest[:, :]))
                s.wait()
                nc.vector.tensor_tensor(m_bc[0:32, :], m_rest[0:32, :], m_bc[0:32, :], ALU.subtract)\
                    .then_inc(parts_done, 1)

            def step_sizes(seq, s):
                dve.wait_ge(soft_log, (seq + 1) * NB)
                dve.wait_ge(soft_low, (seq + 1) * NB)
                s.mark(nc.vector.tensor_tensor(m_h[:, :, :], m_h[:, :, :], m_dBx[:, :, :], ALU.max))
                s.wait()
                nc.vector.tensor_tensor(m_dt[:, :, :], m_dt[:, :, :], m_h[:, :, :], ALU.add).then_inc(dt_done, 1)

            def scan_state(seq, n, between):
                at = (seq * N + n) * 2
                rows = [slice(q * HALF, (q + 1) * HALF) for q in range(2)]
                for q in range(2):
                    dve.wait_ge(dA_done, at + q + 1)
                    dve.wait_ge(dBx_done, at + q + 1)
                    if n:
                        dve.wait_ge(summed, at - 1 + q)
                    h, a, b = (v[:, rows[q], :].rearrange("p j t -> p (j t)") for v in (m_h, m_dA, m_dBx))
                    nc.vector.tensor_tensor_scan(h, a, b, 0.0, ALU.mult, ALU.add).then_inc(scanned, 1)
                    between(q)
                pm.wait_read(dve, seq, "C", n)
                for q in range(2):
                    dve.wait_ge(scanned, at + q + 1)
                    state_c = m_C[:, :].unsqueeze(1).to_broadcast([P, HALF, L])
                    nc.vector.tensor_tensor(m_h[:, rows[q], :], m_h[:, rows[q], :], state_c, ALU.mult)\
                        .then_inc(m_product, 1)
                    between(2 + q)
                if n == 0:
                    dve.wait_ge(y_begun, (seq + 1) * NB)
                for q in range(2):
                    dve.wait_ge(m_product, at + q + 1)
                    if n:
                        dve.wait_ge(summed, at - 1 + q)
                    nc.vector.tensor_tensor(m_xs[:, rows[q], :], m_xs[:, rows[q], :], m_h[:, rows[q], :], ALU.add)\
                        .then_inc(summed, 1)

            def add_scan(seq):
                dve.wait_ge(x2_moved, 16 * (seq + 1))
                for i in range(NT):
                    dve.wait_ge(p1.ready, p1.done(seq, "out", i))
                    nc.vector.tensor_tensor(f1_x[:, i, :], p1.psum("out", i)[:, 0:E], f1_x[:, i, :], ALU.add)\
                        .then_inc(p1.free("out", i), 1)
                for i in range(NT):
                    p1.wait_read(dve, seq, "out", i)

            def split_xT(seq):
                for k in range(KE):
                    dve.wait_ge(f1_high_out, seq * KE + k + 1)
                    nc.vector.tensor_tensor(f1_low[:, k, :], p1.psum("xT", k)[:, :],
                                            f1_high[:, k, :].bitcast(FP32), ALU.subtract)\
                        .then_inc(p1.free("xT", k), 1)

            def begin_acc(seq):
                dve.wait_ge(stored, 16 * seq + 1)
                for i in range(NT):
                    dve.wait_ge(p1.ready, p1.done(seq, "b2", i))
                    nc.vector.tensor_tensor(f1_acc[:, i, :], p1.psum("b2", i)[:, 0:E], f1_x[:, i, :], ALU.add)\
                        .then_inc(p1.free("b2", i), 1)

            def add_expert(seq, e, i):
                dve.wait_ge(p1.ready, p1.done(seq, "y", e, i // 2))
                if e:
                    p1.wait_read(dve, seq, "y", e - 1, i // 2)
                else:
                    p1.wait_read(dve, seq, "b2", i)
                add = nc.vector.scalar_tensor_tensor(f1_acc[:, i, :], p1.psum("y", e, i // 2)[:, i % 2 * E:(i % 2 + 1) * E],
                                                     r1.comb[:, i, 0, e:e + 1], f1_acc[:, i, :], ALU.mult, ALU.add)
                if i % 2:
                    add.then_inc(p1.free("y", e, i // 2), 1)

            for i in range(NT):
                add_o(0, i)
            enter_statistics(0)
            normalise(f0, 0)
            dve.wait_ge(loaded, LOADED)
            nc.vector.tensor_copy(pick32[:, :], pick32f[:, :]).then_inc(pick_set, 1)
            nc.vector.tensor_copy(picks, picks_f).then_inc(pick_set, 1)
            nc.vector.tensor_scalar(A[:, :, :], A[:, :, :], A_LOG_MAX, None, ALU.min).then_inc(A_done, 1)
            dve.wait_ge(A_done, 2)
            nc.vector.tensor_scalar(A[:, :, :], A[:, :, :], -1.0, None, ALU.mult).then_inc(A_done, 1)

            s = Steps(dve, f0_step, STEPS_F0, 0)
            rank(r0, p0, 0, s)
            weigh(r0, 0, s)
            split_comb(0, s)
            s.close()

            def turn(t, first, scan, second, more):
                s0 = Steps(dve, f0_step, STEPS_F0, t + 1)
                sm = Steps(dve, m_step, STEPS_M, t - 1)
                s1 = Steps(dve, f1_step, STEPS_F1, t - 2)

                def hides(start, end):
                    if first:
                        for j in range(start, end):
                            hide(t, j)

                hides(0, 2)
                if second:
                    add_scan(t - 2)
                    statistics(f1, t - 2)
                if scan:
                    convolve(t - 1, sm)
                if second:
                    normalise(f1, t - 2)
                hides(2, 4)
                if second:
                    split_xT(t - 2)
                if scan:
                    split(t - 1, sm)
                if second:
                    rank(r1, p1, t - 2, s1)
                hides(4, 5)
                if second:
                    weigh(r1, t - 2, s1)
                    begin_acc(t - 2)
                if scan:
                    step_sizes(t - 1, sm)
                hides(5, H0)
                for n in range(N):
                    def between(q):
                        if second and q >= 2 and n >= 2:
                            add_expert(t - 2, n // 2 - 1, n % 2 * 2 + q - 2)
                        if first:
                            if n in DOWN_AT and q == 3:
                                add_down(t, DOWN_AT.index(n))
                            if n == M_STATS_AT and q == 0:
                                leave_statistics(t)
                            if n == M_STATS_AT + 1 and q == 2:
                                leave_normalise(t)
                        if more:
                            if n in OUTPUTS_AT and q == 3:
                                for i in range(NT):
                                    if OUTPUTS_AT[i] == n:
                                        add_o(t + 1, i)
                            if n == X_STATS_AT and q == 0:
                                enter_statistics(t + 1)
                            if n == X_STATS_AT + 1 and q == 2:
                                dve.wait_ge(p0.ready, p0.done(t, "mxT", KE - 1))
                                normalise(f0, t + 1)
                            if n == RANK_AT and q == 3:
                                rank(r0, p0, t + 1, s0)
                            if n == RANK_AT + 1 and q == 3:
                                weigh(r0, t + 1, s0)
                    if scan:
                        scan_state(t - 1, n, between)
                    else:
                        for q in range(NT):
                            between(q)
                if second:
                    for i in range(NT):
                        add_expert(t - 2, E1 - 1, i)
                if more:
                    split_comb(t + 1, s0)
                    s0.close()
                if scan:
                    sm.close()
                if second:
                    s1.close()

            turns(dve, turn)

        @block.scalar
        def _(act):
            act.wait_ge(A_done, 1)
            nc.scalar.activation(A[:, :, :], A[:, :, :], ACT.Exp).then_inc(A_done, 1)
            act.wait_ge(A_done, 3)
            act.wait_ge(pad_set, 1)

            def copy_xT(n, p, seq, name):
                for k in range(KE):
                    act.wait_ge(p.ready, p.done(seq, name, k))
                    nc.scalar.copy(n.xT[:, k, :], p.psum(name, k)[:, :]).then_inc(p.free(name, k), 1)

            def copy_xc(seq, j, after):
                act.wait_ge(pm.ready, pm.done(seq, "xc", j))
                if after and j == 0:
                    act.wait_ge(dBx_done, seq * N * 2)
                psum = pm.psum("xc", j)[:, :]
                nc.scalar.copy(m_xc[:, j, TAPS - 1:], psum).then_inc(xc_copied, 1)
                if after and j == 0:
                    act.wait_ge(p1.ready, p1.done(seq - 1, "out", NT - 1))
                nc.scalar.activation(m_xs[:, j, :], psum, ACT.Identity, bias=conv_b[:, j:j + 1],
                                     scale=conv_w[:, j, TAPS - 1:TAPS]).then_inc(pm.free("xc", j), 1)

            def gate(seq, j):
                act.wait_ge(pm.ready, pm.done(seq, "res", j))
                nc.scalar.activation(m_res[:, j, :], pm.psum("res", j)[:, :], ACT.Silu)\
                    .then_inc(pm.free("res", j), 1)

            def activate_conv(seq, j):
                act.wait_ge(conv_done, seq * NB + j + 1)
                nc.scalar.activation(m_xs[:, j, :], m_xs[:, j, :], ACT.Silu).then_inc(xs_done, 1)

            def exp_gap(r, seq):
                act.wait_ge(r.gap_done, seq + 1)
                nc.scalar.activation(r.exp[:, :, :], r.gap[:, :, :], ACT.Exp).then_inc(r.exp_done, 1)

            def copy_comb1T(seq):
                act.wait_ge(p1.ready, p1.done(seq, "combT"))
                nc.scalar.copy(comb1T, p1.psum("combT")[0:E1, :]).then_inc(p1.free("combT"), 1)

            def round_comb0T(seq):
                act.wait_ge(p0.ready, p0.done(seq, "combT"))
                nc.scalar.copy(parts, p0.psum("combT")[0:3 * E0, :]).then_inc(comb_high, 1)

            def low_rank(seq):
                act.wait_ge(pm.ready, pm.done(seq, "dtr"))
                nc.scalar.copy(m_dtr[:, :], pm.psum("dtr")[0:RK, :]).then_inc(pm.free("dtr"), 1)
                act.wait_ge(pm.ready, pm.done(seq, "bc"))
                nc.scalar.copy(m_bc[:, :], pm.psum("bc")[0:96, :]).then_inc(high_out, 1)

            def softplus_in(seq):
                for j in range(NB):
                    act.wait_ge(pm.ready, pm.done(seq, "dt", j))
                    psum = pm.psum("dt", j)[:, :]
                    nc.scalar.activation(m_dA[:, j, :], psum, ACT.Abs, bias=dt_b[:, j:j + 1]).then_inc(soft_in, 1)
                    nc.scalar.activation(m_dt[:, j, :], psum, ACT.Relu, bias=dt_b[:, j:j + 1])\
                        .then_inc(pm.free("dt", j), 1)

            def softplus(seq):
                for j in range(NB):
                    act.wait_ge(soft_in, seq * NB + j + 1)
                    nc.scalar.activation(m_dA[:, j, :], m_dA[:, j, :], ACT.Exp, scale=-1.0).then_inc(soft_exp, 1)
                for j in range(NB):
                    act.wait_ge(soft_exp, seq * NB + j + 1)
                    nc.scalar.activation(m_h[:, j, :], m_dA[:, j, :], ACT.Ln, bias=1.0).then_inc(soft_log, 1)

            def begin_y(seq):
                act.wait_ge(dtx_done, seq + 1)
                for j in range(NB):
                    nc.scalar.activation(m_xs[:, j, :], m_xs[:, j, :], ACT.Identity, scale=D[:, j:j + 1])\
                        .then_inc(y_begun, 1)

            def copy_B(seq, n):
                act.wait_ge(pm.ready, pm.done(seq, "B", n))
                if n >= 2:
                    act.wait_ge(dBx_done, (seq * N + n - 1) * 2)
                nc.scalar.copy(m_B[:, n % 2, :], pm.psum("B", n)[:, :]).then_inc(pm.free("B", n), 1)

            def copy_C(seq, n):
                act.wait_ge(pm.ready, pm.done(seq, "C", n))
                if n:
                    act.wait_ge(m_product, (seq * N + n) * 2)
                nc.scalar.copy(m_C[:, :], pm.psum("C", n)[:, :]).then_inc(pm.free("C", n), 1)

            def decays(seq, n, q):
                if n:
                    act.wait_ge(scanned, (seq * N + n - 1) * 2 + q + 1)
                elif q == 0:
                    act.wait_ge(dA_zero, seq + 1)
                    act.wait_ge(dt_done, seq + 1)
                for j in range(q * HALF, (q + 1) * HALF):
                    last = nc.scalar.activation(m_dA[:, j, 1:], m_dt[:, j, 1:], ACT.Exp, scale=A[:, j, n:n + 1])
                last.then_inc(dA_done, 1)

            def round_xT(seq):
                for k in range(KE):
                    act.wait_ge(p1.ready, p1.done(seq, "xT", k))
                    nc.scalar.copy(f1_high[:, k, :], p1.psum("xT", k)[:, :]).then_inc(f1_high_out, 1)

            def relu(seq, e, j):
                act.wait_ge(p1.ready, p1.done(seq, "z", e, j))
                nc.scalar.activation(f1_h[:, e % 2, j, :], p1.psum("z", e, j)[:, :], ACT.Relu, bias=b1[:, e, j:j + 1])\
                    .then_inc(p1.free("z", e, j), 1)

            def silu(seq, j):
                act.wait_ge(p0.ready, p0.done(seq, "g", j))
                if j >= 2:
                    p0.wait_read(act, seq, "up", j - 2)
                elif j == 0:
                    act.wait_ge(comb_parts, seq + 1)
                nc.scalar.activation(f0_act[:, j % 2, :], p0.psum("g", j)[:, :], ACT.Silu)\
                    .then_inc(p0.free("g", j), 1)

            copy_xT(f0, p0, 0, "xT")
            exp_gap(r0, 0)
            round_comb0T(0)

            def turn(t, first, scan, second, more):
                def silus(start, end):
                    if first:
                        for j in range(start, end):
                            silu(t, j)

                silus(0, 2)
                if scan:
                    for j in range(NB):
                        copy_xc(t - 1, j, second)
                    for j in range(NB):
                        gate(t - 1, j)
                silus(2, 3)
                if scan:
                    for j in range(NB):
                        activate_conv(t - 1, j)
                silus(3, 4)
                if second:
                    round_xT(t - 2)
                if scan:
                    low_rank(t - 1)
                silus(4, 5)
                if second:
                    exp_gap(r1, t - 2)
                if scan:
                    softplus_in(t - 1)
                if second:
                    copy_comb1T(t - 2)
                if scan:
                    softplus(t - 1)
                silus(5, H0)
                if scan:
                    copy_B(t - 1, 0)
                    for q in range(2):
                        decays(t - 1, 0, q)
                    copy_C(t - 1, 0)
                    begin_y(t - 1)
                for n in range(N):
                    if scan and n + 1 < N:
                        copy_B(t - 1, n + 1)
                        decays(t - 1, n + 1, 0)
                    if second:
                        relu(t - 2, n // 2, n % 2 * 2)
                    if scan and n + 1 < N:
                        decays(t - 1, n + 1, 1)
                    if second:
                        relu(t - 2, n // 2, n % 2 * 2 + 1)
                    if scan and n + 1 < N:
                        copy_C(t - 1, n + 1)
                    if first and n == M_TRANSPOSE_AT:
                        copy_xT(m, p0, t, "mxT")
                    if more and n == X_TRANSPOSE_AT:
                        copy_xT(f0, p0, t + 1, "xT")
                    if more and n == RANK_AT + 1:
                        exp_gap(r0, t + 1)
                if more:
                    round_comb0T(t + 1)

            turns(act, turn)

        @block.tensor
        def _(pe):
            def transpose_x(n, p, seq, name):
                pe.wait_ge(n.xn_done, (seq + 1) * NT)
                for k in range(KE):
                    pe.wait_ge(p.free(name, k), p.before(seq, name, k))
                    for i in range(NT):
                        last = nc.tensor.transpose(p.psum(name, k)[:, i * P:(i + 1) * P],
                                                   n.xn[:, i, k * P:(k + 1) * P], ident[:, :])
                    last.then_inc(p.ready, 1)

            def product(p, seq, key, out, pairs):
                pe.wait_ge(p.free(*key), p.before(seq, *key))
                for k, (weights, moving) in enumerate(pairs):
                    last = nc.tensor.matmul(out, weights, moving, start=(k == 0), stop=(k == len(pairs) - 1))
                last.then_inc(p.ready, 1)

            def logits(n, p, seq, weights, experts):
                for k in range(KE):
                    p.wait_read(pe, seq, "xT", k)
                pe.wait_ge(p.free("logits"), p.before(seq, "logits"))
                xTs = (n.xT,) if n is not f1 else (f1_high[:, :, :].bitcast(FP32), f1_low[:, :, :].bitcast(FP32))
                pairs = [(xT, k) for xT in xTs for k in range(KE)]
                for i in range(NT):
                    for at, (xT, k) in enumerate(pairs):
                        last = nc.tensor.matmul(p.psum("logits")[:, i * experts:(i + 1) * experts],
                                                xT[:, k, i * P:(i + 1) * P], weights[:, k, :],
                                                start=(at == 0), stop=(at == len(pairs) - 1))
                last.then_inc(p.ready, 1)

            def transpose_comb(r, p, seq):
                pe.wait_ge(r.comb_done, seq + 1)
                pe.wait_ge(p.free("combT"), p.before(seq, "combT"))
                for i in range(NT):
                    comb = r.comb[:, i, :, :].rearrange("p a n -> p (a n)")
                    last = nc.tensor.matmul(p.psum("combT")[0:comb.shape[1], i * P:(i + 1) * P], comb,
                                            ident[:, :], start=True, stop=True)
                last.then_inc(p.ready, 1)

            def outputs(seq, tiles):
                pe.wait_ge(gated_in, 16 * (seq + 1))
                for i in tiles:
                    product(p0, seq, ("o", i), p0.psum("o", i)[:, 0:E],
                            [(f0_h[:, k, i * P:(i + 1) * P], o_w[:, k, :]) for k in range(NCG)])

            def gate_up(seq, j):
                r = j % RING_G
                loads = len(range(r, H0, RING_G))
                pe.wait_ge(gu_in[r], (seq * loads + j // RING_G + 1) * 16)
                for w, name in enumerate(("g", "up")):
                    product(p0, seq, (name, j), p0.psum(name, j)[:, :],
                            [(gu_w[:, r, w, k, :], f0.xT[:, k, :]) for k in range(KE)])
                if j < H0R:
                    if j == 0:
                        pe.wait_ge(comb_parts, seq + 1)
                    product(p0, seq, ("comb", j), p0.psum("comb", j)[:, :], [(picks[:, j, :], parts)])

            def down(seq, i):
                for key in (("comb", H0R - 1), ("up", H0 - 2), ("up", H0 - 1)):
                    p0.wait_read(pe, seq, *key)
                product(p0, seq, ("down", i), p0.psum("down", i)[:, 0:E],
                        [(f0_h[:, j, i * P:(i + 1) * P], down_w[:, j, :]) for j in range(H0)])

            def enter(seq, name, at, tiles):
                for j in tiles:
                    product(pm, seq, (name, j), pm.psum(name, j)[:, :],
                            [(in_w[:, k, at + j, :], m.xT[:, k, :]) for k in range(KE)])

            def low_rank(seq):
                pe.wait_ge(xs_done, (seq + 1) * NB)
                product(pm, seq, ("dtr",), pm.psum("dtr")[0:RK, :],
                        [(x_w[:, j, 0:RK], m_xs[:, j, :]) for j in range(NB)])
                product(pm, seq, ("bc",), pm.psum("bc")[0:96, :],
                        [(x_w[:, j, RK:], m_xs[:, j, :]) for j in range(NB)])

            def step_sizes(seq):
                pm.wait_read(pe, seq, "dtr")
                for j in range(NB):
                    product(pm, seq, ("dt", j), pm.psum("dt", j)[:, :], [(dt_w[:, j, :], m_dtr[:, :])])

            def spread(seq, name, n):
                row = n if name == "B" else N + n
                product(pm, seq, (name, n), pm.psum(name, n)[:, :],
                        [(pick32[:, row:row + 1].to_broadcast([96, P]), m_bc[:, :])])

            def leave(seq):
                pe.wait_ge(y_done, 2 * (seq + 1))
                for i in range(NT):
                    product(p1, seq, ("out", i), p1.psum("out", i)[:, 0:E],
                            [(m_xs[:, j, i * P:(i + 1) * P], y_w[:, j, :]) for j in range(NB)])

            def bias2(seq):
                p1.wait_read(pe, seq, "combT")
                for i in range(NT):
                    product(p1, seq, ("b2", i), p1.psum("b2", i)[:, 0:E],
                            [(comb1T[:, i * P:(i + 1) * P], b2[:, :])])

            def expert(seq, n):
                for key in expert_products(n):
                    w, e, i = key
                    if w == "z":
                        if i == 0:
                            pe.wait_ge(w1_in[e % 2], (seq * (E1 // 2) + e // 2 + 1) * 16)
                        pairs = [(w1[:, e % 2, side, k, i * P:(i + 1) * P].bitcast(F32R), xT[:, k, :])
                                 for k in range(KE) for side, xT in ((0, f1_high), (0, f1_low), (1, f1_high))]
                        product(p1, seq, key, p1.psum(*key)[:, :], pairs)
                    else:
                        if i == 0:
                            pe.wait_ge(w2_in[e % 2], (seq * (E1 // 2) + e // 2 + 1) * 16)
                            for j in (H1 - 2, H1 - 1):
                                p1.wait_read(pe, seq, "z", e, j)
                            pe.sem_inc(passed, 1)
                        pe.wait_ge(p1.free(*key), p1.before(seq, *key))
                        for half in range(2):
                            tile = 2 * i + half
                            for j in range(H1):
                                last = nc.tensor.matmul(p1.psum(*key)[:, half * E:(half + 1) * E],
                                                        f1_h[:, e % 2, j, tile * P:(tile + 1) * P],
                                                        w2[:, e % 2, j, :], start=(j == 0), stop=(j == H1 - 1))
                        last.then_inc(p1.ready, 1)

            pe.wait_ge(entered, ENTERED)
            outputs(0, range(NT))
            transpose_x(f0, p0, 0, "xT")
            pe.wait_ge(loaded, LOADED)
            pe.wait_ge(pick_set, 2)
            logits(f0, p0, 0, router_w, E0)
            transpose_comb(r0, p0, 0)

            def turn(t, first, scan, second, more):
                def gates_up(start, end):
                    if first:
                        for j in range(start, end):
                            gate_up(t, j)

                if scan:
                    for k in range(KE):
                        p0.wait_read(pe, t - 1, "mxT", k)
                    enter(t - 1, "xc", 0, (0, 1))
                gates_up(0, 2)
                if second:
                    leave(t - 2)
                if scan:
                    enter(t - 1, "xc", 0, (2, 3))
                    enter(t - 1, "res", NB, range(NB))
                gates_up(2, 4)
                if second:
                    transpose_x(f1, p1, t - 2, "xT")
                if scan:
                    low_rank(t - 1)
                if second:
                    logits(f1, p1, t - 2, gate_w, E1)
                gates_up(4, 5)
                if scan:
                    step_sizes(t - 1)
                if second:
                    transpose_comb(r1, p1, t - 2)
                    bias2(t - 2)
                    expert(t - 2, 0)
                gates_up(5, H0)
                if scan:
                    pe.wait_ge(parts_done, t)
                    spread(t - 1, "B", 0)
                    spread(t - 1, "C", 0)
                for n in range(N):
                    if scan and n + 1 < N:
                        spread(t - 1, "B", n + 1)
                    if second and n:
                        expert(t - 2, n)
                    if first and n in DOWN_AT:
                        down(t, DOWN_AT.index(n))
                    if first and n == M_TRANSPOSE_AT:
                        transpose_x(m, p0, t, "mxT")
                    if more and n in OUTPUTS_AT:
                        outputs(t + 1, [i for i in range(NT) if OUTPUTS_AT[i] == n])
                    if more and n == X_TRANSPOSE_AT:
                        transpose_x(f0, p0, t + 1, "xT")
                    if more and n == X_TRANSPOSE_AT + 1:
                        logits(f0, p0, t + 1, router_w, E0)
                    if scan and n + 1 < N:
                        spread(t - 1, "C", n + 1)
                if second:
                    expert(t - 2, N)
                    expert(t - 2, N + 1)
                if more:
                    transpose_comb(r0, p0, t + 1)

            turns(pe, turn)


DOWN_AT = [0, 1, 3, 5]
M_STATS_AT = 6
M_TRANSPOSE_AT = 8
OUTPUTS_AT = [9, 9, 10, 10]
X_STATS_AT = 11
X_TRANSPOSE_AT = 13
RANK_AT = 14
STEPS_F0, STEPS_M, STEPS_F1 = 20, 10, 17


def build(nc, a, out):
    pad = nc.dram_tensor("pad_coefficients", (D1, ROW), FP32, kind="Internal").ap()
    gated = nc.dram_tensor("gated", (NCG, P, B, L), FP32, kind="Internal").ap()
    position_coefficients(nc, a, pad)
    conv = nc.dram_tensor("convolved", (NCG, NM, CB // 2, P, P), FP32, kind="Internal").ap()
    w1 = nc.dram_tensor("w1_parts", (E1, P, 2, W1), FP32, kind="Internal").ap()
    toeplitz_unit(nc, a, a["x_back"], pad, conv, gated, w1)
    mixtures_and_scan(nc, a, a["x"], gated, w1, out)


def arrays_of(w):
    def f(name):
        return np.asarray(w[name])

    def rows(m):
        return np.ascontiguousarray(m.reshape(-1, P, m.shape[-1]).transpose(1, 0, 2))

    def columns(v):
        return np.ascontiguousarray(v.reshape(-1, P).T)

    def grouped(m):
        return np.ascontiguousarray(m.reshape(-1, P, m.shape[1] // P, P).transpose(2, 1, 0, 3))

    a = {
        "x": f("L0_attn_x"),
        "x_back": np.ascontiguousarray(f("L0_attn_x").reshape(B, NT, P, E)[:, :, ::-1]).reshape(B, L, E),
        "ident": np.eye(P, dtype=np.float32),
        "positions": columns(np.arange(L, dtype=np.float32)),
        "decay": np.power(np.float32(0.99), np.arange(L, dtype=np.float32)).astype(np.float32),
        "pos_w": f("L0_attn_pos_w")[0], "pos_b": f("L0_attn_pos_b"),
        "layer_w": np.stack([f(f"L0_attn_lw{i}") for i in range(3)], axis=1),
        "layer_b": np.stack([f(f"L0_attn_lb{i}") for i in range(3)]),
        "out_w": f("L0_attn_out_w"), "out_b": columns(f("L0_attn_out_b")),
        "u_w": grouped(f("L0_attn_u_w")), "u_b": f("L0_attn_u_b").reshape(-1, P, 1),
        "v_w": grouped(f("L0_attn_v_w")), "v_b": f("L0_attn_v_b").reshape(-1, P),
        "o_w": rows(f("L0_attn_o_w")), "o_b": f("L0_attn_o_b"),
    }
    def merged(routed, shared):
        both = np.concatenate([m.transpose(1, 0, 2).reshape(E, -1) for m in (routed, shared)], axis=1)
        return np.ascontiguousarray(rows(both).reshape(P, KE, H0, P))

    def down(routed, shared):
        return rows(np.concatenate([m.reshape(-1, E) for m in (routed, shared)], axis=0))

    x_w = f("L1_attn_W_x")
    first = f("L1_ffn_W1").reshape(E1, H1 * P, KE, P).transpose(0, 3, 2, 1).reshape(E1, P, -1)
    second = f("L1_ffn_W2").reshape(E1, E, H1, P).transpose(0, 3, 2, 1).reshape(E1, P, -1)
    a |= {
        "iota": np.arange(E0, dtype=np.float32),
        "picks": np.tile(np.repeat(np.eye(E0, dtype=np.float32), P // 2, axis=1).reshape(E0, H0R, P), (3, 1, 1)),
        "pick32": np.tile(np.eye(32, dtype=np.float32), (3, 1)),
        "router_w": rows(f("L0_ffn_router_w")),
        "gu_w": np.ascontiguousarray(np.stack([merged(f("L0_ffn_wg_r"), f("L0_ffn_wg_s")),
                                               merged(f("L0_ffn_wu_r"), f("L0_ffn_wu_s"))])
                                     .transpose(3, 1, 0, 2, 4)).reshape(H0, P, -1),
        "down_w": down(f("L0_ffn_wd_r"), f("L0_ffn_wd_s")),
        "in_w": np.ascontiguousarray(rows(f("L1_attn_W_in")).reshape(P, KE, 2 * NB, P)),
        "conv_w": rows(f("L1_attn_conv_w")), "conv_b": columns(f("L1_attn_conv_b")),
        "x_w": rows(np.concatenate([x_w[:, :RK]] + [x_w[:, RK:]] * 3, axis=1)),
        "dt_w": np.ascontiguousarray(f("L1_attn_W_dt").reshape(RK, NB, P)), "dt_b": columns(f("L1_attn_b_dt")),
        "A_log": rows(f("L1_attn_A_log")), "D": columns(f("L1_attn_D")), "y_w": rows(f("L1_attn_W_out")),
        "gate_w": rows(np.ascontiguousarray(f("L1_ffn_Wg").T)), "gate_b": f("L1_ffn_bg"),
        "b1": np.ascontiguousarray(f("L1_ffn_b1").reshape(E1, H1, P).transpose(2, 0, 1)), "b2": f("L1_ffn_b2"),
        "w12": np.ascontiguousarray(np.concatenate([first, second], axis=2)),
    }
    return a


def kernel(**inputs):
    import concourse.bacc as bacc
    from concourse.bass_utils import run_bass_kernel_spmd

    nc = bacc.Bacc("TRN2", target_bir_lowering=False, num_devices=1)
    arrays, aps = {}, {}
    for name, array in arrays_of(inputs).items():
        arrays[f"in_{name}"] = array
        aps[name] = nc.dram_tensor(f"in_{name}", array.shape, mybir.dt.from_np(array.dtype), kind="ExternalInput").ap()
    out = nc.dram_tensor("out", (B, L, E), FP32, kind="ExternalOutput").ap()
    build(nc, aps, out)
    result = run_bass_kernel_spmd(nc, [arrays], core_ids=[0])
    return result.results[0]["out"]
```
